# Optimizing a Trainium2 kernel written in Bass

```python
import numpy as np
import jax
import jax.numpy as jnp

def _softmax(x, axis=-1):
    return jax.nn.softmax(x, axis=axis)

def _gelu(x):
    return jax.nn.gelu(x, approximate=True)

def _silu(x):
    return jax.nn.silu(x)

def _sigmoid(x):
    return jax.nn.sigmoid(x)

def _layernorm(x, axis=-1, eps=1e-05):
    m = jnp.mean(x, axis=axis, keepdims=True)
    v = jnp.var(x, axis=axis, keepdims=True)
    return (x - m) / jnp.sqrt(v + eps)

def _scatter_add(tgt, idx, src, axis=0):
    return tgt.at[idx].add(src)

def _segment_sum(src, seg, n):
    return jax.ops.segment_sum(src, seg, n)
kernel_name = 'mk_adaln_d2_jaxref_r8_52d71f'

def setup_inputs(seed: int=0):
    np.random.seed(seed)
    _w = jnp.asarray

    def _L0_attn_setup():
        import jax, jax.numpy as jnp
        import numpy as np
        B, S, D = (16, 64, 256)
        NUM_HEADS, NUM_GROUPS = (16, 4)
        HEAD_DIM = D // NUM_HEADS
        MAX_SEQ_LEN, SHARED_SLOTS = (64, 32)
        EPS = 1e-06

        def _rope_tables(seq_positions):
            inv_freq = 1.0 / 10000.0 ** (jnp.arange(0, HEAD_DIM, 2, dtype=jnp.float32) / HEAD_DIM)
            freqs = jnp.outer(seq_positions.astype(jnp.float32), inv_freq)
            return (jnp.cos(freqs), jnp.sin(freqs))

        def _apply_rope(x, cos, sin):
            x1, x2 = jnp.split(x, 2, axis=-1)
            real = x1 * cos - x2 * sin
            imag = x1 * sin + x2 * cos
            return jnp.concatenate([real, imag], axis=-1).astype(x.dtype)

        def _rmsnorm(x, scale):
            x = x.astype(jnp.float32)
            ms = jnp.mean(jnp.square(x), axis=-1, keepdims=True)
            return x * jax.lax.rsqrt(ms + EPS) * scale
        key = jax.random.key(seed)
        ks = jax.random.split(key, 10)
        w = 0.02
        return {'x': jax.random.normal(ks[0], (B, S, D), dtype=jnp.float32), 'wq': jax.random.normal(ks[1], (D, D), dtype=jnp.float32) * w, 'bq': jnp.zeros((D,), dtype=jnp.float32), 'wk': jax.random.normal(ks[2], (D, NUM_GROUPS * HEAD_DIM), dtype=jnp.float32) * w, 'bk': jnp.zeros((NUM_GROUPS * HEAD_DIM,), dtype=jnp.float32), 'wv': jax.random.normal(ks[3], (D, NUM_GROUPS * HEAD_DIM), dtype=jnp.float32) * w, 'bv': jnp.zeros((NUM_GROUPS * HEAD_DIM,), dtype=jnp.float32), 'wo': jax.random.normal(ks[4], (D, D), dtype=jnp.float32) * w, 'bo': jnp.zeros((D,), dtype=jnp.float32), 'q_norm_scale': jnp.ones((HEAD_DIM,), dtype=jnp.float32), 'k_norm_scale': jnp.ones((HEAD_DIM,), dtype=jnp.float32)}
    _L0_attn_in = _L0_attn_setup()

    def _L0_ffn_setup():
        import jax, jax.numpy as jnp
        import numpy as np
        key = jax.random.key(seed)
        k1, k2, k3, k4 = jax.random.split(key, 4)
        B, S, D_IN, D_OUT = (4, 512, 256, 256)
        x = jax.random.normal(k1, (B, S, D_IN), dtype=jnp.float32)
        weight = jax.random.normal(k2, (D_OUT, D_IN), dtype=jnp.float32) * 0.02
        scale_weight = jax.random.uniform(k3, (D_OUT,), dtype=jnp.float32, minval=0.5, maxval=1.5)
        bias = jax.random.normal(k4, (D_OUT,), dtype=jnp.float32) * 0.02
        return {'x': x, 'weight': weight, 'scale_weight': scale_weight, 'bias': bias}
    _L0_ffn_in = _L0_ffn_setup()
    _L0_c = _w((lambda *s: np.random.randn(*s).astype(np.float32) * 0.05)(4, 256))
    _L0_wmod = _w((lambda *s: np.random.randn(*s).astype(np.float32) * 0.05)(256, 6 * 256) * 256 ** (-0.5))

    def _L1_attn_setup():
        import jax, jax.numpy as jnp
        import numpy as np
        B, N, H = (2, 512, 256)
        NH, HD = (16, 128)
        BLK = 32
        EPS = 1e-06

        def _lightning_attn(x, slope_rate, w_qkv, w_gate, w_out, norm_w):
            b, n, _ = x.shape
            h, d = (NH, HD)
            nb = n // BLK
            qkv = jax.nn.silu(jnp.einsum('bnf,of->bno', x, w_qkv))
            qkv = qkv.reshape(b, n, h, 3 * d)
            q, k, v = jnp.split(qkv, 3, axis=-1)
            q = q.transpose(0, 2, 1, 3)
            k = k.transpose(0, 2, 1, 3)
            v = v.transpose(0, 2, 1, 3)
            s = slope_rate.astype(jnp.float32)
            arr = jnp.arange(1, BLK + 1, dtype=jnp.float32)
            q_decay = jnp.exp(-s * arr[:, None])
            k_decay = jnp.exp(-s * (BLK - arr)[:, None])
            idx = arr[:, None] - arr[None, :]
            diag_decay = jnp.where(idx >= 0, jnp.exp(-s * idx), 0.0)
            block_decay = jnp.exp(-s * BLK)
            qb = q.reshape(b, h, nb, BLK, d).transpose(2, 0, 1, 3, 4)
            kb = k.reshape(b, h, nb, BLK, d).transpose(2, 0, 1, 3, 4)
            vb = v.reshape(b, h, nb, BLK, d).transpose(2, 0, 1, 3, 4)

            def step(kv, blk):
                qi, ki, vi = blk
                o_inter = jnp.einsum('bhmd,bhde->bhme', qi * q_decay, kv)
                qk = jnp.einsum('bhmd,bhnd->bhmn', qi, ki) * diag_decay
                o_intra = jnp.einsum('bhmn,bhne->bhme', qk, vi)
                kv_new = block_decay * kv + jnp.einsum('bhmd,bhme->bhde', ki * k_decay, vi)
                return (kv_new, o_inter + o_intra)
            kv0 = jnp.zeros((b, h, d, d), dtype=jnp.float32)
            _, out = jax.lax.scan(step, kv0, (qb, kb, vb))
            out = out.transpose(1, 2, 0, 3, 4).reshape(b, h, n, d)
            out = out.transpose(0, 2, 1, 3).reshape(b, n, h * d)
            var = jnp.mean(out * out, axis=-1, keepdims=True)
            out = norm_w * (out * jax.lax.rsqrt(var + EPS))
            gate = jax.nn.sigmoid(jnp.einsum('bnf,of->bno', x, w_gate))
            return jnp.einsum('bno,fo->bnf', gate * out, w_out)
        key = jax.random.key(seed)
        ks = jax.random.split(key, 5)
        scale = 0.02
        x = jax.random.normal(ks[0], (B, N, H), dtype=jnp.float32)
        slopes = (1.0 / 2.0 ** (8.0 * np.arange(1, NH + 1) / NH)).astype(np.float32)
        slope_rate = jnp.asarray(slopes).reshape(NH, 1, 1)
        w_qkv = jax.random.normal(ks[1], (3 * NH * HD, H), dtype=jnp.float32) * scale
        w_gate = jax.random.normal(ks[2], (NH * HD, H), dtype=jnp.float32) * scale
        w_out = jax.random.normal(ks[3], (H, NH * HD), dtype=jnp.float32) * scale
        norm_w = jnp.ones((NH * HD,), dtype=jnp.float32)
        return {'hidden_states': x, 'slope_rate': slope_rate, 'w_qkv': w_qkv, 'w_gate': w_gate, 'w_out': w_out, 'norm_w': norm_w}
    _L1_attn_in = _L1_attn_setup()

    def _L1_ffn_setup():
        import jax, jax.numpy as jnp
        import numpy as np
        from jax import lax
        TOP_K = 2
        N_EXPERTS = 8
        key = jax.random.key(seed)
        ks = jax.random.split(key, 7)
        B, S, H, I, E = (4, 256, 256, 176, N_EXPERTS)
        s_h = 1.0 / np.sqrt(H)
        s_i = 1.0 / np.sqrt(I)
        return {'hidden_states': jax.random.normal(ks[0], (B, S, H), jnp.float32), 'gate_w': jax.random.normal(ks[1], (E, H), jnp.float32) * s_h, 'w1': jax.random.normal(ks[2], (E, H, 2 * I), jnp.float32) * s_h, 'w2': jax.random.normal(ks[3], (E, I, H), jnp.float32) * s_i, 'sw1': jax.random.normal(ks[4], (I, H), jnp.float32) * s_h, 'sw2': jax.random.normal(ks[5], (I, H), jnp.float32) * s_h, 'sw3': jax.random.normal(ks[6], (H, I), jnp.float32) * s_i}
    _L1_ffn_in = _L1_ffn_setup()
    _L1_c = _w((lambda *s: np.random.randn(*s).astype(np.float32) * 0.05)(4, 256))
    _L1_wmod = _w((lambda *s: np.random.randn(*s).astype(np.float32) * 0.05)(256, 6 * 256) * 256 ** (-0.5))
    _d = {'L0_attn_x': _L0_attn_in['x'], 'L0_attn_wq': _L0_attn_in['wq'], 'L0_attn_bq': _L0_attn_in['bq'], 'L0_attn_wk': _L0_attn_in['wk'], 'L0_attn_bk': _L0_attn_in['bk'], 'L0_attn_wv': _L0_attn_in['wv'], 'L0_attn_bv': _L0_attn_in['bv'], 'L0_attn_wo': _L0_attn_in['wo'], 'L0_attn_bo': _L0_attn_in['bo'], 'L0_attn_q_norm_scale': _L0_attn_in['q_norm_scale'], 'L0_attn_k_norm_scale': _L0_attn_in['k_norm_scale'], 'L0_ffn_weight': _L0_ffn_in['weight'], 'L0_ffn_scale_weight': _L0_ffn_in['scale_weight'], 'L0_ffn_bias': _L0_ffn_in['bias'], 'L0_c': _L0_c, 'L0_wmod': _L0_wmod, 'L1_attn_slope_rate': _L1_attn_in['slope_rate'], 'L1_attn_w_qkv': _L1_attn_in['w_qkv'], 'L1_attn_w_gate': _L1_attn_in['w_gate'], 'L1_attn_w_out': _L1_attn_in['w_out'], 'L1_attn_norm_w': _L1_attn_in['norm_w'], 'L1_ffn_gate_w': _L1_ffn_in['gate_w'], 'L1_ffn_w1': _L1_ffn_in['w1'], 'L1_ffn_w2': _L1_ffn_in['w2'], 'L1_ffn_sw1': _L1_ffn_in['sw1'], 'L1_ffn_sw2': _L1_ffn_in['sw2'], 'L1_ffn_sw3': _L1_ffn_in['sw3'], 'L1_c': _L1_c, 'L1_wmod': _L1_wmod}
    _x0 = _d['L0_attn_x']
    _d['L0_attn_x'] = jax.random.normal(jax.random.fold_in(jax.random.key(seed), 1), (4, 512, 256), dtype=_x0.dtype)
    del _x0
    return _d

def reference(L0_attn_x, L0_attn_wq, L0_attn_bq, L0_attn_wk, L0_attn_bk, L0_attn_wv, L0_attn_bv, L0_attn_wo, L0_attn_bo, L0_attn_q_norm_scale, L0_attn_k_norm_scale, L0_ffn_weight, L0_ffn_scale_weight, L0_ffn_bias, L0_c, L0_wmod, L1_attn_slope_rate, L1_attn_w_qkv, L1_attn_w_gate, L1_attn_w_out, L1_attn_norm_w, L1_ffn_gate_w, L1_ffn_w1, L1_ffn_w2, L1_ffn_sw1, L1_ffn_sw2, L1_ffn_sw3, L1_c, L1_wmod):

    def _L0_attn_ref(x, wq, bq, wk, bk, wv, bv, wo, bo, q_norm_scale, k_norm_scale):
        import jax, jax.numpy as jnp
        import numpy as np
        B, S, D = (16, 64, 256)
        NUM_HEADS, NUM_GROUPS = (16, 4)
        HEAD_DIM = D // NUM_HEADS
        MAX_SEQ_LEN, SHARED_SLOTS = (64, 32)
        EPS = 1e-06

        def _rope_tables(seq_positions):
            inv_freq = 1.0 / 10000.0 ** (jnp.arange(0, HEAD_DIM, 2, dtype=jnp.float32) / HEAD_DIM)
            freqs = jnp.outer(seq_positions.astype(jnp.float32), inv_freq)
            return (jnp.cos(freqs), jnp.sin(freqs))

        def _apply_rope(x, cos, sin):
            x1, x2 = jnp.split(x, 2, axis=-1)
            real = x1 * cos - x2 * sin
            imag = x1 * sin + x2 * cos
            return jnp.concatenate([real, imag], axis=-1).astype(x.dtype)

        def _rmsnorm(x, scale):
            x = x.astype(jnp.float32)
            ms = jnp.mean(jnp.square(x), axis=-1, keepdims=True)
            return x * jax.lax.rsqrt(ms + EPS) * scale
        b, s, d = x.shape
        rep = NUM_HEADS // NUM_GROUPS
        head_scale = HEAD_DIM ** (-0.5)
        xh = x.astype(jnp.float16)
        q = (xh @ wq.astype(jnp.float16) + bq.astype(jnp.float16)).reshape(b, s, NUM_HEADS, HEAD_DIM)
        k = (xh @ wk.astype(jnp.float16) + bk.astype(jnp.float16)).reshape(b, s, NUM_GROUPS, HEAD_DIM)
        v = (xh @ wv.astype(jnp.float16) + bv.astype(jnp.float16)).reshape(b, s, NUM_GROUPS, HEAD_DIM)
        q = _rmsnorm(q, q_norm_scale)
        k = _rmsnorm(k, k_norm_scale)
        pos = jnp.arange(s)
        cos, sin = _rope_tables(pos)
        cos = cos[:, None, :]
        sin = sin[:, None, :]
        q = _apply_rope(q, cos, sin) * head_scale
        k = _apply_rope(k, cos, sin)
        q = q.astype(jnp.float16)
        k = k.astype(jnp.float16)
        v = v.astype(jnp.float16)
        qg = q.reshape(b, s, NUM_GROUPS, rep, HEAD_DIM)
        logits = jnp.einsum('btgrh,bsgh->bgrts', qg, k, preferred_element_type=jnp.float32) * head_scale
        causal = pos[:, None] >= pos[None, :]
        logits = jnp.where(causal[None, None, None, :, :], logits, jnp.finfo(jnp.float32).min)
        probs = jax.nn.softmax(logits, axis=-1).astype(jnp.float16)
        out = jnp.einsum('bgrts,bsgh->btgrh', probs, v)
        out = out.reshape(b, s, d)
        return out @ wo.astype(jnp.float16) + bo.astype(jnp.float16)

    def _L0_ffn_ref(x, weight, scale_weight, bias):
        import jax, jax.numpy as jnp
        import numpy as np
        w = weight * scale_weight[:, None]
        out = jnp.einsum('bsi,oi->bso', x, w) + bias
        return out

    def _L1_attn_ref(hidden_states, slope_rate, w_qkv, w_gate, w_out, norm_w):
        import jax, jax.numpy as jnp
        import numpy as np
        B, N, H = (2, 512, 256)
        NH, HD = (16, 128)
        BLK = 32
        EPS = 1e-06

        def _lightning_attn(x, slope_rate, w_qkv, w_gate, w_out, norm_w):
            b, n, _ = x.shape
            h, d = (NH, HD)
            nb = n // BLK
            qkv = jax.nn.silu(jnp.einsum('bnf,of->bno', x, w_qkv))
            qkv = qkv.reshape(b, n, h, 3 * d)
            q, k, v = jnp.split(qkv, 3, axis=-1)
            q = q.transpose(0, 2, 1, 3)
            k = k.transpose(0, 2, 1, 3)
            v = v.transpose(0, 2, 1, 3)
            s = slope_rate.astype(jnp.float32)
            arr = jnp.arange(1, BLK + 1, dtype=jnp.float32)
            q_decay = jnp.exp(-s * arr[:, None])
            k_decay = jnp.exp(-s * (BLK - arr)[:, None])
            idx = arr[:, None] - arr[None, :]
            diag_decay = jnp.where(idx >= 0, jnp.exp(-s * idx), 0.0)
            block_decay = jnp.exp(-s * BLK)
            qb = q.reshape(b, h, nb, BLK, d).transpose(2, 0, 1, 3, 4)
            kb = k.reshape(b, h, nb, BLK, d).transpose(2, 0, 1, 3, 4)
            vb = v.reshape(b, h, nb, BLK, d).transpose(2, 0, 1, 3, 4)

            def step(kv, blk):
                qi, ki, vi = blk
                o_inter = jnp.einsum('bhmd,bhde->bhme', qi * q_decay, kv)
                qk = jnp.einsum('bhmd,bhnd->bhmn', qi, ki) * diag_decay
                o_intra = jnp.einsum('bhmn,bhne->bhme', qk, vi)
                kv_new = block_decay * kv + jnp.einsum('bhmd,bhme->bhde', ki * k_decay, vi)
                return (kv_new, o_inter + o_intra)
            kv0 = jnp.zeros((b, h, d, d), dtype=jnp.float32)
            _, out = jax.lax.scan(step, kv0, (qb, kb, vb))
            out = out.transpose(1, 2, 0, 3, 4).reshape(b, h, n, d)
            out = out.transpose(0, 2, 1, 3).reshape(b, n, h * d)
            var = jnp.mean(out * out, axis=-1, keepdims=True)
            out = norm_w * (out * jax.lax.rsqrt(var + EPS))
            gate = jax.nn.sigmoid(jnp.einsum('bnf,of->bno', x, w_gate))
            return jnp.einsum('bno,fo->bnf', gate * out, w_out)
        return _lightning_attn(hidden_states, slope_rate, w_qkv, w_gate, w_out, norm_w)

    def _L1_ffn_ref(hidden_states, gate_w, w1, w2, sw1, sw2, sw3):
        import jax, jax.numpy as jnp
        import numpy as np
        from jax import lax
        TOP_K = 2
        N_EXPERTS = 8
        B, S, H = hidden_states.shape
        x = hidden_states.reshape(-1, H)
        T = x.shape[0]
        logits = jnp.einsum('th,eh->te', x.astype(jnp.float32), gate_w.astype(jnp.float32))
        scores = jax.nn.softmax(logits, axis=-1)
        topk_w, topk_idx = lax.top_k(scores, TOP_K)
        topk_w = topk_w / (topk_w.sum(-1, keepdims=True) + 1e-20)
        topk_w = topk_w.astype(hidden_states.dtype)
        cw = jnp.zeros((T, N_EXPERTS), hidden_states.dtype).at[jnp.arange(T)[:, None], topk_idx].add(topk_w)

        def body(acc, ew):
            w1e, w2e, cwe = ew
            h = x @ w1e
            g, u = jnp.split(h, 2, axis=-1)
            y = jax.nn.silu(g) * u @ w2e
            return (acc + cwe[:, None] * y, None)
        moe, _ = lax.scan(body, jnp.zeros_like(x), (w1, w2, cw.T))
        moe = moe.reshape(B, S, H)
        shared = jnp.einsum('bsi,hi->bsh', jax.nn.silu(jnp.einsum('bsh,ih->bsi', hidden_states, sw1)) * jnp.einsum('bsh,ih->bsi', hidden_states, sw2), sw3)
        return moe + shared
    x = L0_attn_x
    mod = (_silu(L0_c) @ L0_wmod).reshape(L0_c.shape[0], 6, 1, -1)
    sa, ca, ga, sb, cb, gb = (mod[:, 0], mod[:, 1], mod[:, 2], mod[:, 3], mod[:, 4], mod[:, 5])
    ga = (2 * (ga >= 0) - 1) * jnp.maximum(jnp.abs(ga), 0.25)
    gb = (2 * (gb >= 0) - 1) * jnp.maximum(jnp.abs(gb), 0.25)
    h = _layernorm(x, axis=-1) * (1 + ca) + sa
    x = x + ga * _L0_attn_ref(h, L0_attn_wq, L0_attn_bq, L0_attn_wk, L0_attn_bk, L0_attn_wv, L0_attn_bv, L0_attn_wo, L0_attn_bo, L0_attn_q_norm_scale, L0_attn_k_norm_scale)
    h = _layernorm(x, axis=-1) * (1 + cb) + sb
    x = x + gb * _L0_ffn_ref(h, L0_ffn_weight, L0_ffn_scale_weight, L0_ffn_bias)
    mod = (_silu(L1_c) @ L1_wmod).reshape(L1_c.shape[0], 6, 1, -1)
    sa, ca, ga, sb, cb, gb = (mod[:, 0], mod[:, 1], mod[:, 2], mod[:, 3], mod[:, 4], mod[:, 5])
    ga = (2 * (ga >= 0) - 1) * jnp.maximum(jnp.abs(ga), 0.25)
    gb = (2 * (gb >= 0) - 1) * jnp.maximum(jnp.abs(gb), 0.25)
    h = _layernorm(x, axis=-1) * (1 + ca) + sa
    x = x + ga * _L1_attn_ref(h, L1_attn_slope_rate, L1_attn_w_qkv, L1_attn_w_gate, L1_attn_w_out, L1_attn_norm_w)
    h = _layernorm(x, axis=-1) * (1 + cb) + sb
    x = x + gb * _L1_ffn_ref(h, L1_ffn_gate_w, L1_ffn_w1, L1_ffn_w2, L1_ffn_sw1, L1_ffn_sw2, L1_ffn_sw3)
    return x

_drawn_inputs = setup_inputs


def setup_inputs(seed=0):
    import zlib

    import numpy as np

    out = dict(_drawn_inputs(seed))
    spreads = {'L0_attn_bq': (0.0, 2.0),
     'L0_attn_bk': (0.0, 2.0),
     'L0_attn_bv': (0.0, 0.733),
     'L0_attn_bo': (0.0, 0.274),
     'L0_attn_q_norm_scale': (1.0, 0.6),
     'L0_attn_k_norm_scale': (1.0, 0.6),
     'L1_attn_norm_w': (1.0, 0.578)}
    factors = {'L0_attn_wq': 8.0,
     'L0_attn_wk': 8.0,
     'L0_attn_wv': 8.0,
     'L0_attn_wo': 5.141,
     'L0_ffn_bias': 6.728,
     'L1_attn_w_gate': 2.731}
    for name, (base, spread) in spreads.items():
        noise = np.random.default_rng([zlib.crc32(name.encode()), seed]).standard_normal(out[name].shape)
        drawn = base * np.exp(spread * noise) if base else spread * noise
        out[name] = jnp.asarray(drawn.astype(out[name].dtype))
    for name, factor in factors.items():
        out[name] = (out[name] * factor).astype(out[name].dtype)
    return out
```

```python
from contextlib import ExitStack

import numpy as np
import concourse.bass as bass
from concourse import mybir

F32 = mybir.dt.float32
F32R = mybir.dt.float32r
F16 = mybir.dt.float16
BF16 = mybir.dt.bfloat16
U32 = mybir.dt.uint32
ALU = mybir.AluOpType
ACT = mybir.ActivationFunctionType
AX = mybir.AxisListType

P = 128
D = 256
KT = D // P
B, S = 4, 512
NT = B * S // P
TB = S // P
EPS_LN = 1e-5
EPS_RMS = 1e-6

H0, G0, D0 = 16, 4, 16
R0 = H0 // G0
QKV0 = (H0 + 2 * G0) * D0
SLOT = 32
SHIFT = 256.0
MASKED = -1e30

H1, D1 = 16, 128
PAIRS = H1 // 2
UNITS = 2 * B

E, I = 8, 176
FE = E * I
FA = FE + I
FT = -(-FA // P)
EROWS = E * 3


class Names:

    def __init__(self, nc, ctx, stage):
        self.nc, self.ctx, self.stage = nc, ctx, stage

    def sb(self, name, shape, dt):
        return self.ctx.enter_context(self.nc.sbuf_tensor(f"{self.stage}_{name}", shape, dt))

    def psum(self):
        return self.ctx.enter_context(self.nc.psum_tensor(f"{self.stage}_psum", [P, 8, 512], F32))

    def sem(self, name):
        return self.nc.alloc_semaphore(f"{self.stage}_{name}")

    def sems(self, name, n):
        return [self.sem(f"{name}{k}") for k in range(n)]


def modulation_stage(nc, t, d):
    with ExitStack() as ctx:
        n = Names(nc, ctx, "mod")
        cond = n.sb("cond", [P, 2, KT, B], F32)
        scond = n.sb("scond", [P, 2, KT, B], F32)
        wmod = n.sb("wmod", [P, 2, KT, 6 * D], F32)
        gneg = n.sb("gneg", [P, 2, 2, KT, B], F32)
        gsign = n.sb("gsign", [P, 2, 2, KT, B], F32)
        diag = n.sb("diag", [P, 4, KT * B, P], F32)
        ones = n.sb("ones", [P, P], F32)
        dist = n.sb("dist", [P, S], F32)
        nslope = n.sb("nslope", [P, H1], F32)
        decay = n.sb("decay", [P, H1, S], F32)
        ps = n.psum()
        loaded, silu_done = n.sem("loaded"), n.sem("silu_done")
        cond_loaded = n.sem("cond_loaded")
        mod_ready, mod_copied, plus_one = n.sem("mod_ready"), n.sem("mod_copied"), n.sem("plus_one")
        gate_step, diag_ready, gates_ready = n.sem("gate_step"), n.sem("diag_ready"), n.sem("gates_ready")
        ident_step, const_ready = n.sem("ident_step"), n.sem("const_ready")
        slope_loaded, slope_neg, decay_ready = n.sem("slope_loaded"), n.sem("slope_neg"), n.sem("decay_ready")
        masked, stored, dist_step = n.sem("masked"), n.sem("stored"), n.sem("dist_step")
        gates_copied = n.sem("gates_copied")

        with nc.Block() as block:

            @block.sync
            def _(sp):
                sp.dma_start(cond[:, :, :, :], d["cond"]).then_inc(cond_loaded, 16)
                sp.dma_start(wmod[:, 0], d["wmod0"]).then_inc(loaded, 16)
                sp.dma_start(wmod[:, 1], d["wmod1"]).then_inc(loaded, 16)
                sp.dma_start(nslope[:, :], d["slope"]).then_inc(slope_loaded, 16)
                sp.dma_start(t["x"][:, :, :], d["x"]).then_inc(loaded, 16)
                for h in range(H1):
                    sp.wait_ge(masked, h + 1)
                    sp.dma_start(t["decay_dram"][h], decay[:, h, :]).then_inc(stored, 16)
                sp.wait_ge(loaded, 48)
                sp.wait_ge(stored, 16 * H1)

            @block.gpsimd
            def _(pool):
                nc.gpsimd.memset(t["ident"][:, :], 0.0).then_inc(ident_step, 1)
                nc.gpsimd.memset(t["ident16"][:, :], 0.0).then_inc(ident_step, 1)
                nc.gpsimd.memset(t["identb"][:, :], 0.0).then_inc(ident_step, 1)
                nc.gpsimd.memset(t["later_key"][:, :], 0.0).then_inc(ident_step, 1)
                nc.gpsimd.memset(t["later_key_t"][:, :], 0.0).then_inc(ident_step, 1)
                nc.gpsimd.memset(ones[:, :], 1.0)
                nc.gpsimd.memset(t["neg_half"][:, :], -0.5)
                nc.gpsimd.iota(dist[:, :], [[1, S]], base=0, channel_multiplier=-1,
                               allow_small_or_imprecise_dtypes=True).then_inc(dist_step, 1)
                pool.wait_ge(ident_step, 5)
                for m in ("ident", "ident16", "identb"):
                    nc.gpsimd.affine_select(out=t[m][:, :], in_=t[m][:, :], compare_op=ALU.not_equal, fill=1.0,
                                            base=0, pattern=[[-1, P]], channel_multiplier=1)
                nc.gpsimd.affine_select(out=t["later_key"][:, :], in_=t["later_key"][:, :], compare_op=ALU.is_ge,
                                        fill=MASKED, base=0, pattern=[[-1, P]], channel_multiplier=1)
                nc.gpsimd.affine_select(out=t["later_key_t"][:, :], in_=t["later_key_t"][:, :], compare_op=ALU.is_ge,
                                        fill=MASKED, base=0, pattern=[[1, P]],
                                        channel_multiplier=-1).then_inc(const_ready, 1)
                for h in range(H1):
                    pool.wait_ge(decay_ready, h + 1)
                    nc.gpsimd.affine_select(out=decay[:, h, 0:P], in_=decay[:, h, 0:P], compare_op=ALU.is_ge,
                                            fill=0.0, base=0, pattern=[[1, P]],
                                            channel_multiplier=-1).then_inc(masked, 1)

            @block.scalar
            def _(act):
                act.wait_ge(cond_loaded, 16)
                nc.scalar.activation(scond[:, :, :, :], cond[:, :, :, :], ACT.Silu).then_inc(silu_done, 1)
                act.wait_ge(dist_step, 2)
                act.wait_ge(slope_neg, 1)
                for h in range(H1):
                    nc.scalar.activation(decay[:, h, :], dist[:, :], ACT.Exp,
                                         scale=nslope[:, h:h + 1]).then_inc(decay_ready, 1)
                for g in range(4):
                    act.wait_ge(gates_ready, g + 1)
                    nc.scalar.copy(t["gate"][:, g].rearrange("p (c b) n -> p c (b n)", c=2),
                                   ps[:, 2 * (g % 4):2 * (g % 4) + 2, :]).then_inc(gates_copied, 1)

            @block.vector
            def _(dve):
                dve.wait_ge(dist_step, 1)
                nc.vector.tensor_scalar(dist[:, :], dist[:, :], 0.0, None, ALU.max).then_inc(dist_step, 1)
                dve.wait_ge(slope_loaded, 16)
                nc.vector.tensor_scalar(nslope[:, :], nslope[:, :], -1.0, None, ALU.mult).then_inc(slope_neg, 1)
                dve.wait_ge(mod_ready, 1)
                nc.vector.tensor_copy(t["mod"][:, :, :, :, :], ps[:, 0, 0:96].rearrange(
                    "p (l c k b) -> p l c (k b)", l=2, c=6, k=KT).rearrange("p l c (k b) -> p l c k b", k=KT)
                    ).then_inc(mod_copied, 1)
                dve.wait_ge(mod_copied, 1)
                for l in range(2):
                    for c in (1, 4):
                        nc.vector.tensor_scalar(t["mod"][:, l, c], t["mod"][:, l, c], 1.0, None,
                                                ALU.add).then_inc(plus_one, 1)
                for l in range(2):
                    for j, c in enumerate((2, 5)):
                        g = t["mod"][:, l, c].rearrange("p k b -> p (k b)")
                        a = gneg[:, l, j].rearrange("p k b -> p (k b)")
                        s = gsign[:, l, j].rearrange("p k b -> p (k b)")
                        nc.vector.scalar_tensor_tensor(a, g, -1.0, g, ALU.mult, ALU.max).then_inc(gate_step, 1)
                        nc.vector.tensor_scalar(s, g, 0.0, 2.0, ALU.is_ge, ALU.mult).then_inc(gate_step, 1)
                dve.wait_ge(gate_step, 8)
                gn = gneg[:, :, :, :, :].rearrange("p l j k b -> p (l j k b)")
                gs = gsign[:, :, :, :, :].rearrange("p l j k b -> p (l j k b)")
                nc.vector.tensor_scalar(gn, gn, 0.25, None, ALU.max).then_inc(gate_step, 1)
                dve.wait_ge(gate_step, 9)
                nc.vector.scalar_tensor_tensor(gn, gs, -1.0, gn, ALU.add, ALU.mult).then_inc(gate_step, 1)
                dve.wait_ge(gate_step, 10)
                dve.wait_ge(const_ready, 1)
                for g in range(4):
                    for k in range(KT):
                        for b in range(B):
                            last = nc.vector.tensor_scalar(diag[:, g, k * B + b, :], t["ident"][:, :],
                                                           gneg[:, g // 2, g % 2, k, b:b + 1], None, ALU.mult)
                    last.then_inc(diag_ready, 1)

            @block.tensor
            def _(pe):
                pe.wait_ge(silu_done, 1)
                pe.wait_ge(loaded, 48)
                for l in range(2):
                    for c in range(6):
                        for f in range(KT):
                            at = ((l * 6 + c) * KT + f) * B
                            for k in range(KT):
                                last = nc.tensor.matmul(ps[:, 0, at:at + B], wmod[:, l, k, c * D + f * P:c * D + (f + 1) * P],
                                                        scond[:, l, k, :], start=(k == 0), stop=(k == KT - 1))
                last.then_inc(mod_ready, 1)
                for g in range(4):
                    pe.wait_ge(diag_ready, g + 1)
                    for b in range(B):
                        for k in range(KT):
                            last = nc.tensor.matmul(ps[:, 2 * g + b // 2, (b % 2) * D + k * P:(b % 2) * D + (k + 1) * P],
                                                    ones[:, :], diag[:, g, k * B + b, :], start=True, stop=True)
                    last.then_inc(gates_ready, 1)


def attention0_tasks():
    before = [("xn",), ("qkv", 0), ("qkv", 1), ("kt",), ("qt",)]
    scores = [[("s", g, tt, pr) for tt in range(TB) for pr in range(2)] for g in range(G0)] + [[]]
    order, late = list(before) + scores[0], []
    for g in range(G0):
        nxt = list(scores[g + 1])
        order += nxt[:2]
        nxt = nxt[2:]
        own = ([("q2", g)] + [("st", g, 0, j) for j in range(2)] + late + [("st", g, 0, 2), ("st", g, 0, 3)]
               + [("st", g, 1, 0), ("st", g, 1, 1), ("pv", g, 0), ("st", g, 1, 2), ("st", g, 1, 3)])
        late = [("pv", g, 1)]
        for n, task in enumerate(own):
            order.append(task)
            if n >= 1 and nxt:
                order.append(nxt.pop(0))
        order += nxt
    return order + late + [("aot",), ("out", 0), ("out", 1)]


def attention0_stage(nc, t, d):
    tasks = attention0_tasks()
    place = {task: n for n, task in enumerate(tasks)}
    assert len(tasks) % 4 == 0 and len(place) == len(tasks)
    turns = len(tasks) // 4
    x = t["x"]
    with ExitStack() as ctx:
        n = Names(nc, ctx, "attn0")
        wqkv32 = n.sb("wqkv32", [P, KT, QKV0], F32)
        wo32 = n.sb("wo32", [P, KT, D], F32)
        bias32 = n.sb("bias32", [1, QKV0 + D], F32)
        wqkv = n.sb("wqkv", [P, KT, QKV0], F16)
        wo = n.sb("wo", [P, KT, D], F16)
        bias = n.sb("bias", [1, QKV0 + D], F16)
        ones = n.sb("ones", [1, P], F16)
        norm_scale = n.sb("norm_scale", [P, 2, D0], F32)
        cosd = n.sb("cosd", [P, TB, D0], F32)
        sind = n.sb("sind", [P, TB, D0], F32)
        cos_t = n.sb("cos_t", [P, TB, 2, D0], F32)
        sin_t = n.sb("sin_t", [P, TB, 2, D0], F32)
        st = n.sb("st", [P, TB, 6], F32)
        mv = n.sb("mv", [P, TB, 2], F32)
        rstd = n.sb("rstd", [P, TB], F32)
        xn = n.sb("xn", [P, TB, D], F32)
        ht = n.sb("ht", [P, KT, S], F16)
        qkv = n.sb("qkv", [P, TB, QKV0], F16)
        NH = H0 + G0
        sq = n.sb("sq", [P, TB, NH, D0], F32)
        ss = n.sb("ss", [P, TB, NH], F32)
        qn = n.sb("qn", [P, TB, NH, D0], F32)
        rc_ = n.sb("rope_cos", [P, TB, NH, D0], F32)
        rs_ = n.sb("rope_sin", [P, TB, NH, D0], F32)
        kr = n.sb("kr", [P, TB, G0, D0], F16)
        qa = n.sb("qa", [P, TB, H0, SLOT], F16)
        ka = n.sb("ka", [P, TB * G0, R0, SLOT], F16)
        va = n.sb("va", [P, TB, G0, D0 + 1], F16)
        qt = n.sb("qt", [P, G0, S], F16)
        qt2 = n.sb("qt2", [P, G0, S], F16)
        kt = n.sb("kt", [P, G0, S], F16)
        top = n.sb("top", [P, TB, H0], F32)
        probs = n.sb("probs", [P, 2, TB, 2, S], F16)
        rden = n.sb("rden", [P, 2, TB, 2], F32)
        ao = n.sb("ao", [P, TB, H0, D0], F16)
        aot = n.sb("aot", [P, KT, S], F16)
        upd = n.sb("upd", [P, TB, D], F32)
        ps = n.psum()
        eps_rms = n.sb("eps_rms", [P, 1], F32)

        weights_loaded = n.sem("weights_loaded")
        tables_loaded = n.sem("tables_loaded")
        weights_cast, tables_ready, padding_set = n.sem("weights_cast"), n.sem("tables_ready"), n.sem("padding_set")
        slot_full = n.sems("slot_full", 4)
        stats_done, aggr_done, var_eps, rstd_done = (n.sem(s) for s in ("stats_done", "aggr_done", "var_eps", "rstd_done"))
        xn_done, ht_done, qkv_done = n.sem("xn_done"), n.sem("ht_done"), n.sem("qkv_done")
        sq_done, ss_done, std_done, rrms_done = (n.sem(s) for s in ("sq_done", "ss_done", "std_done", "rrms_done"))
        qn_done, rot_done, q_roped, k_roped, k_spread, v_copied = (
            n.sem(s) for s in ("qn_done", "rot_done", "q_roped", "k_roped", "k_spread", "v_copied"))
        krot_done = n.sem("krot_done")
        kt_done, qt_done, top_done, shift_set, qt2_done = (
            n.sem(s) for s in ("kt_done", "qt_done", "top_done", "shift_set", "qt2_done"))
        exp_done, rden_done, ao_done, aot_done = (
            n.sem(s) for s in ("exp_done", "rden_done", "ao_done", "aot_done"))
        upd_done, x_done = n.sem("upd_done"), n.sem("x_done")
        eps_set, dve_held, pool_held = n.sem("eps_set"), n.sem("dve_held"), n.sem("pool_held")

        def banks(task):
            s = place[task] % 4
            return ps[:, 2 * s:2 * s + 2, :]

        def banks16(task):
            return banks(task).rearrange("p a n -> p (a n)").bitcast(F16)

        def filled(eng, task, it):
            m = place[task]
            eng.wait_ge(slot_full[m % 4], it * turns + (m // 4 + 1))

        def emptied(eng, task, it):
            kind = task[0]
            if kind == "xn":
                eng.wait_ge(ht_done, it * KT + KT)
            elif kind == "qkv":
                eng.wait_ge(qkv_done, it * 2 + (task[1] + 1))
            elif kind in ("kt", "qt", "aot"):
                eng.wait_ge({"kt": kt_done, "qt": qt_done, "aot": aot_done}[kind], it + 1)
            elif kind == "s":
                _, g, tt, pr = task
                eng.wait_ge(top_done, it * 32 + (g * 8 + tt * 2 + pr + 1))
            elif kind == "q2":
                eng.wait_ge(qt2_done, it * G0 + (task[1] + 1))
            elif kind == "st":
                _, g, pr, j = task
                eng.wait_ge(exp_done, it * (8 * TB) + ((2 * g + pr) * TB + j + 1))
            elif kind == "pv":
                _, g, pr = task
                eng.wait_ge(ao_done, it * 8 + (2 * g + pr + 1))
            else:
                eng.wait_ge(upd_done, it * 2 + (task[1] + 1))

        with nc.Block() as block:

            @block.sync
            def _(sp):
                sp.dma_start(wqkv32[:, :, :], d["wqkv0"]).then_inc(weights_loaded, 16)
                sp.dma_start(wo32[:, :, :], d["wo0"]).then_inc(weights_loaded, 16)
                sp.dma_start(bias32[:, :], d["bias0"]).then_inc(weights_loaded, 16)
                sp.dma_start(norm_scale[:, :, :], d["norm_scale0"]).then_inc(tables_loaded, 16)
                sp.dma_start(cosd[:, :, :], d["cosd"]).then_inc(tables_loaded, 16)
                sp.dma_start(sind[:, :, :], d["sind"]).then_inc(tables_loaded, 16)

            @block.tensor
            def _(pe):
                pe.wait_ge(weights_cast, 3)
                pe.wait_ge(padding_set, 5)

                def batch(it, first):
                    for m, task in enumerate(tasks):
                        kind, out = task[0], banks(task)
                        if m >= 4:
                            emptied(pe, tasks[m - 4], it)
                        elif not first:
                            emptied(pe, tasks[m - 4], it - 1)
                        if kind == "xn":
                            pe.wait_ge(xn_done, it + 1)
                            for k in range(KT):
                                for tt in range(TB):
                                    last = nc.tensor.transpose(out[:, k, tt * P:(tt + 1) * P],
                                                               xn[:, tt, k * P:(k + 1) * P], t["ident"][:, :])
                        elif kind == "qkv":
                            pe.wait_ge(ht_done, it * KT + KT)
                            for h in range(2):
                                tt = 2 * task[1] + h
                                for k in range(KT):
                                    nc.tensor.matmul(out[:, h, 0:QKV0], ht[:, k, tt * P:(tt + 1) * P], wqkv[:, k, :],
                                                     start=(k == 0), stop=False)
                                last = nc.tensor.matmul(out[:, h, 0:QKV0], ones[0:1, :], bias[0:1, 0:QKV0],
                                                        start=False, stop=True)
                        elif kind in ("kt", "qt"):
                            if kind == "kt":
                                pe.wait_ge(k_spread, it + 1)
                            else:
                                pe.wait_ge(q_roped, it * 2 + 2)
                            o = banks16(task)
                            for g in range(G0):
                                for tt in range(TB):
                                    src = (ka[:, tt * G0 + g].rearrange("p r c -> p (r c)") if kind == "kt" else
                                           qa[:, tt, R0 * g:R0 * (g + 1)].rearrange("p r c -> p (r c)"))
                                    last = nc.tensor.transpose(o[:, g * S + tt * P:g * S + (tt + 1) * P], src,
                                                               t["ident16"][:, :])
                        elif kind == "s":
                            _, g, tt, pr = task
                            if (g, tt, pr) == (0, 0, 0):
                                pe.wait_ge(kt_done, it + 1)
                                pe.wait_ge(qt_done, it + 1)
                            for h in range(2):
                                r = SLOT * (2 * pr + h)
                                nc.tensor.matmul(out[:, h, 0:(tt + 1) * P], qt[r:r + D0, g, tt * P:(tt + 1) * P],
                                                 kt[r:r + D0, g, 0:(tt + 1) * P], start=True, stop=False)
                            for h in range(2):
                                last = nc.tensor.matmul(out[:, h, tt * P:(tt + 1) * P], t["identb"][:, :],
                                                        t["later_key"][:, :], start=False, stop=True)
                        elif kind == "q2":
                            g = task[1]
                            pe.wait_ge(shift_set, it * G0 + (g + 1))
                            o = banks16(task)
                            for tt in range(TB):
                                last = nc.tensor.transpose(o[:, tt * P:(tt + 1) * P],
                                                           qa[:, tt, R0 * g:R0 * (g + 1)].rearrange("p r c -> p (r c)"),
                                                           t["ident16"][:, :])
                        elif kind == "st":
                            _, g, pr, j = task
                            if (pr, j) == (0, 0):
                                pe.wait_ge(qt2_done, it * G0 + (g + 1))
                            for h in range(2):
                                r = SLOT * (2 * pr + h)
                                nc.tensor.matmul(out[:, h, 0:S - j * P], kt[r:r + D0 + 1, g, j * P:(j + 1) * P],
                                                 qt2[r:r + D0 + 1, g, j * P:S], start=True, stop=False)
                            for h in range(2):
                                last = nc.tensor.matmul(out[:, h, 0:P], t["identb"][:, :], t["later_key_t"][:, :],
                                                        start=False, stop=True)
                        elif kind == "pv":
                            _, g, pr = task
                            pe.wait_ge(exp_done, it * (8 * TB) + (2 * g + pr + 1) * TB)
                            if (g, pr) == (0, 0):
                                pe.wait_ge(v_copied, it + 1)
                            for tt in range(TB):
                                for h in range(2):
                                    o = out[:, 0, (tt * 2 + h) * (D0 + 1):(tt * 2 + h + 1) * (D0 + 1)]
                                    for j in range(tt + 1):
                                        last = nc.tensor.matmul(o, probs[:, pr, j, h, (tt - j) * P:(tt - j + 1) * P],
                                                                va[:, j, g, :], start=(j == 0), stop=(j == tt))
                        elif kind == "aot":
                            pe.wait_ge(ao_done, it * 8 + 8)
                            o = banks16(task)
                            for k in range(KT):
                                for tt in range(TB):
                                    last = nc.tensor.transpose(
                                        o[:, k * S + tt * P:k * S + (tt + 1) * P],
                                        ao[:, tt, k * 8:(k + 1) * 8].rearrange("p h c -> p (h c)"), t["ident16"][:, :])
                        else:
                            pe.wait_ge(aot_done, it + 1)
                            for h in range(2):
                                tt = 2 * task[1] + h
                                for k in range(KT):
                                    nc.tensor.matmul(out[:, h, 0:D], aot[:, k, tt * P:(tt + 1) * P], wo[:, k, :],
                                                     start=(k == 0), stop=False)
                                last = nc.tensor.matmul(out[:, h, 0:D], ones[0:1, :], bias[0:1, QKV0:QKV0 + D],
                                                        start=False, stop=True)
                        last.then_inc(slot_full[m % 4], 1)

                batch(0, True)
                with pe.Fori(1, B) as it:
                    batch(it, False)

            @block.scalar
            def _(act):
                act.wait_ge(weights_loaded, 48)
                nc.scalar.copy(wqkv[:, :, :], wqkv32[:, :, :]).then_inc(weights_cast, 1)
                nc.scalar.copy(wo[:, :, :], wo32[:, :, :]).then_inc(weights_cast, 1)
                nc.scalar.copy(bias[:, :], bias32[:, :]).then_inc(weights_cast, 1)
                act.wait_ge(eps_set, 1)
                with act.Fori(0, B) as it:
                    filled(act, ("xn",), it)
                    for k in range(KT):
                        last = nc.scalar.activation(ht[:, k, :], banks(("xn",))[:, k, :], ACT.Identity,
                                                    scale=t["mod"][:, 0, 1, k, bass.ds(it, 1)],
                                                    bias=t["mod"][:, 0, 0, k, bass.ds(it, 1)])
                        last.then_inc(ht_done, 1)
                    for i in range(2):
                        filled(act, ("qkv", i), it)
                        nc.scalar.copy(qkv[:, 2 * i:2 * i + 2, :], banks(("qkv", i))[:, :, 0:QKV0]).then_inc(qkv_done, 1)
                    act.wait_ge(ss_done, it + 1)
                    nc.scalar.activation(ss[:, :, :], ss[:, :, :], ACT.Sqrt, bias=eps_rms[:, 0:1], scale=1.0 / D0).then_inc(std_done, 1)
                    for task in tasks:
                        if task[0] == "st":
                            _, g, pr, j = task
                            filled(act, task, it)
                            if j == 0 and g:
                                filled(act, ("pv", g - 1, pr), it)
                            nc.scalar.activation(probs[:, pr, j, :, 0:S - j * P], banks(task)[:, :, 0:S - j * P],
                                                 ACT.Exp, scale=D0 ** -0.5).then_inc(exp_done, 1)

            @block.vector
            def _(dve):
                nc.vector.memset(eps_rms[:, :], EPS_RMS).then_inc(eps_set, 1)
                dve.wait_ge(padding_set, 5)
                with dve.Fori(0, B) as it:
                    for tt in range(TB):
                        nc.vector.bn_stats(st[:, tt, :], x[:, bass.ds(it * TB + tt, 1), :]).then_inc(stats_done, 1)
                    dve.wait_ge(stats_done, it * TB + TB)
                    dve.sem_inc(dve_held, 1)
                    for tt in range(TB):
                        last = nc.vector.bn_aggr(mv[:, tt, :], st[:, tt, :])
                    last.then_inc(aggr_done, 1)
                    dve.wait_ge(rstd_done, it + 1)
                    for tt in range(TB):
                        last = nc.vector.tensor_scalar(xn[:, tt, :], x[:, bass.ds(it * TB + tt, 1), :], mv[:, tt, 0:1],
                                                       rstd[:, tt:tt + 1], ALU.subtract, ALU.mult)
                    last.then_inc(xn_done, 1)
                    qk = qkv[:, :, 0:NH * D0]
                    dve.wait_ge(qkv_done, it * 2 + 2)
                    sqf = sq[:, :, :, :].rearrange("p t h c -> p t (h c)")
                    nc.vector.tensor_tensor(sqf, qk, qk, ALU.mult).then_inc(sq_done, 1)
                    dve.wait_ge(sq_done, it + 1)
                    nc.vector.tensor_reduce(ss[:, :, :], sq[:, :, :, :], AX.X, ALU.add).then_inc(ss_done, 1)
                    dve.wait_ge(std_done, it + 1)
                    nc.vector.reciprocal(ss[:, :, :], ss[:, :, :]).then_inc(rrms_done, 1)
                    dve.wait_ge(rrms_done, it + 1)
                    nc.vector.tensor_tensor(qn[:, :, :, :].rearrange("p t h c -> p (t h) c"),
                                            qkv[:, :, 0:NH * D0].rearrange("p t (h c) -> p t h c", c=D0),
                                            ss[:, :, :].unsqueeze(3).to_broadcast([P, TB, NH, D0]),
                                            ALU.mult).then_inc(qn_done, 1)
                    dve.wait_ge(qn_done, it + 1)
                    q4 = [P, TB, H0, D0]
                    nc.vector.tensor_tensor(rc_[:, :, 0:H0, :], qn[:, :, 0:H0, :],
                                            cos_t[:, :, 0, :].unsqueeze(2).to_broadcast(q4), ALU.mult)
                    nc.vector.tensor_tensor(rs_[:, :, 0:H0, :], qn[:, :, 0:H0, :],
                                            sin_t[:, :, 0, :].unsqueeze(2).to_broadcast(q4), ALU.mult).then_inc(rot_done, 1)
                    dve.wait_ge(rot_done, it + 1)
                    hd = D0 // 2
                    nc.vector.tensor_tensor(qa[:, :, :, 0:hd], rc_[:, :, 0:H0, 0:hd], rs_[:, :, 0:H0, hd:D0],
                                            ALU.subtract).then_inc(q_roped, 1)
                    nc.vector.tensor_tensor(qa[:, :, :, hd:D0], rc_[:, :, 0:H0, hd:D0], rs_[:, :, 0:H0, 0:hd],
                                            ALU.add).then_inc(q_roped, 1)
                    for task in tasks:
                        kind = task[0]
                        if kind not in ("kt", "qt", "s", "q2", "pv", "aot", "out"):
                            continue
                        filled(dve, task, it)
                        if kind in ("kt", "qt"):
                            dst, done = (kt, kt_done) if kind == "kt" else (qt, qt_done)
                            nc.vector.tensor_copy(dst[:, :, :].rearrange("p g n -> p (g n)"), banks16(task)).then_inc(done, 1)
                        elif kind == "s":
                            _, g, tt, pr = task
                            h = R0 * g + 2 * pr
                            nc.vector.tensor_reduce(top[:, tt, h:h + 2], banks(task)[:, :, 0:(tt + 1) * P], AX.X,
                                                    ALU.max).then_inc(top_done, 1)
                            if (tt, pr) == (TB - 1, 1):
                                dve.wait_ge(top_done, it * 32 + (g * 8 + tt * 2 + pr + 1))
                                nc.vector.tensor_scalar(qa[:, :, R0 * g:R0 * (g + 1), D0], top[:, :, R0 * g:R0 * (g + 1)],
                                                        -1.0 / SHIFT, None, ALU.mult).then_inc(shift_set, 1)
                        elif kind == "q2":
                            g = task[1]
                            nc.vector.tensor_copy(qt2[:, g, :], banks16(task)[:, 0:S]).then_inc(qt2_done, 1)
                        elif kind == "pv":
                            _, g, pr = task
                            o = banks(task)[:, 0, 0:8 * (D0 + 1)].rearrange("p (t h c) -> p t h c", h=2, c=D0 + 1)
                            nc.vector.reciprocal(rden[:, pr, :, :], o[:, :, :, D0]).then_inc(rden_done, 1)
                            dve.wait_ge(rden_done, it * 8 + (2 * g + pr + 1))
                            h = R0 * g + 2 * pr
                            nc.vector.tensor_tensor(ao[:, :, h:h + 2, :], o[:, :, :, 0:D0],
                                                    rden[:, pr, :, :].unsqueeze(3).to_broadcast([P, TB, 2, D0]),
                                                    ALU.mult).then_inc(ao_done, 1)
                        elif kind == "aot":
                            nc.vector.tensor_copy(aot[:, :, :].rearrange("p k n -> p (k n)"),
                                                  banks16(task)[:, 0:KT * S]).then_inc(aot_done, 1)
                        else:
                            i = task[1]
                            nc.vector.tensor_tensor(upd[:, 2 * i:2 * i + 2, :], banks(task)[:, :, 0:D],
                                                    t["gate"][:, 0, bass.ds(it, 1), :].to_broadcast([P, 2, D]),
                                                    ALU.mult).then_inc(upd_done, 1)

            @block.gpsimd
            def _(pool):
                nc.gpsimd.memset(qa[:, :, :, :], 0.0).then_inc(padding_set, 1)
                nc.gpsimd.memset(ka[:, :, :, :], 0.0).then_inc(padding_set, 1)
                nc.gpsimd.memset(va[:, :, :, :], 1.0).then_inc(padding_set, 1)
                nc.gpsimd.memset(ones[:, :], 1.0).then_inc(padding_set, 1)
                pool.wait_ge(padding_set, 4)
                nc.gpsimd.memset(ka[:, :, :, D0:D0 + 1], SHIFT).then_inc(padding_set, 1)
                pool.wait_ge(tables_loaded, 48)
                nc.gpsimd.tensor_scalar(norm_scale[:, 0, :], norm_scale[:, 0, :], D0 ** -0.5, None,
                                        ALU.mult).then_inc(tables_ready, 1)
                pool.wait_ge(tables_ready, 1)
                for which in range(2):
                    sc = norm_scale[:, which, :].unsqueeze(1).to_broadcast([P, TB, D0])
                    nc.gpsimd.tensor_tensor(cos_t[:, :, which, :], cosd[:, :, :], sc, ALU.mult)
                    last = nc.gpsimd.tensor_tensor(sin_t[:, :, which, :], sind[:, :, :], sc, ALU.mult)
                last.then_inc(tables_ready, 1)
                pool.wait_ge(tables_ready, 2)
                with pool.Fori(0, B) as it:
                    pool.wait_ge(aggr_done, it + 1)
                    pool.sem_inc(pool_held, 1)
                    nc.gpsimd.tensor_scalar(rstd[:, :], mv[:, :, 1], EPS_LN, None, ALU.add).then_inc(var_eps, 1)
                    pool.wait_ge(var_eps, it + 1)
                    nc.gpsimd.tensor_tensor(rstd[:, :], rstd[:, :], t["neg_half"][:, 0:TB], ALU.pow).then_inc(rstd_done, 1)
                    pool.wait_ge(qkv_done, it * 2 + 2)
                    pool.sem_inc(pool_held, 1)
                    nc.gpsimd.tensor_copy(va[:, :, :, 0:D0], qkv[:, :, NH * D0:QKV0].rearrange(
                        "p t (g c) -> p t g c", c=D0)).then_inc(v_copied, 1)
                    pool.wait_ge(qn_done, it + 1)
                    k4 = [P, TB, G0, D0]
                    nc.gpsimd.tensor_tensor(rc_[:, :, H0:NH, :], qn[:, :, H0:NH, :],
                                            cos_t[:, :, 1, :].unsqueeze(2).to_broadcast(k4), ALU.mult).then_inc(krot_done, 1)
                    nc.gpsimd.tensor_tensor(rs_[:, :, H0:NH, :], qn[:, :, H0:NH, :],
                                            sin_t[:, :, 1, :].unsqueeze(2).to_broadcast(k4), ALU.mult).then_inc(krot_done, 1)
                    pool.wait_ge(krot_done, it * 2 + 2)
                    hd = D0 // 2
                    nc.gpsimd.tensor_tensor(kr[:, :, :, 0:hd], rc_[:, :, H0:NH, 0:hd], rs_[:, :, H0:NH, hd:D0],
                                            ALU.subtract).then_inc(k_roped, 1)
                    nc.gpsimd.tensor_tensor(kr[:, :, :, hd:D0], rc_[:, :, H0:NH, hd:D0], rs_[:, :, H0:NH, 0:hd],
                                            ALU.add).then_inc(k_roped, 1)
                    pool.wait_ge(k_roped, it * 2 + 2)
                    pool.sem_inc(pool_held, 1)
                    nc.gpsimd.tensor_copy(ka[:, :, :, 0:D0], kr[:, :, :, :].rearrange("p t g c -> p (t g) c").unsqueeze(2)
                                          .to_broadcast([P, TB * G0, R0, D0])).then_inc(k_spread, 1)
                    for i in range(2):
                        pool.wait_ge(upd_done, it * 2 + (i + 1))
                        xs = x[:, bass.ds(it * TB + 2 * i, 2), :]
                        nc.gpsimd.tensor_tensor(xs, xs, upd[:, 2 * i:2 * i + 2, :], ALU.add).then_inc(x_done, 1)


def at(i, size=1):
    return slice(i, i + size) if isinstance(i, int) else bass.ds(i, size)


class SplitNorm:

    def __init__(self, n, tag, layer, shift_part, parts, psum_slot):
        self.layer, self.shift_part, self.parts, self.slot = layer, shift_part, parts, psum_slot
        self.st = n.sb(f"{tag}_st", [P, TB, 6], F32)
        self.mv = n.sb(f"{tag}_mv", [P, TB, 2], F32)
        self.rstd = n.sb(f"{tag}_rstd", [P, TB], F32)
        self.xn = n.sb(f"{tag}_xn", [P, TB, D], F32)
        self.ht = n.sb(f"{tag}_ht", [P, KT, S], F32)
        self.stats_done, self.aggr_done = n.sem(f"{tag}_stats_done"), n.sem(f"{tag}_aggr_done")
        self.var_eps, self.rstd_done = n.sem(f"{tag}_var_eps"), n.sem(f"{tag}_rstd_done")
        self.xn_done, self.turned = n.sem(f"{tag}_xn_done"), n.sem(f"{tag}_turned")
        self.ht_done, self.high_done = n.sem(f"{tag}_ht_done"), n.sem(f"{tag}_high_done")
        self.low_done = n.sem(f"{tag}_low_done")

    def out(self, part, it):
        if self.parts.shape[3] == S:
            return self.parts[:, part, :, :]
        return self.parts[:, part, :, at(it * S, S)]

    def vector_norm(self, nc, dve, x, held, it):
        for tt in range(TB):
            nc.vector.bn_stats(self.st[:, tt, :], x[:, at(it * TB + tt), :]).then_inc(self.stats_done, 1)
        dve.wait_ge(self.stats_done, it * TB + TB)
        dve.sem_inc(held, 1)
        for tt in range(TB):
            last = nc.vector.bn_aggr(self.mv[:, tt, :], self.st[:, tt, :])
        last.then_inc(self.aggr_done, 1)
        dve.wait_ge(self.rstd_done, it + 1)
        for tt in range(TB):
            last = nc.vector.tensor_scalar(self.xn[:, tt, :], x[:, at(it * TB + tt), :], self.mv[:, tt, 0:1],
                                           self.rstd[:, tt:tt + 1], ALU.subtract, ALU.mult)
        last.then_inc(self.xn_done, 1)

    def pool_rstd(self, nc, pool, t, held, it):
        pool.wait_ge(self.aggr_done, it + 1)
        pool.sem_inc(held, 1)
        nc.gpsimd.tensor_scalar(self.rstd[:, :], self.mv[:, :, 1], EPS_LN, None, ALU.add).then_inc(self.var_eps, 1)
        pool.wait_ge(self.var_eps, it + 1)
        nc.gpsimd.tensor_tensor(self.rstd[:, :], self.rstd[:, :], t["neg_half"][:, 0:TB], ALU.pow).then_inc(self.rstd_done, 1)

    def tensor_turn(self, nc, pe, t, ps, it):
        pe.wait_ge(self.xn_done, it + 1)
        for k in range(KT):
            for tt in range(TB):
                last = nc.tensor.transpose(ps[:, self.slot + k, tt * P:(tt + 1) * P], self.xn[:, tt, k * P:(k + 1) * P],
                                           t["ident"][:, :])
        last.then_inc(self.turned, 1)

    def scalar_high(self, nc, act, t, ps, it):
        act.wait_ge(self.turned, it + 1)
        for k in range(KT):
            nc.scalar.activation(self.ht[:, k, :], ps[:, self.slot + k, :], ACT.Identity,
                                 scale=t["mod"][:, self.layer, self.shift_part + 1, k, at(it)],
                                 bias=t["mod"][:, self.layer, self.shift_part, k, at(it)]).then_inc(self.ht_done, 1)
        act.wait_ge(self.ht_done, it * KT + KT)
        nc.scalar.copy(self.out(0, it), self.ht[:, :, :]).then_inc(self.high_done, 1)

    def vector_low(self, nc, dve, it):
        dve.wait_ge(self.high_done, it + 1)
        nc.vector.tensor_tensor(self.out(1, it), self.ht[:, :, :], self.out(0, it).bitcast(F32),
                                ALU.subtract).then_inc(self.low_done, 1)


def ffn0_stage(nc, t, d):
    x = t["x"]
    with ExitStack() as ctx:
        n = Names(nc, ctx, "ffn0")
        hp = n.sb("hp", [P, 2, KT, S], F32R)
        wraw = n.sb("wraw", [P, KT, D], F32)
        rows = n.sb("rows", [P, 2, D], F32)
        w = n.sb("w", [P, KT, D], F32)
        wp = n.sb("wp", [P, 2, KT, D], F32R)
        gbias = n.sb("gbias", [P, B, D], F32)
        upd = n.sb("upd", [P, TB, D], F32)
        ps = n.psum()
        norm_a = SplitNorm(n, "a", 0, 3, hp, 0)
        norm_b = SplitNorm(n, "b", 1, 0, t["h_parts"], 2)
        loaded, w_scaled, w_high, w_ready = n.sem("loaded"), n.sem("w_scaled"), n.sem("w_high"), n.sem("w_ready")
        gbias_ready = n.sem("gbias_ready")
        made, upd_done, x_done, bias_added = n.sem("made"), n.sem("upd_done"), n.sem("x_done"), n.sem("bias_added")
        dve_held, pool_held = n.sem("dve_held"), n.sem("pool_held")
        OUT = 4

        with nc.Block() as block:

            @block.sync
            def _(sp):
                sp.dma_start(wraw[:, :, :], d["wffn"]).then_inc(loaded, 16)
                sp.dma_start(rows[:, :, :], d["ffn_rows"]).then_inc(loaded, 16)

            @block.tensor
            def _(pe):
                pe.wait_ge(w_ready, 1)

                def batch(it, first):
                    norm_a.tensor_turn(nc, pe, t, ps, it)
                    pe.wait_ge(norm_a.low_done, it + 1)
                    if not first:
                        pe.wait_ge(upd_done, it * 2)
                    for tt in range(TB):
                        for m, (k, (a, c)) in enumerate([(k, tc) for k in range(KT) for tc in TERMS]):
                            last = nc.tensor.matmul(ps[:, OUT + tt // 2, (tt % 2) * D:(tt % 2 + 1) * D],
                                                    hp[:, a, k, tt * P:(tt + 1) * P], wp[:, c, k, :],
                                                    start=(m == 0), stop=(m == 5))
                        if tt % 2:
                            last.then_inc(made, 1)
                    norm_b.tensor_turn(nc, pe, t, ps, it)

                batch(0, True)
                with pe.Fori(1, B) as it:
                    batch(it, False)

            @block.scalar
            def _(act):
                act.wait_ge(w_scaled, 1)
                nc.scalar.copy(wp[:, 0], w[:, :, :]).then_inc(w_high, 1)
                with act.Fori(0, B) as it:
                    norm_a.scalar_high(nc, act, t, ps, it)
                    norm_b.scalar_high(nc, act, t, ps, it)

            @block.vector
            def _(dve):
                dve.wait_ge(loaded, 32)
                nc.vector.tensor_tensor(w[:, :, :], wraw[:, :, :], rows[:, 0:1, :].to_broadcast([P, KT, D]),
                                        ALU.mult).then_inc(w_scaled, 1)
                dve.wait_ge(w_high, 1)
                nc.vector.tensor_tensor(wp[:, 1], w[:, :, :], wp[:, 0].bitcast(F32), ALU.subtract).then_inc(w_ready, 1)
                with dve.Fori(0, B) as it:
                    norm_a.vector_norm(nc, dve, x, dve_held, it)
                    norm_a.vector_low(nc, dve, it)
                    for i in range(2):
                        dve.wait_ge(made, it * 2 + (i + 1))
                        nc.vector.tensor_tensor(upd[:, 2 * i:2 * i + 2, :],
                                                ps[:, OUT + i, :].rearrange("p (t n) -> p t n", t=2),
                                                t["gate"][:, 1, bass.ds(it, 1), :].to_broadcast([P, 2, D]),
                                                ALU.mult).then_inc(upd_done, 1)
                    dve.wait_ge(x_done, it * 2 + 2)
                    dve.sem_inc(dve_held, 1)
                    norm_b.vector_norm(nc, dve, x, dve_held, it)
                    norm_b.vector_low(nc, dve, it)

            @block.gpsimd
            def _(pool):
                pool.wait_ge(loaded, 32)
                nc.gpsimd.tensor_tensor(gbias[:, :, :], t["gate"][:, 1], rows[:, 1:2, :].to_broadcast([P, B, D]),
                                        ALU.mult).then_inc(gbias_ready, 1)
                pool.wait_ge(gbias_ready, 1)
                with pool.Fori(0, B) as it:
                    norm_a.pool_rstd(nc, pool, t, pool_held, it)
                    pool.wait_ge(norm_a.xn_done, it + 1)
                    pool.sem_inc(pool_held, 1)
                    xb = x[:, bass.ds(it * TB, TB), :]
                    nc.gpsimd.tensor_tensor(xb, xb, gbias[:, bass.ds(it, 1), :].to_broadcast([P, TB, D]),
                                            ALU.add).then_inc(bias_added, 1)
                    pool.wait_ge(bias_added, it + 1)
                    pool.sem_inc(pool_held, 1)
                    for i in range(2):
                        pool.wait_ge(upd_done, it * 2 + (i + 1))
                        pool.sem_inc(pool_held, 1)
                        xs = x[:, bass.ds(it * TB + 2 * i, 2), :]
                        nc.gpsimd.tensor_tensor(xs, xs, upd[:, 2 * i:2 * i + 2, :], ALU.add).then_inc(x_done, 1)
                    norm_b.pool_rstd(nc, pool, t, pool_held, it)


TERMS = ((0, 0), (0, 1), (1, 0))


def attention1_order():
    order = []
    for u in range(UNITS):
        order += [("s", u, 0), ("q", u), ("s", u, 1), ("pv", u, 0), ("s", u, 2)]
        if u % 2 == 0:
            order += [("y", u, 0), ("y", u, 1)]
        order += [("k", u), ("pv", u, 1), ("s", u, 3), ("pv", u, 2), ("g", u)]
        if u % 2 == 1:
            order += [("v", u, 0), ("v", u, 1)]
        order += [("pv", u, 3)]
    return order


def attention1_stage(nc, t, d):
    order = attention1_order()
    ring_tasks = [task for task in order if task[0] in "sqkgv"]
    RING, AHEAD = 4, 5
    first_tasks = [("q", -1), ("k", -1), ("g", -1), ("v", -1, 0), ("v", -1, 1)]
    place = {task: n + AHEAD for n, task in enumerate(ring_tasks)} | {task: n for n, task in enumerate(first_tasks)}
    assert len(ring_tasks) % RING == 0
    turns = len(ring_tasks) // RING
    NB = S // P
    OFF = [sum(S - i * P for i in range(j)) for j in range(NB)]
    NP = sum(S - j * P for j in range(NB))
    hh = t["h_parts"]
    with ExitStack() as ctx:
        n = Names(nc, ctx, "attn1")
        wraw = n.sb("wraw", [P, KT, 8 * P], F32)
        wp = n.sb("wp", [P, 2, KT, 8 * P], F32R)
        woraw = n.sb("woraw", [P, 2, D], F32)
        wop = n.sb("wop", [P, 2, 2, D], F32R)
        normw = n.sb("normw", [P, H1], F32)
        mask = n.sb("mask", [P, 2, S], F32)
        qk = n.sb("qk", [P, 2, S], F32)
        qkp = n.sb("qkp", [P, 2, 2, 2, S], F32R)
        v = n.sb("v", [P, TB, 2 * P], F32)
        vp = n.sb("vp", [P, 2, 2, TB, 2 * P], F32R)
        gate = n.sb("gate", [P, 2, S], F32)
        p = n.sb("p", [P, NP], F32)
        pp = n.sb("pp", [P, 2, NP], F32R)
        y = n.sb("y", [P, 2, S], F32)
        yp = n.sb("yp", [P, 2, 2, S], F32R)
        sq = n.sb("sq", [P, 2, S], F32)
        ssq = n.sb("ssq", [P, B * S], F32)
        ones = n.sb("ones", [P, 1], F32)
        yacc, rms = t["yacc"], t["rms"]
        ps = n.psum()
        O_BANK, Y_BANK = 4, 6

        ring_full = n.sems("ring_full", RING)
        w_loaded, wo_loaded, mask_loaded = n.sem("w_loaded"), n.sem("wo_loaded"), n.sems("mask_loaded", 2)
        w_hi, w_ready = n.sems("w_hi", 3), n.sems("w_ready", 3)
        norm_loaded, norm_halved = n.sem("norm_loaded"), n.sem("norm_halved")
        wo_scaled, wo_hi, wo_ready = n.sem("wo_scaled"), n.sem("wo_hi"), n.sem("wo_ready")
        q_silu, q_hi, q_ready = n.sem("q_silu"), n.sem("q_hi"), n.sem("q_ready")
        k_silu, k_hi, k_ready = n.sem("k_silu"), n.sem("k_hi"), n.sem("k_ready")
        v_silu, v_hi, v_ready = n.sem("v_silu"), n.sem("v_hi"), n.sem("v_ready")
        gate_done = n.sem("gate_done")
        p_masked, p_hi, p_ready = n.sem("p_masked"), n.sem("p_hi"), n.sem("p_ready")
        o_full, gated, y_hi, y_ready = n.sem("o_full"), n.sem("gated"), n.sem("y_hi"), n.sem("y_ready")
        squared, summed = n.sem("squared"), n.sem("summed")
        y_full, y_added = n.sem("y_full"), n.sem("y_added")
        zeroed, ssq_full, mean_done, rms_done = n.sem("zeroed"), n.sem("ssq_full"), n.sem("mean_done"), n.sem("rms_done")

        def bank(task):
            return ps[:, place[task] % RING, :]

        def filled(eng, task, it):
            m = place[task]
            missing = 1 if isinstance(it, int) and it == PAIRS - 1 and task == ("s", UNITS - 1, NB - 1) else 0
            eng.wait_ge(ring_full[m % RING], it * turns + (m // RING + 1 - missing))

        def emptied(eng, task, it):
            kind, u = task[0], task[1]
            if kind == "s":
                eng.wait_ge(p_masked, it * (UNITS * NB) + (u * NB + task[2] + 1))
            elif kind == "v":
                eng.wait_ge(v_silu, it * (2 * B) + (u + 1 + task[2] + 1))
            else:
                eng.wait_ge({"q": q_silu, "k": k_silu, "g": gate_done}[kind], it * UNITS + (u + 2))

        PART = (slice(0, 3 * P), slice(3 * P, 6 * P), slice(6 * P, 8 * P))

        def over_pairs(eng, body):
            body(0, True, False)
            with eng.Fori(1, PAIRS - 1) as it:
                body(it, False, False)
            body(PAIRS - 1, False, True)

        with nc.Block() as block:

            @block.sync
            def _(sp):
                sp.dma_start(wraw[:, :, :], d["w1p"][0]).then_inc(w_loaded, 16)
                sp.dma_start(normw[:, :], d["norm_w"]).then_inc(norm_loaded, 16)
                for h in range(2):
                    sp.dma_start(mask[:, h, :], t["decay_dram"][h]).then_inc(mask_loaded[h], 16)
                sp.dma_start(woraw[:, :, :], d["wout"][0]).then_inc(wo_loaded, 16)
                with sp.Fori(0, PAIRS - 1) as it:
                    sp.wait_ge(w_ready[1], it + 1)
                    sp.dma_start(wraw[:, :, :], d["w1p"][bass.ds(it + 1, 1)].rearrange("a p k n -> (a p) k n")
                                 ).then_inc(w_loaded, 16)
                    sp.wait_ge(wo_ready, it + 1)
                    sp.dma_start(woraw[:, :, :], d["wout"][bass.ds(it + 1, 1)].rearrange("a p k n -> (a p) k n")
                                 ).then_inc(wo_loaded, 16)
                    for h in range(2):
                        sp.wait_ge(p_masked, it * (UNITS * NB) + (UNITS - 1 + h) * NB)
                        sp.dma_start(mask[:, h, :], t["decay_dram"][bass.ds(it * 2 + (2 + h), 1)].rearrange(
                            "a p n -> (a p) n")).then_inc(mask_loaded[h], 16)

            @block.tensor
            def _(pe):
                def project(task, unit, it):
                    kind, nx = task[0], (unit + 1) % UNITS
                    b, h = nx // 2, nx % 2
                    pair = it + (unit + 1) // UNITS
                    out = bank(task)
                    if kind == "v":
                        if nx == 0:
                            pe.wait_ge(w_ready[2], pair + 1)
                        for i in range(2):
                            tt = b * TB + 2 * task[2] + i
                            for m, (k, (a, c)) in enumerate([(k, tc) for k in range(KT) for tc in TERMS]):
                                last = nc.tensor.matmul(out[:, i * 2 * P:(i + 1) * 2 * P], hh[:, a, k, tt * P:(tt + 1) * P],
                                                        wp[:, c, k, PART[2]], start=(m == 0), stop=(m == 5))
                    else:
                        if kind == "q" and b == 0:
                            pe.wait_ge(w_ready[h], pair + 1)
                        col = h * 3 * P + "qkg".index(kind) * P
                        for m, (k, (a, c)) in enumerate([(k, tc) for k in range(KT) for tc in TERMS]):
                            last = nc.tensor.matmul(out, wp[:, a, k, col:col + P], hh[:, c, k, b * S:(b + 1) * S],
                                                    start=(m == 0), stop=(m == 5))
                    last.then_inc(ring_full[place[task] % RING], 1)

                def output(task, pair, b):
                    i = task[2]
                    for half in range(2):
                        tt = 2 * i + half
                        for m, (h, (a, c)) in enumerate([(h, tc) for h in range(2) for tc in TERMS]):
                            last = nc.tensor.matmul(ps[:, Y_BANK + i, half * D:(half + 1) * D],
                                                    yp[:, a, h, tt * P:(tt + 1) * P], wop[:, c, h, :],
                                                    start=(m == 0), stop=(m == 5))
                    last.then_inc(y_full, 1)

                def body(it, first, last_pair):
                    for task in order:
                        kind, u = task[0], task[1]
                        b, h = u // 2, u % 2
                        if kind in "sqkgv":
                            if kind != "s" and u == UNITS - 1 and last_pair:
                                continue
                            m = place[task]
                            i = ring_tasks.index(task) - RING
                            if last_pair and i >= 0 and ring_tasks[i] == ("q", UNITS - 1):
                                i -= RING
                            if i >= 0:
                                emptied(pe, ring_tasks[i], it)
                            elif first:
                                emptied(pe, first_tasks[i], 0)
                            else:
                                emptied(pe, ring_tasks[i], it - 1)
                            if kind != "s":
                                project(task, u, it)
                                continue
                            j = task[2]
                            if j == 0:
                                pe.wait_ge(q_ready, it * UNITS + (u + 1))
                                pe.wait_ge(k_ready, it * UNITS + (u + 1))
                            for m3, (a, c) in enumerate(TERMS):
                                last = nc.tensor.matmul(bank(task)[:, 0:S - j * P], qkp[:, h, a, 1, j * P:(j + 1) * P],
                                                        qkp[:, h, c, 0, j * P:S], start=(m3 == 0), stop=(m3 == 2))
                            last.then_inc(ring_full[m % RING], 1)
                        elif kind == "pv":
                            j = task[2]
                            if j == 0 and h == 0:
                                pe.wait_ge(v_ready, it * (2 * B) + (2 * b + 2))
                            if j == 0 and not (first and u < 2):
                                pe.wait_ge(squared, it * UNITS + (u - 1))
                            pe.wait_ge(p_ready, it * (UNITS * NB) + (u * NB + j + 1))
                            for m3, (a, c) in enumerate(TERMS):
                                last = nc.tensor.matmul(ps[:, O_BANK + h, j * P:S], vp[:, b % 2, a, j, h * P:(h + 1) * P],
                                                        pp[:, c, OFF[j]:OFF[j] + S - j * P],
                                                        start=(j == 0 and m3 == 0), stop=(j == NB - 1 and m3 == 2))
                            if j == NB - 1:
                                last.then_inc(o_full, 1)
                        else:
                            if first and u == 0:
                                continue
                            if task[2] == 0:
                                pe.wait_ge(y_ready, it * UNITS + u)
                                if u == 2:
                                    pe.wait_ge(wo_ready, it + 1)
                                if not (first and u == 2):
                                    pe.wait_ge(y_added, it * (2 * B) + (u - 2))
                            output(task, it, None)

                for n0, task in enumerate(first_tasks):
                    if n0 >= RING:
                        emptied(pe, first_tasks[n0 - RING], 0)
                    project(task, -1, 0)
                over_pairs(pe, body)
                pe.wait_ge(y_ready, PAIRS * UNITS)
                pe.wait_ge(y_added, PAIRS * 2 * B - 2)
                for i in range(2):
                    output(("y", 0, i), PAIRS, None)
                pe.wait_ge(summed, PAIRS * UNITS)
                for tt in range(NT):
                    last = nc.tensor.matmul(ps[:, 0, tt:tt + 1], ssq[:, tt * P:(tt + 1) * P], ones[:, :],
                                            start=True, stop=True)
                last.then_inc(ssq_full, 1)

            @block.scalar
            def _(act):
                def split_weights(part, it):
                    act.wait_ge(w_loaded, it * 16 + 16)
                    nc.scalar.copy(wp[:, 0, :, PART[part]], wraw[:, :, PART[part]]).then_inc(w_hi[part], 1)

                def silu_split(task, which, unit, it, last_count):
                    silu_sem, hi_sem, ready = ((q_silu, q_hi, q_ready), (k_silu, k_hi, k_ready))[which]
                    filled(act, task, it)
                    if unit >= 0:
                        act.wait_ge(ready, it * UNITS + (unit + 1))
                    ins = nc.scalar.activation(qk[:, which, :], bank(task), ACT.Silu)
                    ins.then_inc(silu_sem, 1)
                    act.wait_ge(silu_sem, it * UNITS + (unit + 2))
                    nc.scalar.copy(qkp[:, (unit + 1) % 2, 0, which, :], qk[:, which, :]).then_inc(hi_sem, 1)

                def gate_of(task, unit, it, first):
                    filled(act, task, it)
                    if unit >= 0 and not (first and unit == 0):
                        act.wait_ge(gated, it * UNITS + unit)
                    nc.scalar.activation(gate[:, (unit + 1) % 2, :], bank(task), ACT.Tanh, scale=0.5).then_inc(gate_done, 1)

                def values_of(task, unit, it):
                    i, nb = task[2], (unit + 1) // 2
                    filled(act, task, it)
                    if unit >= 0:
                        act.wait_ge(v_ready, it * (2 * B) + (2 * nb - 1 + i))
                    nc.scalar.activation(v[:, 2 * i:2 * i + 2, :].rearrange("p t n -> p (t n)"), bank(task),
                                         ACT.Silu).then_inc(v_silu, 1)
                    act.wait_ge(v_silu, it * (2 * B) + (2 * nb + i + 1))
                    nc.scalar.copy(vp[:, nb % 2, 0, 2 * i:2 * i + 2, :], v[:, 2 * i:2 * i + 2, :]).then_inc(v_hi, 1)

                def scores_hi(u, j, it):
                    act.wait_ge(p_masked, it * (UNITS * NB) + (u * NB + j + 1))
                    cols = slice(OFF[j], OFF[j] + S - j * P)
                    nc.scalar.copy(pp[:, 0, cols], p[:, cols]).then_inc(p_hi, 1)

                def finish_unit(u, it):
                    h = (u - 1) % 2
                    act.wait_ge(gated, it * UNITS + u)
                    nc.scalar.copy(yp[:, 0, h, :], y[:, h, :]).then_inc(y_hi, 1)

                def square_unit(u, it, few):
                    h = (u - 1) % 2
                    if not few:
                        act.wait_ge(summed, it * UNITS + (u - 2))
                    nc.scalar.activation(sq[:, h, :], ps[:, O_BANK + h, :], ACT.Square).then_inc(squared, 1)

                for part in (0, 2, 1):
                    split_weights(part, 0)
                silu_split(("q", -1), 0, -1, 0, None)
                silu_split(("k", -1), 1, -1, 0, None)
                gate_of(("g", -1), -1, 0, True)
                for i in range(2):
                    values_of(("v", -1, i), -1, 0)

                def body(it, first, last_pair):
                    for u in range(UNITS):
                        more = not (last_pair and u == UNITS - 1)
                        scores_hi(u, 0, it)
                        if u == UNITS - 2 and not last_pair:
                            filled(act, ("v", UNITS - 3, 1), it)
                            for part in (0, 2):
                                split_weights(part, it + 1)
                        if u == UNITS - 1 and not last_pair:
                            filled(act, ("g", UNITS - 2), it)
                            split_weights(1, it + 1)
                        if not (first and u == 0):
                            finish_unit(u, it)
                            square_unit(u, it, first and u < 3)
                        if more:
                            silu_split(("q", u), 0, u, it, None)
                        scores_hi(u, 1, it)
                        scores_hi(u, 2, it)
                        if more:
                            silu_split(("k", u), 1, u, it, None)
                        scores_hi(u, 3, it)
                        if more:
                            gate_of(("g", u), u, it, first)
                            if u % 2 == 1:
                                for i in range(2):
                                    values_of(("v", u, i), u, it)
                        if u == 1:
                            if not first:
                                act.wait_ge(y_full, it * (2 * B))
                            act.wait_ge(wo_scaled, it * 2 + 2)
                            nc.scalar.copy(wop[:, 0], woraw[:, :, :]).then_inc(wo_hi, 1)

                over_pairs(act, body)
                finish_unit(UNITS, PAIRS - 1)
                square_unit(UNITS, PAIRS - 1, False)

            @block.vector
            def _(dve):
                def low(out, whole, high, ready):
                    nc.vector.tensor_tensor(out, whole, high.bitcast(F32), ALU.subtract).then_inc(ready, 1)

                def qk_low(which, unit, it):
                    hi_sem, ready = ((q_hi, q_ready), (k_hi, k_ready))[which]
                    dve.wait_ge(hi_sem, it * UNITS + (unit + 2))
                    low(qkp[:, (unit + 1) % 2, 1, which, :], qk[:, which, :], qkp[:, (unit + 1) % 2, 0, which, :], ready)

                def values_low(i, unit, it):
                    nb = (unit + 1) // 2
                    dve.wait_ge(v_hi, it * (2 * B) + (2 * nb + i + 1))
                    rows = slice(2 * i, 2 * i + 2)
                    low(vp[:, nb % 2, 1, rows, :], v[:, rows, :], vp[:, nb % 2, 0, rows, :], v_ready)

                def masked(u, j, it):
                    task = ("s", u, j)
                    cols = slice(OFF[j], OFF[j] + S - j * P)
                    filled(dve, task, it)
                    if u < 2 and j == 0:
                        dve.wait_ge(mask_loaded[u % 2], it * 16 + 16)
                    nc.vector.tensor_tensor(p[:, cols], bank(task)[:, 0:S - j * P], mask[:, u % 2, 0:S - j * P],
                                            ALU.mult).then_inc(p_masked, 1)

                def scores_low(u, j, it):
                    cols = slice(OFF[j], OFF[j] + S - j * P)
                    dve.wait_ge(p_hi, it * (UNITS * NB) + (u * NB + j + 1))
                    low(pp[:, 1, cols], p[:, cols], pp[:, 0, cols], p_ready)

                def gate_unit(u, it):
                    h = (u - 1) % 2
                    dve.wait_ge(o_full, it * UNITS + u)
                    dve.wait_ge(gate_done, it * UNITS + u)
                    nc.vector.scalar_tensor_tensor(y[:, h, :], gate[:, h, :], 1.0, ps[:, O_BANK + h, :],
                                                   ALU.add, ALU.mult).then_inc(gated, 1)

                def y_low(u, it):
                    h = (u - 1) % 2
                    dve.wait_ge(y_hi, it * UNITS + u)
                    low(yp[:, 1, h, :], y[:, h, :], yp[:, 0, h, :], y_ready)

                def add_output(u, i, it):
                    b = (u // 2 - 1) % B
                    dve.wait_ge(y_full, it * (2 * B) + (u - 1 + i))
                    rows = yacc[:, b * TB + 2 * i:b * TB + 2 * i + 2, :].rearrange("p t n -> p (t n)")
                    nc.vector.tensor_tensor(rows, rows, ps[:, Y_BANK + i, :], ALU.add).then_inc(y_added, 1)

                nc.vector.memset(yacc[:, :, :], 0.0).then_inc(zeroed, 1)
                dve.wait_ge(norm_loaded, 16)
                nc.vector.tensor_scalar(normw[:, :], normw[:, :], 0.5, None, ALU.mult).then_inc(norm_halved, 1)
                dve.wait_ge(norm_halved, 1)
                dve.wait_ge(zeroed, 1)
                qk_low(0, -1, 0)
                qk_low(1, -1, 0)
                for i in range(2):
                    values_low(i, -1, 0)

                def body(it, first, last_pair):
                    for u in range(UNITS):
                        more = not (last_pair and u == UNITS - 1)
                        before = not (first and u == 0)
                        if u == 1:
                            dve.wait_ge(wo_loaded, it * 16 + 16)
                            for h in range(2):
                                col = normw[:, bass.ds(it * 2 + h, 1)] if not isinstance(it, int) else normw[:, 2 * it + h:2 * it + h + 1]
                                nc.vector.tensor_scalar(woraw[:, h, :], woraw[:, h, :], col, None,
                                                        ALU.mult).then_inc(wo_scaled, 1)
                        if before:
                            gate_unit(u, it)
                        masked(u, 0, it)
                        if before:
                            y_low(u, it)
                        scores_low(u, 0, it)
                        masked(u, 1, it)
                        if more:
                            qk_low(0, u, it)
                        scores_low(u, 1, it)
                        masked(u, 2, it)
                        scores_low(u, 2, it)
                        if before and u % 2 == 0:
                            for i in range(2):
                                add_output(u, i, it)
                        if more:
                            qk_low(1, u, it)
                        masked(u, 3, it)
                        scores_low(u, 3, it)
                        if more and u % 2 == 1:
                            for i in range(2):
                                values_low(i, u, it)

                over_pairs(dve, body)
                gate_unit(UNITS, PAIRS - 1)
                y_low(UNITS, PAIRS - 1)
                for i in range(2):
                    add_output(UNITS, i, PAIRS - 1)
                dve.wait_ge(ssq_full, 1)
                nc.vector.tensor_scalar(rms[:, :], ps[:, 0, 0:NT], 1.0 / (H1 * D1), EPS_RMS, ALU.mult,
                                        ALU.add).then_inc(mean_done, 1)

            @block.gpsimd
            def _(pool):
                nc.gpsimd.memset(ones[:, :], 1.0)

                def weights_low(part, it):
                    pool.wait_ge(w_hi[part], it + 1)
                    nc.gpsimd.tensor_tensor(wp[:, 1, :, PART[part]], wraw[:, :, PART[part]],
                                            wp[:, 0, :, PART[part]].bitcast(F32), ALU.subtract).then_inc(w_ready[part], 1)

                def sum_unit(u, it, first_pair):
                    b, h = ((u - 1) % UNITS) // 2, (u - 1) % 2
                    pool.wait_ge(squared, it * UNITS + u)
                    if h == 1:
                        pool.wait_ge(summed, it * UNITS + (u - 1))
                    cols = ssq[:, b * S:(b + 1) * S]
                    nc.gpsimd.tensor_tensor(cols, cols, sq[:, h, :], ALU.add).then_inc(summed, 1)

                sums_zeroed = n.sem("sums_zeroed")
                nc.gpsimd.memset(ssq[:, :], 0.0).then_inc(sums_zeroed, 1)
                for part in (0, 2, 1):
                    weights_low(part, 0)
                pool.wait_ge(sums_zeroed, 1)

                def body(it, first, last_pair):
                    for u in range(UNITS):
                        if u == UNITS - 2 and not last_pair:
                            for part in (0, 2):
                                weights_low(part, it + 1)
                        if u == UNITS - 1 and not last_pair:
                            weights_low(1, it + 1)
                        if not (first and u == 0):
                            sum_unit(u, it, first)
                        if u == 1:
                            pool.wait_ge(wo_hi, it + 1)
                            nc.gpsimd.tensor_tensor(wop[:, 1], woraw[:, :, :], wop[:, 0].bitcast(F32),
                                                    ALU.subtract).then_inc(wo_ready, 1)

                over_pairs(pool, body)
                sum_unit(UNITS, PAIRS - 1, False)
                pool.wait_ge(mean_done, 1)
                nc.gpsimd.tensor_tensor(rms[:, :], rms[:, :], t["neg_half"][:, :], ALU.pow).then_inc(rms_done, 1)


def experts_stage(nc, t, d):
    x, yacc, rms, hh = t["x"], t["yacc"], t["rms"], t["h_parts"]
    TE = FE // P
    PIECES = 12
    PC = FT * P // 2
    LEFT = PIECES - 2
    with ExitStack() as ctx:
        n = Names(nc, ctx, "experts")
        wg = n.sb("wg", [P, 2, KT, FT * P], F32R)
        wu = n.sb("wu", [P, 2, KT, FT * P], F32R)
        w2 = n.sb("w2", [P, 2, FT, D], F32R)
        raw = n.sb("raw", [P, 2, PC], F32)
        rw = n.sb("rw", [P, KT, E], F32)
        rwp = n.sb("rwp", [P, 2, KT, E], F32R)
        spread32 = n.sb("spread32", [EROWS, FE], F32)
        spread = n.sb("spread", [EROWS, FE], BF16)
        expert_id = n.sb("expert_id", [P, E], F32)
        tile8 = [P, NT, E]
        scores = n.sb("scores", tile8, F32)
        norm1 = n.sb("norm1", [P, NT], F32)
        best = n.sb("best", tile8, F32)
        best_id = n.sb("best_id", tile8, U32)
        best_idf = n.sb("best_idf", tile8, F32)
        chosen = n.sb("chosen", [P, 2, NT, E], F32)
        cw = n.sb("cw", tile8, F32)
        rest = n.sb("rest", tile8, F32)
        cwp = n.sb("cwp", [P, NT, 3, E], BF16)
        cwt = n.sb("cwt", [EROWS, B * S], BF16)
        hid = n.sb("hid", [P, 2, S], F32)
        hidp = n.sb("hidp", [P, 2, 2, S], F32R)
        ps = n.psum()
        norm = SplitNorm(n, "n", 1, 3, hh, 0)
        sg = yacc[:, 0:4, :].rearrange("p (b t) n -> p b (t n)", b=2)
        paired = yacc[:, 4:8, :].rearrange("p (b t) n -> p b (t n)", b=2)
        upd = norm.xn

        raw_loaded, raw_high, raw_low = n.sems("raw_loaded", 2), n.sem("raw_high"), n.sem("raw_low")
        small_loaded, spread_cast, rw_high, rw_low = (n.sem(s) for s in ("small_loaded", "spread_cast", "rw_high", "rw_low"))
        scaled, x_added, dve_held, pool_held = n.sem("scaled"), n.sem("x_added"), n.sem("dve_held"), n.sem("pool_held")
        logits_made, router, exp_done = n.sem("logits_made"), n.sem("router"), n.sem("exp_done")
        ids_ready, cwp_done, cw_turned, cwt_done = (n.sem(s) for s in ("ids_ready", "cwp_done", "cw_turned", "cwt_done"))
        g_made, u_made, c_made, y_made = (n.sem(s) for s in ("g_made", "u_made", "c_made", "y_made"))
        silu_done, pair_done, hid_done, hid_high, hid_low = (
            n.sem(s) for s in ("silu_done", "pair_done", "hid_done", "hid_high", "hid_low"))
        down_done, pe_held = n.sem("down_done"), n.sem("pe_held")
        upd_done, stored = n.sem("upd_done"), n.sem("stored")
        G_BANK, U_BANK, C_BANK, Y_BANK, L_BANK = 0, 1, 2, 4, 3

        def piece(m):
            which, rest_ = m // 4, m % 4
            k, cols = rest_ // 2, slice((rest_ % 2) * PC, (rest_ % 2 + 1) * PC)
            if which < 2:
                return d["wg" if which == 0 else "wu"][:, k, cols], [(wg, wu)[which][:, c, k, cols] for c in range(2)]
            cols = slice(rest_ * (FT * D // 4), (rest_ + 1) * (FT * D // 4))
            return (d["w2"].rearrange("p f n -> p (f n)")[:, cols],
                    [w2[:, c].rearrange("p f n -> p (f n)")[:, cols] for c in range(2)])

        with nc.Block() as block:

            @block.sync
            def _(sp):
                sp.dma_start(rw[:, :, :], d["router"]).then_inc(small_loaded, 16)
                sp.dma_start(spread32[:, :], d["spread"]).then_inc(small_loaded, 16)
                for m in range(PIECES):
                    if m >= 2:
                        sp.wait_ge(raw_low, m - 1)
                    sp.dma_start(raw[:, m % 2, :], piece(m)[0]).then_inc(raw_loaded[m % 2], 16)
                with sp.Fori(0, B) as it:
                    sp.wait_ge(x_added, it + (B + 1))
                    sp.dma_start(t["out"][:, bass.ds(it * TB, TB), :], x[:, bass.ds(it * TB, TB), :]).then_inc(stored, 16)
                sp.wait_ge(stored, 16 * B)

            @block.tensor
            def _(pe):
                with pe.Fori(0, B) as it:
                    norm.tensor_turn(nc, pe, t, ps, it)
                pe.wait_ge(norm.low_done, B)
                pe.wait_ge(rw_low, 1)
                for tt in range(NT):
                    for m, (k, (a, c)) in enumerate([(k, tc) for k in range(KT) for tc in TERMS]):
                        last = nc.tensor.matmul(ps[:, L_BANK, tt * E:(tt + 1) * E], hh[:, a, k, tt * P:(tt + 1) * P],
                                                rwp[:, c, k, :], start=(m == 0), stop=(m == 5))
                last.then_inc(logits_made, 1)

                def hidden(w, bank, f, it, full):
                    for m, (k, (a, c)) in enumerate([(k, tc) for k in range(KT) for tc in TERMS]):
                        last = nc.tensor.matmul(ps[:, bank, :], w[:, a, k, f * P:(f + 1) * P],
                                                hh[:, c, k, at(it * S, S)], start=(m == 0), stop=(m == 5))
                    last.then_inc(full, 1)

                def down(f, it, it_f):
                    pe.wait_ge(hid_low, it_f)
                    for tt in range(TB):
                        for m, (a, c) in enumerate(TERMS):
                            last = nc.tensor.matmul(ps[:, Y_BANK + tt, 0:D], hidp[:, f % 2, a, tt * P:(tt + 1) * P],
                                                    w2[:, c, f, :], start=(f == 0 and m == 0), stop=(f == FT - 1 and m == 2))
                    if f == FT - 1:
                        last.then_inc(y_made, 1)
                    else:
                        last.then_inc(down_done, 1)

                def batch(it, first):
                    for f in range(FT):
                        at_f = it * FT + f
                        if not (first and f == 0):
                            pe.wait_ge(silu_done, at_f)
                        hidden(wg, G_BANK, f, it, g_made)
                        if f > TE:
                            pe.wait_ge(hid_done, at_f)
                        elif not (first and f == 0):
                            if f == 0:
                                pe.wait_ge(hid_done, at_f)
                            else:
                                pe.wait_ge(pair_done, it * TE + f)
                        hidden(wu, U_BANK, f, it, u_made)
                        if f < TE:
                            if first and f == 0:
                                pe.wait_ge(cwp_done, 3)
                                turned = ps[:, 6:8, :].bitcast(BF16).rearrange("p a n -> p (a n)")
                                for tt in range(NT):
                                    last = nc.tensor.transpose(turned[0:EROWS, tt * P:(tt + 1) * P],
                                                               cwp[:, tt, :, :].rearrange("p a e -> p (a e)"), t["identb"][:, :])
                                last.then_inc(cw_turned, 1)
                                pe.wait_ge(cwt_done, 1)
                            else:
                                pe.wait_ge(hid_done, at_f)
                            pe.sem_inc(pe_held, 1)
                            nc.tensor.matmul(ps[:, C_BANK, :], spread[:, f * P:(f + 1) * P], cwt[:, at(it * S, S)],
                                             start=True, stop=True).then_inc(c_made, 1)
                        if f > 0:
                            if f == 1 and not first:
                                pe.wait_ge(upd_done, it)
                            down(f - 1, it, at_f)
                        elif not first:
                            down(FT - 1, it, at_f)

                pe.wait_ge(raw_low, PIECES)
                batch(0, True)
                with pe.Fori(1, B) as it:
                    batch(it, False)
                down(FT - 1, B, B * FT)

            @block.scalar
            def _(act):
                def split(m):
                    act.wait_ge(raw_loaded[m % 2], 16 * (m // 2 + 1))
                    nc.scalar.copy(piece(m)[1][0], raw[:, m % 2, :]).then_inc(raw_high, 1)

                act.wait_ge(small_loaded, 32)
                nc.scalar.copy(rwp[:, 0], rw[:, :, :]).then_inc(rw_high, 1)
                nc.scalar.copy(spread[:, :], spread32[:, :]).then_inc(spread_cast, 1)
                for m in range(PIECES):
                    split(m)
                    if m % 3 == 2:
                        norm.scalar_high(nc, act, t, ps, m // 3)
                act.wait_ge(router, 2)
                nc.scalar.activation(scores[:, :, :], scores[:, :, :], ACT.Exp).then_inc(exp_done, 1)

                def high(f, count):
                    act.wait_ge(hid_done, count)
                    nc.scalar.copy(hidp[:, f % 2, 0, :], hid[:, f % 2, :]).then_inc(hid_high, 1)

                def batch(it, first):
                    for f in range(FT):
                        at_f = it * FT + f
                        act.wait_ge(g_made, at_f + 1)
                        nc.scalar.activation(sg[:, f % 2, :], ps[:, G_BANK, :], ACT.Silu).then_inc(silu_done, 1)
                        if f > 0:
                            high(f - 1, at_f)
                    high(FT - 1, it * FT + FT)

                batch(0, True)
                with act.Fori(1, B) as it:
                    batch(it, False)

            @block.vector
            def _(dve):
                dve.wait_ge(rw_high, 1)
                nc.vector.tensor_tensor(rwp[:, 1], rw[:, :, :], rwp[:, 0].bitcast(F32), ALU.subtract).then_inc(rw_low, 1)
                with dve.Fori(0, B) as it:
                    for tt in range(TB):
                        tile = yacc[:, bass.ds(it * TB + tt, 1), :]
                        last = nc.vector.scalar_tensor_tensor(tile, tile, rms[:, bass.ds(it * TB + tt, 1)],
                                                              t["gate"][:, 2, bass.ds(it, 1), :], ALU.mult, ALU.mult)
                    last.then_inc(scaled, 1)
                for b in range(B):
                    dve.wait_ge(x_added, b + 1)
                    norm.vector_norm(nc, dve, x, dve_held, b)
                    norm.vector_low(nc, dve, b)

                step = 0

                def then(ins):
                    nonlocal step
                    step += 1
                    ins.then_inc(router, 1)
                    dve.wait_ge(router, step)

                wide = [P, NT, E]
                lg = ps[:, L_BANK, 0:NT * E].rearrange("p (t e) -> p t e", e=E)
                dve.wait_ge(logits_made, 1)
                then(nc.vector.tensor_reduce(norm1[:, :], lg, AX.X, ALU.max))
                then(nc.vector.tensor_tensor(scores[:, :, :], lg, norm1[:, :].unsqueeze(2).to_broadcast(wide), ALU.subtract))
                dve.wait_ge(exp_done, 1)
                then(nc.vector.tensor_reduce(norm1[:, :], scores[:, :, :], AX.X, ALU.add))
                then(nc.vector.reciprocal(norm1[:, :], norm1[:, :]))
                then(nc.vector.tensor_tensor(scores[:, :, :], scores[:, :, :], norm1[:, :].unsqueeze(2).to_broadcast(wide),
                                             ALU.mult))
                for tt in range(NT):
                    last = nc.vector.max(out=best[:, tt, :], in_=scores[:, tt, :])
                then(last)
                for tt in range(NT):
                    last = nc.vector.max_index(best_id[:, tt, :], best[:, tt, :], scores[:, tt, :])
                then(last)
                then(nc.vector.tensor_copy(best_idf[:, :, :], best_id[:, :, :]))
                then(nc.vector.tensor_reduce(norm1[:, :], best[:, :, 0:2], AX.X, ALU.add))
                then(nc.vector.tensor_scalar(norm1[:, :], norm1[:, :], 1e-20, None, ALU.add))
                then(nc.vector.reciprocal(norm1[:, :], norm1[:, :]))
                then(nc.vector.tensor_tensor(best[:, :, 0:2], best[:, :, 0:2],
                                             norm1[:, :].unsqueeze(2).to_broadcast([P, NT, 2]), ALU.mult))
                dve.wait_ge(ids_ready, 1)
                for c in range(2):
                    last = nc.vector.tensor_tensor(chosen[:, c], expert_id[:, :].unsqueeze(1).to_broadcast(wide),
                                                   best_idf[:, :, c:c + 1].to_broadcast(wide), ALU.is_equal)
                then(last)
                for c in range(2):
                    last = nc.vector.tensor_tensor(chosen[:, c], chosen[:, c], best[:, :, c:c + 1].to_broadcast(wide), ALU.mult)
                then(last)
                then(nc.vector.tensor_tensor(cw[:, :, :], chosen[:, 0], chosen[:, 1], ALU.add))
                nc.vector.tensor_copy(cwp[:, :, 0, :], cw[:, :, :]).then_inc(cwp_done, 1)
                dve.wait_ge(cwp_done, 1)
                then(nc.vector.tensor_tensor(rest[:, :, :], cw[:, :, :], cwp[:, :, 0, :], ALU.subtract))
                nc.vector.tensor_copy(cwp[:, :, 1, :], rest[:, :, :]).then_inc(cwp_done, 1)
                dve.wait_ge(cwp_done, 2)
                nc.vector.tensor_tensor(cwp[:, :, 2, :], rest[:, :, :], cwp[:, :, 1, :], ALU.subtract).then_inc(cwp_done, 1)
                dve.wait_ge(cw_turned, 1)
                nc.vector.tensor_copy(cwt[:, :], ps[0:EROWS, 6:8, :].bitcast(BF16).rearrange("p a n -> p (a n)")
                                      ).then_inc(cwt_done, 1)

                def low(f, count):
                    dve.wait_ge(hid_high, count)
                    nc.vector.tensor_tensor(hidp[:, f % 2, 1, :], hid[:, f % 2, :], hidp[:, f % 2, 0, :].bitcast(F32),
                                            ALU.subtract).then_inc(hid_low, 1)

                def batch(it, first):
                    for f in range(FT):
                        at_f = it * FT + f
                        dve.wait_ge(u_made, at_f + 1)
                        dve.wait_ge(silu_done, at_f + 1)
                        if f < TE:
                            nc.vector.tensor_tensor(paired[:, f % 2, :], ps[:, U_BANK, :], sg[:, f % 2, :],
                                                    ALU.mult).then_inc(pair_done, 1)
                            dve.wait_ge(pair_done, it * TE + (f + 1))
                            dve.wait_ge(c_made, it * TE + (f + 1))
                            nc.vector.tensor_tensor(hid[:, f % 2, :], ps[:, C_BANK, :], paired[:, f % 2, :],
                                                    ALU.mult).then_inc(hid_done, 1)
                        else:
                            nc.vector.tensor_tensor(hid[:, f % 2, :], ps[:, U_BANK, :], sg[:, f % 2, :],
                                                    ALU.mult).then_inc(hid_done, 1)
                        if f > 0:
                            low(f - 1, at_f)
                        if f == 0 and not first:
                            output(it)
                    low(FT - 1, it * FT + FT)

                def output(it):
                    dve.wait_ge(y_made, it)
                    dve.wait_ge(x_added, it + (B - 1))
                    if isinstance(it, int):
                        g = t["gate"][:, 3, it - 1:it, :]
                    else:
                        g = t["gate"][:, 3, bass.ds(it - 1, 1), :]
                    nc.vector.tensor_tensor(upd[:, :, :], ps[:, Y_BANK:Y_BANK + TB, 0:D], g.to_broadcast([P, TB, D]),
                                            ALU.mult).then_inc(upd_done, 1)

                batch(0, True)
                with dve.Fori(1, B) as it:
                    batch(it, False)
                output(B)

            @block.gpsimd
            def _(pool):
                nc.gpsimd.iota(expert_id[:, :], [[1, E]], base=0, channel_multiplier=0,
                               allow_small_or_imprecise_dtypes=True).then_inc(ids_ready, 1)
                with pool.Fori(0, B) as it:
                    pool.wait_ge(scaled, it + 1)
                    pool.sem_inc(pool_held, 1)
                    xb = x[:, bass.ds(it * TB, TB), :]
                    nc.gpsimd.tensor_tensor(xb, xb, yacc[:, bass.ds(it * TB, TB), :], ALU.add).then_inc(x_added, 1)

                def low(m):
                    pool.wait_ge(raw_high, m + 1)
                    hi, lo = piece(m)[1]
                    nc.gpsimd.tensor_tensor(lo, raw[:, m % 2, :], hi.bitcast(F32), ALU.subtract).then_inc(raw_low, 1)

                for m in range(PIECES):
                    if m % 3 == 0:
                        norm.pool_rstd(nc, pool, t, pool_held, m // 3)
                    low(m)
                with pool.Fori(0, B) as it:
                    pool.wait_ge(upd_done, it + 1)
                    pool.sem_inc(pool_held, 1)
                    xb = x[:, bass.ds(it * TB, TB), :]
                    nc.gpsimd.tensor_tensor(xb, xb, upd[:, :, :], ALU.add).then_inc(x_added, 1)


ALL_STAGES = [modulation_stage, attention0_stage, ffn0_stage, attention1_stage, experts_stage]



def build(nc, ins, out):
    d = dram_views(ins)
    with ExitStack() as ctx:
        n = Names(nc, ctx, "all")
        t = {
            "x": n.sb("x", [P, NT, D], F32),
            "mod": n.sb("mod", [P, 2, 6, KT, B], F32),
            "gate": n.sb("gate", [P, 4, B, D], F32),
            "ident": n.sb("ident", [P, P], F32),
            "ident16": n.sb("ident16", [P, P], F16),
            "identb": n.sb("identb", [P, P], BF16),
            "later_key": n.sb("later_key", [P, P], BF16),
            "later_key_t": n.sb("later_key_t", [P, P], BF16),
            "neg_half": n.sb("neg_half", [P, NT], F32),
            "h_parts": n.sb("h_parts", [P, 2, KT, B * S], F32R),
            "yacc": n.sb("yacc", [P, NT, D], F32),
            "rms": n.sb("rms", [P, NT], F32),
            "out": out,
            "decay_dram": nc.dram_tensor("decay_masks", [H1, P, S], F32, kind="Internal").ap(),
        }
        for stage in ALL_STAGES:
            before = nc.snapshot_sems()
            stage(nc, t, d)
            if stage is not ALL_STAGES[-1]:
                nc.clear_and_free_semaphores(nc.allocated_since(before))
                nc.all_engine_barrier()


def dram_views(ins):
    return {
        "x": ins["x"],
        "cond": ins["cond"],
        "wmod0": ins["wmod0"],
        "wmod1": ins["wmod1"],
        "slope": ins["slope"].partition_broadcast(P),
        "wqkv0": ins["wqkv0"],
        "wo0": ins["wo0"],
        "bias0": ins["bias0"],
        "norm_scale0": ins["norm_scale0"].partition_broadcast(P),
        "cosd": ins["cosd"],
        "sind": ins["sind"],
        "wffn": ins["wffn"],
        "ffn_rows": ins["ffn_rows"].partition_broadcast(P),
        "w1p": ins["w1p"],
        "wout": ins["wout"],
        "norm_w": ins["norm_w"],
        "router": ins["router"],
        "wg": ins["wg"], "wu": ins["wu"], "w2": ins["w2"], "spread": ins["spread"],
    }


def laid_out(i):
    a = {k: np.asarray(v) for k, v in i.items()}

    def rows(w):
        w = np.asarray(w)
        return np.ascontiguousarray(w.reshape(-1, P, w.shape[1]).transpose(1, 0, 2))

    r = {"x": np.ascontiguousarray(a["L0_attn_x"].reshape(NT, P, D).transpose(1, 0, 2))}
    c = np.stack([a["L0_c"], a["L1_c"]])
    r["cond"] = np.ascontiguousarray(c.reshape(2, B, KT, P).transpose(3, 0, 2, 1))
    r["wmod0"], r["wmod1"] = rows(a["L0_wmod"]), rows(a["L1_wmod"])
    r["slope"] = np.ascontiguousarray(a["L1_attn_slope_rate"].reshape(H1))
    r["wqkv0"] = rows(np.concatenate([a["L0_attn_wq"], a["L0_attn_wk"], a["L0_attn_wv"]], 1))
    r["wo0"] = rows(a["L0_attn_wo"])
    r["bias0"] = np.concatenate([a["L0_attn_bq"], a["L0_attn_bk"], a["L0_attn_bv"], a["L0_attn_bo"]])[None]
    r["norm_scale0"] = np.stack([a["L0_attn_q_norm_scale"], a["L0_attn_k_norm_scale"]])
    f = np.float32
    inv = (f(1.0) / np.power(f(10000.0), np.arange(0, D0, 2, dtype=f) / f(D0))).astype(f)
    ang = np.outer(np.arange(S, dtype=f), inv).astype(f)

    def table(v):
        v = np.concatenate([v, v], 1).astype(f)
        return np.ascontiguousarray(v.reshape(TB, P, D0).transpose(1, 0, 2))

    r["cosd"], r["sind"] = table(np.cos(ang)), table(np.sin(ang))
    r["wffn"] = rows(a["L0_ffn_weight"].T)
    r["ffn_rows"] = np.stack([a["L0_ffn_scale_weight"], a["L0_ffn_bias"]])
    wqkv = a["L1_attn_w_qkv"].reshape(H1, 3, D1, D)
    wgate = a["L1_attn_w_gate"].reshape(H1, D1, D)
    pairs = []
    for p in range(PAIRS):
        h = [2 * p, 2 * p + 1]
        pairs.append(rows(np.concatenate([wqkv[h[0], 0], wqkv[h[0], 1], wgate[h[0]], wqkv[h[1], 0], wqkv[h[1], 1],
                                          wgate[h[1]], wqkv[h[0], 2], wqkv[h[1], 2]], 0).T))
    r["w1p"] = np.stack(pairs)
    r["wout"] = np.ascontiguousarray(a["L1_attn_w_out"].T.reshape(PAIRS, 2, P, D).transpose(0, 2, 1, 3))
    r["norm_w"] = np.ascontiguousarray(a["L1_attn_norm_w"].reshape(H1, P).T)
    r["router"] = rows(a["L1_ffn_gate_w"].T)
    w1 = a["L1_ffn_w1"]

    def hidden(w, s):
        w = np.concatenate([w.transpose(1, 0, 2).reshape(D, FE), s.T, np.zeros((D, FT * P - FA), w.dtype)], 1)
        return rows(w)

    r["wg"], r["wu"] = hidden(w1[:, :, :I], a["L1_ffn_sw1"]), hidden(w1[:, :, I:], a["L1_ffn_sw2"])
    w2 = np.concatenate([a["L1_ffn_w2"].reshape(FE, D), a["L1_ffn_sw3"].T, np.zeros((FT * P - FA, D), f)], 0)
    r["w2"] = rows(w2)
    own = np.zeros((3, E, FE), f)
    for e in range(E):
        own[:, e, e * I:(e + 1) * I] = 1.0
    r["spread"] = own.reshape(EROWS, FE)
    return r


def kernel(**inputs):
    import concourse.bacc as bacc
    from concourse.bass_utils import run_bass_kernel_spmd

    nc = bacc.Bacc("TRN2", target_bir_lowering=False, num_devices=1)
    arrays = laid_out(inputs)
    ins = {k: nc.dram_tensor(f"in_{k}", v.shape, mybir.dt.from_np(v.dtype), kind="ExternalInput").ap()
           for k, v in arrays.items()}
    out = nc.dram_tensor("out", (P, NT, D), F32, kind="ExternalOutput").ap()
    build(nc, ins, out)
    r = run_bass_kernel_spmd(nc, [{f"in_{k}": v for k, v in arrays.items()}], core_ids=[0])
    return r.results[0]["out"].transpose(1, 0, 2).reshape(B, S, D)
```

```python
from contextlib import ExitStack

import numpy as np
import concourse.bass as bass
from concourse import mybir

F32 = mybir.dt.float32
F32R = mybir.dt.float32r
F16 = mybir.dt.float16
BF16 = mybir.dt.bfloat16
U32 = mybir.dt.uint32
ALU = mybir.AluOpType
ACT = mybir.ActivationFunctionType
AX = mybir.AxisListType

P = 128
D = 256
KT = D // P
B, S = 4, 512
NT = B * S // P
TB = S // P
EPS_LN = 1e-5
EPS_RMS = 1e-6

H0, G0, D0 = 16, 4, 16
R0 = H0 // G0
QKV0 = (H0 + 2 * G0) * D0
SLOT = 32
SHIFT = 256.0
MASKED = -1e30

H1, D1 = 16, 128
PAIRS = H1 // 2
UNITS = 2 * B

E, I = 8, 176
FE = E * I
FA = FE + I
FT = -(-FA // P)
EROWS = E * 3


class Names:

    def __init__(self, nc, ctx, stage):
        self.nc, self.ctx, self.stage = nc, ctx, stage

    def sb(self, name, shape, dt):
        return self.ctx.enter_context(self.nc.sbuf_tensor(f"{self.stage}_{name}", shape, dt))

    def psum(self):
        return self.ctx.enter_context(self.nc.psum_tensor(f"{self.stage}_psum", [P, 8, 512], F32))

    def sem(self, name):
        return self.nc.alloc_semaphore(f"{self.stage}_{name}")

    def sems(self, name, n):
        return [self.sem(f"{name}{k}") for k in range(n)]


def modulation_stage(nc, t, d):
    with ExitStack() as ctx:
        n = Names(nc, ctx, "mod")
        cond = n.sb("cond", [P, 2, KT, B], F32)
        scond = n.sb("scond", [P, 2, KT, B], F32)
        wmod = n.sb("wmod", [P, 2, KT, 6 * D], F32)
        gneg = n.sb("gneg", [P, 2, 2, KT, B], F32)
        gsign = n.sb("gsign", [P, 2, 2, KT, B], F32)
        gpart = n.sb("gpart", [P, 2, 4, B, KT], F32R)
        diag = n.sb("diag", [P, 4, 2, B * KT, P], F32R)
        ones32 = n.sb("ones32", [P, P], F32)
        ones = n.sb("ones", [P, P], F32R)
        dist = n.sb("dist", [P, S], F32)
        nslope = n.sb("nslope", [P, H1], F32)
        decay = n.sb("decay", [P, H1, S], F32)
        ps = n.psum()
        loaded, silu_done = n.sem("loaded"), n.sem("silu_done")
        cond_loaded, wmod_loaded = n.sem("cond_loaded"), n.sems("wmod_loaded", 2)
        mod_ready, mod_copied, plus_one = n.sem("mod_ready"), n.sem("mod_copied"), n.sem("plus_one")
        gate_step, diag_ready, gates_ready = n.sem("gate_step"), n.sem("diag_ready"), n.sem("gates_ready")
        ident_step, const_ready = n.sem("ident_step"), n.sem("const_ready")
        slope_loaded, slope_neg, decay_ready = n.sem("slope_loaded"), n.sem("slope_neg"), n.sem("decay_ready")
        masked, stored, dist_step = n.sem("masked"), n.sem("stored"), n.sem("dist_step")
        gates_copied = n.sem("gates_copied")
        ones_set, ones_ready, gate_parts = n.sem("ones_set"), n.sem("ones_ready"), n.sem("gate_parts")

        with nc.Block() as block:

            @block.sync
            def _(sp):
                sp.dma_start(cond[:, :, :, :], d["cond"]).then_inc(cond_loaded, 16)
                for l in range(2):
                    sp.dma_start(wmod[:, l], d[f"wmod{l}"]).then_inc(wmod_loaded[l], 16)
                sp.dma_start(nslope[:, :], d["slope"]).then_inc(slope_loaded, 16)
                sp.dma_start(t["x"][:, :, :], d["x"]).then_inc(loaded, 16)
                for h in range(H1):
                    sp.wait_ge(masked, h + 1)
                    sp.dma_start(t["decay_dram"][h], decay[:, h, :]).then_inc(stored, 16)
                sp.wait_ge(loaded, 16)
                sp.wait_ge(stored, 16 * H1)

            @block.gpsimd
            def _(pool):
                nc.gpsimd.memset(t["ident"][:, :], 0.0).then_inc(ident_step, 1)
                nc.gpsimd.memset(t["ident16"][:, :], 0.0).then_inc(ident_step, 1)
                nc.gpsimd.memset(t["identb"][:, :], 0.0).then_inc(ident_step, 1)
                nc.gpsimd.memset(t["later_key"][:, :], 0.0).then_inc(ident_step, 1)
                nc.gpsimd.memset(t["later_key_t"][:, :], 0.0).then_inc(ident_step, 1)
                nc.gpsimd.memset(ones32[:, :], 1.0).then_inc(ones_set, 1)
                nc.gpsimd.memset(t["neg_half"][:, :], -0.5)
                nc.gpsimd.iota(dist[:, :], [[1, S]], base=0, channel_multiplier=-1,
                               allow_small_or_imprecise_dtypes=True).then_inc(dist_step, 1)
                pool.wait_ge(ident_step, 5)
                for m in ("ident", "ident16", "identb"):
                    nc.gpsimd.affine_select(out=t[m][:, :], in_=t[m][:, :], compare_op=ALU.not_equal, fill=1.0,
                                            base=0, pattern=[[-1, P]], channel_multiplier=1)
                nc.gpsimd.affine_select(out=t["later_key"][:, :], in_=t["later_key"][:, :], compare_op=ALU.is_ge,
                                        fill=MASKED, base=0, pattern=[[-1, P]], channel_multiplier=1)
                nc.gpsimd.affine_select(out=t["later_key_t"][:, :], in_=t["later_key_t"][:, :], compare_op=ALU.is_ge,
                                        fill=MASKED, base=0, pattern=[[1, P]],
                                        channel_multiplier=-1).then_inc(const_ready, 1)
                for h in range(H1):
                    pool.wait_ge(decay_ready, h + 1)
                    nc.gpsimd.affine_select(out=decay[:, h, 0:P], in_=decay[:, h, 0:P], compare_op=ALU.is_ge,
                                            fill=0.0, base=0, pattern=[[1, P]],
                                            channel_multiplier=-1).then_inc(masked, 1)

            @block.scalar
            def _(act):
                act.wait_ge(cond_loaded, 16)
                nc.scalar.activation(scond[:, :, :, :], cond[:, :, :, :], ACT.Silu).then_inc(silu_done, 1)
                act.wait_ge(ones_set, 1)
                nc.scalar.copy(ones[:, :], ones32[:, :]).then_inc(ones_ready, 1)
                act.wait_ge(dist_step, 2)
                act.wait_ge(slope_neg, 1)
                for h in range(H1):
                    nc.scalar.activation(decay[:, h, :], dist[:, :], ACT.Exp,
                                         scale=nslope[:, h:h + 1]).then_inc(decay_ready, 1)
                for g in range(4):
                    act.wait_ge(gates_ready, g + 1)
                    nc.scalar.copy(t["gate"][:, g].rearrange("p (c b) n -> p c (b n)", c=2),
                                   ps[:, 2 * (g % 4):2 * (g % 4) + 2, :]).then_inc(gates_copied, 1)

            @block.vector
            def _(dve):
                dve.wait_ge(dist_step, 1)
                nc.vector.tensor_scalar(dist[:, :], dist[:, :], 0.0, None, ALU.max).then_inc(dist_step, 1)
                dve.wait_ge(slope_loaded, 16)
                nc.vector.tensor_scalar(nslope[:, :], nslope[:, :], -1.0, None, ALU.mult).then_inc(slope_neg, 1)
                dve.wait_ge(mod_ready, 1)
                nc.vector.tensor_copy(t["mod"][:, :, :, :, :], ps[:, 0, 0:96].rearrange(
                    "p (l c k b) -> p l c (k b)", l=2, c=6, k=KT).rearrange("p l c (k b) -> p l c k b", k=KT)
                    ).then_inc(mod_copied, 1)
                dve.wait_ge(mod_copied, 1)
                for l in range(2):
                    for c in (1, 4):
                        nc.vector.tensor_scalar(t["mod"][:, l, c], t["mod"][:, l, c], 1.0, None,
                                                ALU.add).then_inc(plus_one, 1)
                for l in range(2):
                    for j, c in enumerate((2, 5)):
                        g = t["mod"][:, l, c].rearrange("p k b -> p (k b)")
                        a = gneg[:, l, j].rearrange("p k b -> p (k b)")
                        s = gsign[:, l, j].rearrange("p k b -> p (k b)")
                        nc.vector.scalar_tensor_tensor(a, g, -1.0, g, ALU.mult, ALU.max).then_inc(gate_step, 1)
                        nc.vector.tensor_scalar(s, g, 0.0, 2.0, ALU.is_ge, ALU.mult).then_inc(gate_step, 1)
                dve.wait_ge(gate_step, 8)
                gn = gneg[:, :, :, :, :].rearrange("p l j k b -> p (l j k b)")
                gs = gsign[:, :, :, :, :].rearrange("p l j k b -> p (l j k b)")
                nc.vector.tensor_scalar(gn, gn, 0.25, None, ALU.max).then_inc(gate_step, 1)
                dve.wait_ge(gate_step, 9)
                nc.vector.scalar_tensor_tensor(gn, gs, -1.0, gn, ALU.add, ALU.mult).then_inc(gate_step, 1)
                dve.wait_ge(gate_step, 10)
                dve.wait_ge(const_ready, 1)
                gnb = gneg[:, :, :, :, :].rearrange("p l j k b -> p (l j) b k")
                nc.vector.tensor_copy(gpart[:, 0], gnb).then_inc(gate_parts, 1)
                dve.wait_ge(gate_parts, 1)
                nc.vector.tensor_tensor(gpart[:, 1], gnb, gpart[:, 0].bitcast(F32), ALU.subtract).then_inc(gate_parts, 1)
                dve.wait_ge(gate_parts, 2)
                for g in range(4):
                    for part in range(2):
                        last = nc.vector.tensor_tensor(
                            diag[:, g, part], t["ident"][:, :].unsqueeze(1).to_broadcast([P, B * KT, P]),
                            gpart[:, part, g].bitcast(F32).rearrange("p b k -> p (b k)").unsqueeze(2)
                            .to_broadcast([P, B * KT, P]), ALU.mult)
                    last.then_inc(diag_ready, 1)

            @block.tensor
            def _(pe):
                pe.wait_ge(silu_done, 1)
                for l in range(2):
                    pe.wait_ge(wmod_loaded[l], 16)
                    for c in range(6):
                        for f in range(KT):
                            at = ((l * 6 + c) * KT + f) * B
                            for k in range(KT):
                                last = nc.tensor.matmul(ps[:, 0, at:at + B], wmod[:, l, k, c * D + f * P:c * D + (f + 1) * P],
                                                        scond[:, l, k, :], start=(k == 0), stop=(k == KT - 1))
                last.then_inc(mod_ready, 1)
                pe.wait_ge(ones_ready, 1)
                for g in range(4):
                    pe.wait_ge(diag_ready, g + 1)
                    for half in range(2):
                        for part in range(2):
                            last = nc.tensor.matmul(ps[:, 2 * g + half, :], ones[:, :],
                                                    diag[:, g, part, half * B:(half + 1) * B, :].rearrange("p c n -> p (c n)"),
                                                    start=(part == 0), stop=(part == 1))
                    last.then_inc(gates_ready, 1)


def attention0_tasks():
    before = [("xn",), ("qkv", 0), ("qkv", 1), ("kt",), ("qt",)]
    scores = [[("s", g, tt, pr) for tt in range(TB) for pr in range(2)] for g in range(G0)] + [[]]
    order, late = list(before) + scores[0], []
    for g in range(G0):
        nxt = list(scores[g + 1])
        order += nxt[:2]
        nxt = nxt[2:]
        own = ([("q2", g)] + [("st", g, 0, j) for j in range(2)] + late + [("st", g, 0, 2), ("st", g, 0, 3)]
               + [("st", g, 1, 0), ("st", g, 1, 1), ("pv", g, 0), ("st", g, 1, 2), ("st", g, 1, 3)])
        late = [("pv", g, 1)]
        for n, task in enumerate(own):
            order.append(task)
            if n >= 1 and nxt:
                order.append(nxt.pop(0))
        order += nxt
    return order + late + [("aot",), ("out", 0), ("out", 1)]


def attention0_stage(nc, t, d):
    tasks = attention0_tasks()
    place = {task: n for n, task in enumerate(tasks)}
    assert len(tasks) % 4 == 0 and len(place) == len(tasks)
    turns = len(tasks) // 4
    x = t["x"]
    with ExitStack() as ctx:
        n = Names(nc, ctx, "attn0")
        wqkv32 = n.sb("wqkv32", [P, KT, QKV0], F32)
        wo32 = n.sb("wo32", [P, KT, D], F32)
        bias32 = n.sb("bias32", [1, QKV0 + D], F32)
        wqkv = n.sb("wqkv", [P, KT, QKV0], F16)
        wo = n.sb("wo", [P, KT, D], F16)
        bias = n.sb("bias", [1, QKV0 + D], F16)
        ones = n.sb("ones", [1, P], F16)
        norm_scale = n.sb("norm_scale", [P, 2, D0], F32)
        cosd = n.sb("cosd", [P, TB, D0], F32)
        sind = n.sb("sind", [P, TB, D0], F32)
        cos_t = n.sb("cos_t", [P, TB, 2, D0], F32)
        sin_t = n.sb("sin_t", [P, TB, 2, D0], F32)
        st = n.sb("st", [P, TB, 6], F32)
        mv = n.sb("mv", [P, TB, 2], F32)
        rstd = n.sb("rstd", [P, TB], F32)
        xn = n.sb("xn", [P, TB, D], F32)
        ht = n.sb("ht", [P, KT, S], F16)
        qkv = n.sb("qkv", [P, TB, QKV0], F16)
        NH = H0 + G0
        sq = n.sb("sq", [P, TB, NH, D0], F32)
        ss = n.sb("ss", [P, TB, NH], F32)
        qn = n.sb("qn", [P, TB, NH, D0], F32)
        rc_ = n.sb("rope_cos", [P, TB, NH, D0], F32)
        rs_ = n.sb("rope_sin", [P, TB, NH, D0], F32)
        kr = n.sb("kr", [P, TB, G0, D0], F16)
        qa = n.sb("qa", [P, TB, H0, SLOT], F16)
        ka = n.sb("ka", [P, TB * G0, R0, SLOT], F16)
        va = n.sb("va", [P, TB, G0, D0 + 1], F16)
        qt = n.sb("qt", [P, G0, S], F16)
        qt2 = n.sb("qt2", [P, G0, S], F16)
        kt = n.sb("kt", [P, G0, S], F16)
        top = n.sb("top", [P, TB, H0], F32)
        probs = n.sb("probs", [P, 2, TB, 2, S], F16)
        rden = n.sb("rden", [P, 2, TB, 2], F32)
        ao = n.sb("ao", [P, TB, H0, D0], F16)
        aot = n.sb("aot", [P, KT, S], F16)
        upd = n.sb("upd", [P, TB, D], F32)
        ps = n.psum()
        eps_rms = n.sb("eps_rms", [P, 1], F32)

        weights_loaded = n.sem("weights_loaded")
        tables_loaded = n.sem("tables_loaded")
        weights_cast, tables_ready, padding_set = n.sem("weights_cast"), n.sem("tables_ready"), n.sem("padding_set")
        slot_full = n.sems("slot_full", 4)
        stats_done, aggr_done, var_eps, rstd_done = (n.sem(s) for s in ("stats_done", "aggr_done", "var_eps", "rstd_done"))
        xn_done, ht_done, qkv_done = n.sem("xn_done"), n.sem("ht_done"), n.sem("qkv_done")
        sq_done, ss_done, std_done, rrms_done = (n.sem(s) for s in ("sq_done", "ss_done", "std_done", "rrms_done"))
        qn_done, rot_done, q_roped, k_roped, k_spread, v_copied = (
            n.sem(s) for s in ("qn_done", "rot_done", "q_roped", "k_roped", "k_spread", "v_copied"))
        krot_done = n.sem("krot_done")
        kt_done, qt_done, top_done, shift_set, qt2_done = (
            n.sem(s) for s in ("kt_done", "qt_done", "top_done", "shift_set", "qt2_done"))
        exp_done, rden_done, ao_done, aot_done = (
            n.sem(s) for s in ("exp_done", "rden_done", "ao_done", "aot_done"))
        upd_done, x_done = n.sem("upd_done"), n.sem("x_done")
        eps_set, dve_held, pool_held = n.sem("eps_set"), n.sem("dve_held"), n.sem("pool_held")

        def banks(task):
            s = place[task] % 4
            return ps[:, 2 * s:2 * s + 2, :]

        def banks16(task):
            return banks(task).rearrange("p a n -> p (a n)").bitcast(F16)

        def filled(eng, task, it):
            m = place[task]
            eng.wait_ge(slot_full[m % 4], it * turns + (m // 4 + 1))

        def emptied(eng, task, it):
            kind = task[0]
            if kind == "xn":
                eng.wait_ge(ht_done, it * KT + KT)
            elif kind == "qkv":
                eng.wait_ge(qkv_done, it * 2 + (task[1] + 1))
            elif kind in ("kt", "qt", "aot"):
                eng.wait_ge({"kt": kt_done, "qt": qt_done, "aot": aot_done}[kind], it + 1)
            elif kind == "s":
                _, g, tt, pr = task
                eng.wait_ge(top_done, it * 32 + (g * 8 + tt * 2 + pr + 1))
            elif kind == "q2":
                eng.wait_ge(qt2_done, it * G0 + (task[1] + 1))
            elif kind == "st":
                _, g, pr, j = task
                eng.wait_ge(exp_done, it * (8 * TB) + ((2 * g + pr) * TB + j + 1))
            elif kind == "pv":
                _, g, pr = task
                eng.wait_ge(ao_done, it * 8 + (2 * g + pr + 1))
            else:
                eng.wait_ge(upd_done, it * 2 + (task[1] + 1))

        with nc.Block() as block:

            @block.sync
            def _(sp):
                sp.dma_start(wqkv32[:, :, :], d["wqkv0"]).then_inc(weights_loaded, 16)
                sp.dma_start(wo32[:, :, :], d["wo0"]).then_inc(weights_loaded, 16)
                sp.dma_start(bias32[:, :], d["bias0"]).then_inc(weights_loaded, 16)
                sp.dma_start(norm_scale[:, :, :], d["norm_scale0"]).then_inc(tables_loaded, 16)
                sp.dma_start(cosd[:, :, :], d["cosd"]).then_inc(tables_loaded, 16)
                sp.dma_start(sind[:, :, :], d["sind"]).then_inc(tables_loaded, 16)

            @block.tensor
            def _(pe):
                pe.wait_ge(weights_cast, 3)
                pe.wait_ge(padding_set, 5)

                def batch(it, first):
                    for m, task in enumerate(tasks):
                        kind, out = task[0], banks(task)
                        if m >= 4:
                            emptied(pe, tasks[m - 4], it)
                        elif not first:
                            emptied(pe, tasks[m - 4], it - 1)
                        if kind == "xn":
                            pe.wait_ge(xn_done, it + 1)
                            for k in range(KT):
                                for tt in range(TB):
                                    last = nc.tensor.transpose(out[:, k, tt * P:(tt + 1) * P],
                                                               xn[:, tt, k * P:(k + 1) * P], t["ident"][:, :])
                        elif kind == "qkv":
                            pe.wait_ge(ht_done, it * KT + KT)
                            for h in range(2):
                                tt = 2 * task[1] + h
                                for k in range(KT):
                                    nc.tensor.matmul(out[:, h, 0:QKV0], ht[:, k, tt * P:(tt + 1) * P], wqkv[:, k, :],
                                                     start=(k == 0), stop=False)
                                last = nc.tensor.matmul(out[:, h, 0:QKV0], ones[0:1, :], bias[0:1, 0:QKV0],
                                                        start=False, stop=True)
                        elif kind in ("kt", "qt"):
                            if kind == "kt":
                                pe.wait_ge(k_spread, it + 1)
                            else:
                                pe.wait_ge(q_roped, it * 2 + 2)
                            o = banks16(task)
                            for g in range(G0):
                                for tt in range(TB):
                                    src = (ka[:, tt * G0 + g].rearrange("p r c -> p (r c)") if kind == "kt" else
                                           qa[:, tt, R0 * g:R0 * (g + 1)].rearrange("p r c -> p (r c)"))
                                    last = nc.tensor.transpose(o[:, g * S + tt * P:g * S + (tt + 1) * P], src,
                                                               t["ident16"][:, :])
                        elif kind == "s":
                            _, g, tt, pr = task
                            if (g, tt, pr) == (0, 0, 0):
                                pe.wait_ge(kt_done, it + 1)
                                pe.wait_ge(qt_done, it + 1)
                            for h in range(2):
                                r = SLOT * (2 * pr + h)
                                nc.tensor.matmul(out[:, h, 0:(tt + 1) * P], qt[r:r + D0, g, tt * P:(tt + 1) * P],
                                                 kt[r:r + D0, g, 0:(tt + 1) * P], start=True, stop=False)
                            for h in range(2):
                                last = nc.tensor.matmul(out[:, h, tt * P:(tt + 1) * P], t["identb"][:, :],
                                                        t["later_key"][:, :], start=False, stop=True)
                        elif kind == "q2":
                            g = task[1]
                            pe.wait_ge(shift_set, it * G0 + (g + 1))
                            o = banks16(task)
                            for tt in range(TB):
                                last = nc.tensor.transpose(o[:, tt * P:(tt + 1) * P],
                                                           qa[:, tt, R0 * g:R0 * (g + 1)].rearrange("p r c -> p (r c)"),
                                                           t["ident16"][:, :])
                        elif kind == "st":
                            _, g, pr, j = task
                            if (pr, j) == (0, 0):
                                pe.wait_ge(qt2_done, it * G0 + (g + 1))
                            for h in range(2):
                                r = SLOT * (2 * pr + h)
                                nc.tensor.matmul(out[:, h, 0:S - j * P], kt[r:r + D0 + 1, g, j * P:(j + 1) * P],
                                                 qt2[r:r + D0 + 1, g, j * P:S], start=True, stop=False)
                            for h in range(2):
                                last = nc.tensor.matmul(out[:, h, 0:P], t["identb"][:, :], t["later_key_t"][:, :],
                                                        start=False, stop=True)
                        elif kind == "pv":
                            _, g, pr = task
                            pe.wait_ge(exp_done, it * (8 * TB) + (2 * g + pr + 1) * TB)
                            if (g, pr) == (0, 0):
                                pe.wait_ge(v_copied, it + 1)
                            for tt in range(TB):
                                for h in range(2):
                                    o = out[:, 0, (tt * 2 + h) * (D0 + 1):(tt * 2 + h + 1) * (D0 + 1)]
                                    for j in range(tt + 1):
                                        last = nc.tensor.matmul(o, probs[:, pr, j, h, (tt - j) * P:(tt - j + 1) * P],
                                                                va[:, j, g, :], start=(j == 0), stop=(j == tt))
                        elif kind == "aot":
                            pe.wait_ge(ao_done, it * 8 + 8)
                            o = banks16(task)
                            for k in range(KT):
                                for tt in range(TB):
                                    last = nc.tensor.transpose(
                                        o[:, k * S + tt * P:k * S + (tt + 1) * P],
                                        ao[:, tt, k * 8:(k + 1) * 8].rearrange("p h c -> p (h c)"), t["ident16"][:, :])
                        else:
                            pe.wait_ge(aot_done, it + 1)
                            for h in range(2):
                                tt = 2 * task[1] + h
                                for k in range(KT):
                                    nc.tensor.matmul(out[:, h, 0:D], aot[:, k, tt * P:(tt + 1) * P], wo[:, k, :],
                                                     start=(k == 0), stop=False)
                                last = nc.tensor.matmul(out[:, h, 0:D], ones[0:1, :], bias[0:1, QKV0:QKV0 + D],
                                                        start=False, stop=True)
                        last.then_inc(slot_full[m % 4], 1)

                batch(0, True)
                with pe.Fori(1, B) as it:
                    batch(it, False)

            @block.scalar
            def _(act):
                act.wait_ge(weights_loaded, 48)
                nc.scalar.copy(wqkv[:, :, :], wqkv32[:, :, :]).then_inc(weights_cast, 1)
                nc.scalar.copy(wo[:, :, :], wo32[:, :, :]).then_inc(weights_cast, 1)
                nc.scalar.copy(bias[:, :], bias32[:, :]).then_inc(weights_cast, 1)
                act.wait_ge(eps_set, 1)
                with act.Fori(0, B) as it:
                    filled(act, ("xn",), it)
                    for k in range(KT):
                        last = nc.scalar.activation(ht[:, k, :], banks(("xn",))[:, k, :], ACT.Identity,
                                                    scale=t["mod"][:, 0, 1, k, bass.ds(it, 1)],
                                                    bias=t["mod"][:, 0, 0, k, bass.ds(it, 1)])
                        last.then_inc(ht_done, 1)
                    for i in range(2):
                        filled(act, ("qkv", i), it)
                        nc.scalar.copy(qkv[:, 2 * i:2 * i + 2, :], banks(("qkv", i))[:, :, 0:QKV0]).then_inc(qkv_done, 1)
                    act.wait_ge(ss_done, it + 1)
                    nc.scalar.activation(ss[:, :, :], ss[:, :, :], ACT.Sqrt, bias=eps_rms[:, 0:1], scale=1.0 / D0).then_inc(std_done, 1)
                    for task in tasks:
                        if task[0] == "st":
                            _, g, pr, j = task
                            filled(act, task, it)
                            if j == 0 and g:
                                filled(act, ("pv", g - 1, pr), it)
                            nc.scalar.activation(probs[:, pr, j, :, 0:S - j * P], banks(task)[:, :, 0:S - j * P],
                                                 ACT.Exp, scale=D0 ** -0.5).then_inc(exp_done, 1)

            @block.vector
            def _(dve):
                nc.vector.memset(eps_rms[:, :], EPS_RMS).then_inc(eps_set, 1)
                dve.wait_ge(padding_set, 5)
                with dve.Fori(0, B) as it:
                    for tt in range(TB):
                        nc.vector.bn_stats(st[:, tt, :], x[:, bass.ds(it * TB + tt, 1), :]).then_inc(stats_done, 1)
                    dve.wait_ge(stats_done, it * TB + TB)
                    dve.sem_inc(dve_held, 1)
                    for tt in range(TB):
                        last = nc.vector.bn_aggr(mv[:, tt, :], st[:, tt, :])
                    last.then_inc(aggr_done, 1)
                    dve.wait_ge(rstd_done, it + 1)
                    for tt in range(TB):
                        last = nc.vector.tensor_scalar(xn[:, tt, :], x[:, bass.ds(it * TB + tt, 1), :], mv[:, tt, 0:1],
                                                       rstd[:, tt:tt + 1], ALU.subtract, ALU.mult)
                    last.then_inc(xn_done, 1)
                    qk = qkv[:, :, 0:NH * D0]
                    dve.wait_ge(qkv_done, it * 2 + 2)
                    sqf = sq[:, :, :, :].rearrange("p t h c -> p t (h c)")
                    nc.vector.tensor_tensor(sqf, qk, qk, ALU.mult).then_inc(sq_done, 1)
                    dve.wait_ge(sq_done, it + 1)
                    nc.vector.tensor_reduce(ss[:, :, :], sq[:, :, :, :], AX.X, ALU.add).then_inc(ss_done, 1)
                    dve.wait_ge(std_done, it + 1)
                    nc.vector.reciprocal(ss[:, :, :], ss[:, :, :]).then_inc(rrms_done, 1)
                    dve.wait_ge(rrms_done, it + 1)
                    nc.vector.tensor_tensor(qn[:, :, :, :].rearrange("p t h c -> p (t h) c"),
                                            qkv[:, :, 0:NH * D0].rearrange("p t (h c) -> p t h c", c=D0),
                                            ss[:, :, :].unsqueeze(3).to_broadcast([P, TB, NH, D0]),
                                            ALU.mult).then_inc(qn_done, 1)
                    dve.wait_ge(qn_done, it + 1)
                    q4 = [P, TB, H0, D0]
                    nc.vector.tensor_tensor(rc_[:, :, 0:H0, :], qn[:, :, 0:H0, :],
                                            cos_t[:, :, 0, :].unsqueeze(2).to_broadcast(q4), ALU.mult)
                    nc.vector.tensor_tensor(rs_[:, :, 0:H0, :], qn[:, :, 0:H0, :],
                                            sin_t[:, :, 0, :].unsqueeze(2).to_broadcast(q4), ALU.mult).then_inc(rot_done, 1)
                    dve.wait_ge(rot_done, it + 1)
                    hd = D0 // 2
                    nc.vector.tensor_tensor(qa[:, :, :, 0:hd], rc_[:, :, 0:H0, 0:hd], rs_[:, :, 0:H0, hd:D0],
                                            ALU.subtract).then_inc(q_roped, 1)
                    nc.vector.tensor_tensor(qa[:, :, :, hd:D0], rc_[:, :, 0:H0, hd:D0], rs_[:, :, 0:H0, 0:hd],
                                            ALU.add).then_inc(q_roped, 1)
                    for task in tasks:
                        kind = task[0]
                        if kind not in ("kt", "qt", "s", "q2", "pv", "aot", "out"):
                            continue
                        filled(dve, task, it)
                        if kind in ("kt", "qt"):
                            dst, done = (kt, kt_done) if kind == "kt" else (qt, qt_done)
                            nc.vector.tensor_copy(dst[:, :, :].rearrange("p g n -> p (g n)"), banks16(task)).then_inc(done, 1)
                        elif kind == "s":
                            _, g, tt, pr = task
                            h = R0 * g + 2 * pr
                            nc.vector.tensor_reduce(top[:, tt, h:h + 2], banks(task)[:, :, 0:(tt + 1) * P], AX.X,
                                                    ALU.max).then_inc(top_done, 1)
                            if (tt, pr) == (TB - 1, 1):
                                dve.wait_ge(top_done, it * 32 + (g * 8 + tt * 2 + pr + 1))
                                nc.vector.tensor_scalar(qa[:, :, R0 * g:R0 * (g + 1), D0], top[:, :, R0 * g:R0 * (g + 1)],
                                                        -1.0 / SHIFT, None, ALU.mult).then_inc(shift_set, 1)
                        elif kind == "q2":
                            g = task[1]
                            nc.vector.tensor_copy(qt2[:, g, :], banks16(task)[:, 0:S]).then_inc(qt2_done, 1)
                        elif kind == "pv":
                            _, g, pr = task
                            o = banks(task)[:, 0, 0:8 * (D0 + 1)].rearrange("p (t h c) -> p t h c", h=2, c=D0 + 1)
                            nc.vector.reciprocal(rden[:, pr, :, :], o[:, :, :, D0]).then_inc(rden_done, 1)
                            dve.wait_ge(rden_done, it * 8 + (2 * g + pr + 1))
                            h = R0 * g + 2 * pr
                            nc.vector.tensor_tensor(ao[:, :, h:h + 2, :], o[:, :, :, 0:D0],
                                                    rden[:, pr, :, :].unsqueeze(3).to_broadcast([P, TB, 2, D0]),
                                                    ALU.mult).then_inc(ao_done, 1)
                        elif kind == "aot":
                            nc.vector.tensor_copy(aot[:, :, :].rearrange("p k n -> p (k n)"),
                                                  banks16(task)[:, 0:KT * S]).then_inc(aot_done, 1)
                        else:
                            i = task[1]
                            nc.vector.tensor_tensor(upd[:, 2 * i:2 * i + 2, :], banks(task)[:, :, 0:D],
                                                    t["gate"][:, 0, bass.ds(it, 1), :].to_broadcast([P, 2, D]),
                                                    ALU.mult).then_inc(upd_done, 1)

            @block.gpsimd
            def _(pool):
                nc.gpsimd.memset(qa[:, :, :, :], 0.0).then_inc(padding_set, 1)
                nc.gpsimd.memset(ka[:, :, :, :], 0.0).then_inc(padding_set, 1)
                nc.gpsimd.memset(va[:, :, :, :], 1.0).then_inc(padding_set, 1)
                nc.gpsimd.memset(ones[:, :], 1.0).then_inc(padding_set, 1)
                pool.wait_ge(padding_set, 4)
                nc.gpsimd.memset(ka[:, :, :, D0:D0 + 1], SHIFT).then_inc(padding_set, 1)
                pool.wait_ge(tables_loaded, 48)
                nc.gpsimd.tensor_scalar(norm_scale[:, 0, :], norm_scale[:, 0, :], D0 ** -0.5, None,
                                        ALU.mult).then_inc(tables_ready, 1)
                pool.wait_ge(tables_ready, 1)
                for which in range(2):
                    sc = norm_scale[:, which, :].unsqueeze(1).to_broadcast([P, TB, D0])
                    nc.gpsimd.tensor_tensor(cos_t[:, :, which, :], cosd[:, :, :], sc, ALU.mult)
                    last = nc.gpsimd.tensor_tensor(sin_t[:, :, which, :], sind[:, :, :], sc, ALU.mult)
                last.then_inc(tables_ready, 1)
                pool.wait_ge(tables_ready, 2)
                with pool.Fori(0, B) as it:
                    pool.wait_ge(aggr_done, it + 1)
                    pool.sem_inc(pool_held, 1)
                    nc.gpsimd.tensor_scalar(rstd[:, :], mv[:, :, 1], EPS_LN, None, ALU.add).then_inc(var_eps, 1)
                    pool.wait_ge(var_eps, it + 1)
                    nc.gpsimd.tensor_tensor(rstd[:, :], rstd[:, :], t["neg_half"][:, 0:TB], ALU.pow).then_inc(rstd_done, 1)
                    pool.wait_ge(qkv_done, it * 2 + 2)
                    pool.sem_inc(pool_held, 1)
                    nc.gpsimd.tensor_copy(va[:, :, :, 0:D0], qkv[:, :, NH * D0:QKV0].rearrange(
                        "p t (g c) -> p t g c", c=D0)).then_inc(v_copied, 1)
                    pool.wait_ge(qn_done, it + 1)
                    k4 = [P, TB, G0, D0]
                    nc.gpsimd.tensor_tensor(rc_[:, :, H0:NH, :], qn[:, :, H0:NH, :],
                                            cos_t[:, :, 1, :].unsqueeze(2).to_broadcast(k4), ALU.mult).then_inc(krot_done, 1)
                    nc.gpsimd.tensor_tensor(rs_[:, :, H0:NH, :], qn[:, :, H0:NH, :],
                                            sin_t[:, :, 1, :].unsqueeze(2).to_broadcast(k4), ALU.mult).then_inc(krot_done, 1)
                    pool.wait_ge(krot_done, it * 2 + 2)
                    hd = D0 // 2
                    nc.gpsimd.tensor_tensor(kr[:, :, :, 0:hd], rc_[:, :, H0:NH, 0:hd], rs_[:, :, H0:NH, hd:D0],
                                            ALU.subtract).then_inc(k_roped, 1)
                    nc.gpsimd.tensor_tensor(kr[:, :, :, hd:D0], rc_[:, :, H0:NH, hd:D0], rs_[:, :, H0:NH, 0:hd],
                                            ALU.add).then_inc(k_roped, 1)
                    pool.wait_ge(k_roped, it * 2 + 2)
                    pool.sem_inc(pool_held, 1)
                    nc.gpsimd.tensor_copy(ka[:, :, :, 0:D0], kr[:, :, :, :].rearrange("p t g c -> p (t g) c").unsqueeze(2)
                                          .to_broadcast([P, TB * G0, R0, D0])).then_inc(k_spread, 1)
                    for i in range(2):
                        pool.wait_ge(upd_done, it * 2 + (i + 1))
                        xs = x[:, bass.ds(it * TB + 2 * i, 2), :]
                        nc.gpsimd.tensor_tensor(xs, xs, upd[:, 2 * i:2 * i + 2, :], ALU.add).then_inc(x_done, 1)


def at(i, size=1):
    return slice(i, i + size) if isinstance(i, int) else bass.ds(i, size)


class SplitNorm:

    def __init__(self, n, tag, layer, shift_part, parts, xn, psum_slot):
        self.layer, self.shift_part, self.parts, self.xn, self.slot = layer, shift_part, parts, xn, psum_slot
        self.st = n.sb(f"{tag}_st", [P, NT, 6], F32)
        self.mv = n.sb(f"{tag}_mv", [P, NT, 2], F32)
        self.rstd = n.sb(f"{tag}_rstd", [P, NT], F32)
        self.ht = n.sb(f"{tag}_ht", [P, KT, S], F32)
        self.stats_done, self.aggr_done = n.sem(f"{tag}_stats_done"), n.sem(f"{tag}_aggr_done")
        self.var_eps, self.rstd_done = n.sem(f"{tag}_var_eps"), n.sem(f"{tag}_rstd_done")
        self.xn_done, self.turned = n.sem(f"{tag}_xn_done"), n.sem(f"{tag}_turned")
        self.ht_done, self.high_done = n.sem(f"{tag}_ht_done"), n.sem(f"{tag}_high_done")
        self.low_done = n.sem(f"{tag}_low_done")

    def vector_stats(self, nc, x, it):
        for tt in range(TB):
            nc.vector.bn_stats(self.st[:, at(it * TB + tt), :], x[:, at(it * TB + tt), :]).then_inc(self.stats_done, 1)

    def vector_aggregate(self, nc, dve):
        dve.wait_ge(self.stats_done, NT)
        for tile in range(NT):
            last = nc.vector.bn_aggr(self.mv[:, tile, :], self.st[:, tile, :])
        last.then_inc(self.aggr_done, 1)

    def pool_rstd(self, nc, pool, t):
        pool.wait_ge(self.aggr_done, 1)
        nc.gpsimd.tensor_scalar(self.rstd[:, :], self.mv[:, :, 1], EPS_LN, None, ALU.add).then_inc(self.var_eps, 1)
        pool.wait_ge(self.var_eps, 1)
        nc.gpsimd.tensor_tensor(self.rstd[:, :], self.rstd[:, :], t["neg_half"][:, :], ALU.pow).then_inc(self.rstd_done, 1)

    def vector_norm(self, nc, dve, x):
        dve.wait_ge(self.rstd_done, 1)
        for tile in range(NT):
            last = nc.vector.tensor_scalar(self.xn[:, tile, :], x[:, tile, :], self.mv[:, tile, 0:1],
                                           self.rstd[:, tile:tile + 1], ALU.subtract, ALU.mult)
            if tile % TB == TB - 1:
                last.then_inc(self.xn_done, 1)

    def tensor_turn(self, nc, pe, t, ps, b):
        pe.wait_ge(self.xn_done, b + 1)
        if b:
            pe.wait_ge(self.ht_done, b * KT)
        for k in range(KT):
            for tt in range(TB):
                last = nc.tensor.transpose(ps[:, self.slot + k, tt * P:(tt + 1) * P],
                                           self.xn[:, b * TB + tt, k * P:(k + 1) * P], t["ident"][:, :])
        last.then_inc(self.turned, 1)

    def scalar_high(self, nc, act, t, ps, b):
        act.wait_ge(self.turned, b + 1)
        if b:
            act.wait_ge(self.low_done, b)
        for k in range(KT):
            nc.scalar.activation(self.ht[:, k, :], ps[:, self.slot + k, :], ACT.Identity,
                                 scale=t["mod"][:, self.layer, self.shift_part + 1, k, b:b + 1],
                                 bias=t["mod"][:, self.layer, self.shift_part, k, b:b + 1]).then_inc(self.ht_done, 1)
        act.wait_ge(self.ht_done, b * KT + KT)
        nc.scalar.copy(self.parts[:, 0, :, b * S:(b + 1) * S], self.ht[:, :, :]).then_inc(self.high_done, 1)

    def vector_low(self, nc, dve, b):
        dve.wait_ge(self.high_done, b + 1)
        cols = slice(b * S, (b + 1) * S)
        nc.vector.tensor_tensor(self.parts[:, 1, :, cols], self.ht[:, :, :], self.parts[:, 0, :, cols].bitcast(F32),
                                ALU.subtract).then_inc(self.low_done, 1)


def ffn0_stage(nc, t, d):
    x = t["x"]
    with ExitStack() as ctx:
        n = Names(nc, ctx, "ffn0")
        hp = t["h_parts"]
        wraw = n.sb("wraw", [P, KT, D], F32)
        rows = n.sb("rows", [P, 2, D], F32)
        w = n.sb("w", [P, KT, D], F32)
        wp = n.sb("wp", [P, 2, KT, D], F32R)
        gbias = n.sb("gbias", [P, B, D], F32)
        upd = n.sb("upd", [P, NT, D], F32)
        ps = n.psum()
        norm_a = SplitNorm(n, "a", 0, 3, hp, t["yacc"], 0)
        norm_b = SplitNorm(n, "b", 1, 0, hp, n.sb("xn", [P, NT, D], F32), 2)
        loaded, w_scaled, w_high, w_ready = n.sem("loaded"), n.sem("w_scaled"), n.sem("w_high"), n.sem("w_ready")
        gbias_ready = n.sem("gbias_ready")
        made, upd_done, x_done, bias_added = n.sem("made"), n.sem("upd_done"), n.sem("x_done"), n.sem("bias_added")
        dve_held = n.sem("dve_held")
        OUT = 4

        with nc.Block() as block:

            @block.sync
            def _(sp):
                sp.dma_start(wraw[:, :, :], d["wffn"]).then_inc(loaded, 16)
                sp.dma_start(rows[:, :, :], d["ffn_rows"]).then_inc(loaded, 16)

            @block.tensor
            def _(pe):
                norm_a.tensor_turn(nc, pe, t, ps, 0)
                pe.wait_ge(w_ready, 1)
                for b in range(B):
                    if b + 1 < B:
                        norm_a.tensor_turn(nc, pe, t, ps, b + 1)
                    pe.wait_ge(norm_a.low_done, b + 1)
                    for tt in range(TB):
                        if tt % 2 == 0 and b:
                            pe.wait_ge(upd_done, 2 * b - 1 + tt // 2)
                        for m, (k, (a, c)) in enumerate([(k, tc) for k in range(KT) for tc in TERMS]):
                            last = nc.tensor.matmul(ps[:, OUT + tt // 2, (tt % 2) * D:(tt % 2 + 1) * D],
                                                    hp[:, a, k, b * S + tt * P:b * S + (tt + 1) * P], wp[:, c, k, :],
                                                    start=(m == 0), stop=(m == 5))
                        if tt % 2:
                            last.then_inc(made, 1)
                for b in range(B):
                    norm_b.tensor_turn(nc, pe, t, ps, b)

            @block.scalar
            def _(act):
                act.wait_ge(w_scaled, 1)
                nc.scalar.copy(wp[:, 0], w[:, :, :]).then_inc(w_high, 1)
                for b in range(B):
                    norm_a.scalar_high(nc, act, t, ps, b)
                act.wait_ge(made, 2 * B)
                for b in range(B):
                    norm_b.scalar_high(nc, act, t, ps, b)

            @block.vector
            def _(dve):
                with dve.Fori(0, B) as it:
                    norm_a.vector_stats(nc, x, it)
                norm_a.vector_aggregate(nc, dve)
                dve.wait_ge(loaded, 32)
                nc.vector.tensor_tensor(w[:, :, :], wraw[:, :, :], rows[:, 0:1, :].to_broadcast([P, KT, D]),
                                        ALU.mult).then_inc(w_scaled, 1)
                dve.wait_ge(w_high, 1)
                nc.vector.tensor_tensor(wp[:, 1], w[:, :, :], wp[:, 0].bitcast(F32), ALU.subtract).then_inc(w_ready, 1)
                norm_a.vector_norm(nc, dve, x)

                def update(b):
                    for i in range(2):
                        dve.wait_ge(made, b * 2 + (i + 1))
                        nc.vector.tensor_tensor(upd[:, b * TB + 2 * i:b * TB + 2 * i + 2, :],
                                                ps[:, OUT + i, :].rearrange("p (t n) -> p t n", t=2),
                                                t["gate"][:, 1, b:b + 1, :].to_broadcast([P, 2, D]),
                                                ALU.mult).then_inc(upd_done, 1)

                for b in range(B):
                    norm_a.vector_low(nc, dve, b)
                    if b:
                        update(b - 1)
                update(B - 1)
                with dve.Fori(0, B) as it:
                    dve.wait_ge(x_done, it + 1)
                    dve.sem_inc(dve_held, 1)
                    norm_b.vector_stats(nc, x, it)
                norm_b.vector_aggregate(nc, dve)
                norm_b.vector_norm(nc, dve, x)
                for b in range(B):
                    norm_b.vector_low(nc, dve, b)

            @block.gpsimd
            def _(pool):
                norm_a.pool_rstd(nc, pool, t)
                pool.wait_ge(loaded, 32)
                nc.gpsimd.tensor_tensor(gbias[:, :, :], t["gate"][:, 1], rows[:, 1:2, :].to_broadcast([P, B, D]),
                                        ALU.mult).then_inc(gbias_ready, 1)
                pool.wait_ge(gbias_ready, 1)
                for b in range(B):
                    pool.wait_ge(norm_a.xn_done, b + 1)
                    xb = x[:, b * TB:(b + 1) * TB, :]
                    nc.gpsimd.tensor_tensor(xb, xb, gbias[:, b:b + 1, :].to_broadcast([P, TB, D]),
                                            ALU.add).then_inc(bias_added, 1)
                for b in range(B):
                    pool.wait_ge(bias_added, b + 1)
                    pool.wait_ge(upd_done, b * 2 + 2)
                    xb = x[:, b * TB:(b + 1) * TB, :]
                    nc.gpsimd.tensor_tensor(xb, xb, upd[:, b * TB:(b + 1) * TB, :], ALU.add).then_inc(x_done, 1)
                norm_b.pool_rstd(nc, pool, t)


TERMS = ((0, 0), (0, 1), (1, 0))


def attention1_order():
    order = []
    for u in range(UNITS):
        other = "v" if u % 2 == 0 else "y"
        order += [("s", u, 0), ("k", u), ("pv", u, 0), ("s", u, 1), ("q", u), ("pv", u, 1), ("s", u, 2), (other, u, 0),
                  ("s", u, 3), ("pv", u, 2), (other, u, 1), ("g", u), ("pv", u, 3)]
    return order


def attention1_stage(nc, t, d):
    order = attention1_order()
    ring_tasks = [task for task in order if task[0] in "sqkgv"]
    first_tasks = [("k", -1), ("q", -1)]
    RING, AHEAD = 4, len(first_tasks)
    place = {task: n + AHEAD for n, task in enumerate(ring_tasks)} | {task: n for n, task in enumerate(first_tasks)}
    assert len(ring_tasks) % RING == 0
    unmade = [("q", UNITS - 1), ("k", UNITS - 1)]
    turns = len(ring_tasks) // RING
    NB = S // P
    OFF = [sum(S - i * P for i in range(j)) for j in range(NB)]
    NP = sum(S - j * P for j in range(NB))
    hh = t["h_parts"]
    with ExitStack() as ctx:
        n = Names(nc, ctx, "attn1")
        wraw = n.sb("wraw", [P, KT, 8 * P], F32)
        wp = n.sb("wp", [P, 2, KT, 8 * P], F32R)
        woraw = n.sb("woraw", [P, 2, D], F32)
        wop = n.sb("wop", [P, 2, 2, D], F32R)
        normw = n.sb("normw", [P, H1], F32)
        mask = n.sb("mask", [P, 2, S], F32)
        qk = n.sb("qk", [P, 2, S], F32)
        qkp = n.sb("qkp", [P, 2, 2, 2, S], F32R)
        v = n.sb("v", [P, TB, 2 * P], F32)
        vp = n.sb("vp", [P, 2, 2, TB, 2 * P], F32R)
        gate = n.sb("gate", [P, 2, S], F32)
        p = n.sb("p", [P, NP], F32)
        pp = n.sb("pp", [P, 2, 2, NP], F32R)
        y = n.sb("y", [P, 2, S], F32)
        yp = n.sb("yp", [P, 2, 2, S], F32R)
        sq = n.sb("sq", [P, 2, S], F32)
        ssq = t["gate"][:, 0:2].rearrange("p l b n -> p (l b n)")
        ones = n.sb("ones", [P, 1], F32)
        yacc, rms = t["yacc"], t["rms"]
        ps = n.psum()
        O_BANK, Y_BANK = 4, 6

        ring_full = n.sems("ring_full", RING)
        w_loaded, wo_loaded, mask_loaded = n.sem("w_loaded"), n.sem("wo_loaded"), n.sems("mask_loaded", 2)
        w_hi, w_ready = n.sems("w_hi", 3), n.sems("w_ready", 3)
        norm_loaded, norm_halved = n.sem("norm_loaded"), n.sem("norm_halved")
        wo_scaled, wo_hi, wo_ready = n.sem("wo_scaled"), n.sem("wo_hi"), n.sem("wo_ready")
        q_silu, q_hi, q_ready = n.sem("q_silu"), n.sem("q_hi"), n.sem("q_ready")
        k_silu, k_hi, k_ready = n.sem("k_silu"), n.sem("k_hi"), n.sem("k_ready")
        v_silu, v_hi, v_ready = n.sem("v_silu"), n.sem("v_hi"), n.sem("v_ready")
        gate_done = n.sem("gate_done")
        p_masked, p_hi, p_ready = n.sem("p_masked"), n.sem("p_hi"), n.sem("p_ready")
        o_full, gated, y_hi, y_ready = n.sem("o_full"), n.sem("gated"), n.sem("y_hi"), n.sem("y_ready")
        squared, summed = n.sem("squared"), n.sem("summed")
        y_full, y_added = n.sem("y_full"), n.sem("y_added")
        zeroed, ssq_full, mean_done, rms_done = n.sem("zeroed"), n.sem("ssq_full"), n.sem("mean_done"), n.sem("rms_done")

        def bank(task):
            return ps[:, place[task] % RING, :]

        def filled(eng, task, it):
            m = place[task]
            i = ring_tasks.index(task) - RING if task in ring_tasks else -1
            missing = 1 if isinstance(it, int) and it == PAIRS - 1 and i >= 0 and ring_tasks[i] in unmade else 0
            eng.wait_ge(ring_full[m % RING], it * turns + (m // RING + 1 - missing))

        def emptied(eng, task, it):
            kind, u = task[0], task[1]
            if kind == "s":
                eng.wait_ge(p_masked, it * (UNITS * NB) + (u * NB + task[2] + 1))
            elif kind == "v":
                eng.wait_ge(v_silu, it * (2 * B) + (u + task[2] + 1))
            elif kind == "g":
                eng.wait_ge(gate_done, it * UNITS + (u + 1))
            else:
                eng.wait_ge({"q": q_silu, "k": k_silu}[kind], it * UNITS + (u + 2))

        PART = (slice(0, 2 * P), slice(2 * P, 7 * P), slice(7 * P, 8 * P))
        COLUMN = {("q", 0): 0, ("k", 0): P, ("q", 1): 2 * P, ("k", 1): 3 * P, ("g", 0): 4 * P, ("v", 0): 5 * P,
                  ("g", 1): 7 * P}

        def late(it, u, units):
            return not isinstance(it, int) or it * UNITS + u >= units

        def over_pairs(eng, body):
            body(0, True, False)
            with eng.Fori(1, PAIRS - 1) as it:
                body(it, False, False)
            body(PAIRS - 1, False, True)

        with nc.Block() as block:

            @block.sync
            def _(sp):
                sp.dma_start(wraw[:, :, :], d["w1p"][0]).then_inc(w_loaded, 16)
                sp.dma_start(normw[:, :], d["norm_w"]).then_inc(norm_loaded, 16)
                for h in range(2):
                    sp.dma_start(mask[:, h, :], t["decay_dram"][h]).then_inc(mask_loaded[h], 16)
                sp.dma_start(woraw[:, :, :], d["wout"][0]).then_inc(wo_loaded, 16)
                with sp.Fori(0, PAIRS - 1) as it:
                    sp.wait_ge(w_ready[2], it + 1)
                    sp.dma_start(wraw[:, :, :], d["w1p"][bass.ds(it + 1, 1)].rearrange("a p k n -> (a p) k n")
                                 ).then_inc(w_loaded, 16)
                    sp.wait_ge(wo_ready, it + 1)
                    sp.dma_start(woraw[:, :, :], d["wout"][bass.ds(it + 1, 1)].rearrange("a p k n -> (a p) k n")
                                 ).then_inc(wo_loaded, 16)
                    for h in range(2):
                        sp.wait_ge(p_masked, it * (UNITS * NB) + (UNITS - 1 + h) * NB)
                        sp.dma_start(mask[:, h, :], t["decay_dram"][bass.ds(it * 2 + (2 + h), 1)].rearrange(
                            "a p n -> (a p) n")).then_inc(mask_loaded[h], 16)

            @block.tensor
            def _(pe):
                def project(task, it):
                    kind, u = task[0], task[1]
                    unit = u + 1 if kind in "qk" else u
                    pair, unit = it + unit // UNITS, unit % UNITS
                    b, h = unit // 2, unit % 2
                    out = bank(task)
                    if kind == "k" and b == 0:
                        pe.wait_ge(w_ready[h], pair + 1)
                    if kind == "v" and b == 0 or kind == "g" and unit == 0:
                        pe.wait_ge(w_ready[1], pair + 1)
                    if kind == "g" and unit == 1:
                        pe.wait_ge(w_ready[2], pair + 1)
                    terms = [(k, tc) for k in range(KT) for tc in TERMS]
                    if kind == "v":
                        col = COLUMN[kind, 0]
                        for i in range(2):
                            tt = b * TB + 2 * task[2] + i
                            for m, (k, (a, c)) in enumerate(terms):
                                last = nc.tensor.matmul(out[:, i * 2 * P:(i + 1) * 2 * P], hh[:, a, k, tt * P:(tt + 1) * P],
                                                        wp[:, c, k, col:col + 2 * P], start=(m == 0), stop=(m == 5))
                    else:
                        col = COLUMN[kind, h]
                        for m, (k, (a, c)) in enumerate(terms):
                            last = nc.tensor.matmul(out, wp[:, a, k, col:col + P], hh[:, c, k, b * S:(b + 1) * S],
                                                    start=(m == 0), stop=(m == 5))
                    last.then_inc(ring_full[place[task] % RING], 1)

                def output(task):
                    i = task[2]
                    for half in range(2):
                        tt = 2 * i + half
                        for m, (h, (a, c)) in enumerate([(h, tc) for h in range(2) for tc in TERMS]):
                            last = nc.tensor.matmul(ps[:, Y_BANK + i, half * D:(half + 1) * D],
                                                    yp[:, a, h, tt * P:(tt + 1) * P], wop[:, c, h, :],
                                                    start=(m == 0), stop=(m == 5))
                    last.then_inc(y_full, 1)

                def values(j, u, it):
                    b, h = (u % UNITS) // 2, u % 2
                    if j == 0:
                        if late(it, u, 2):
                            pe.wait_ge(squared, it * UNITS + (u - 1))
                        if h == 0:
                            pe.wait_ge(v_ready, it * (2 * B) + (u + 2))
                    pe.wait_ge(p_ready, it * (UNITS * NB) + (u * NB + j + 1))
                    for m3, (a, c) in enumerate(TERMS):
                        last = nc.tensor.matmul(ps[:, O_BANK + h, j * P:S], vp[:, b % 2, a, j, h * P:(h + 1) * P],
                                                pp[:, h, c, OFF[j]:OFF[j] + S - j * P],
                                                start=(j == 0 and m3 == 0), stop=(j == NB - 1 and m3 == 2))
                    if j == NB - 1:
                        last.then_inc(o_full, 1)

                def body(it, first, last_pair):
                    for task in order:
                        kind, u = task[0], task[1]
                        b, h = u // 2, u % 2
                        if kind in "sqkgv":
                            if kind in "qk" and u == UNITS - 1 and last_pair:
                                continue
                            m = place[task]
                            i = ring_tasks.index(task) - RING
                            if last_pair and i >= 0 and ring_tasks[i] in unmade:
                                i -= RING
                            if i >= 0:
                                emptied(pe, ring_tasks[i], it)
                            elif not first:
                                emptied(pe, ring_tasks[i], it - 1)
                            elif i >= -AHEAD:
                                emptied(pe, first_tasks[i], 0)
                            if kind != "s":
                                project(task, it)
                                continue
                            j = task[2]
                            if j == 0:
                                pe.wait_ge(k_ready, it * UNITS + (u + 1))
                                pe.wait_ge(q_ready, it * UNITS + (u + 1))
                            for m3, (a, c) in enumerate(TERMS):
                                last = nc.tensor.matmul(bank(task)[:, 0:S - j * P], qkp[:, h, a, 1, j * P:(j + 1) * P],
                                                        qkp[:, h, c, 0, j * P:S], start=(m3 == 0), stop=(m3 == 2))
                            last.then_inc(ring_full[m % RING], 1)
                        elif kind == "pv":
                            if late(it, u, 1):
                                values(task[2], u - 1, it)
                        elif late(it, u, 3):
                            if task[2] == 0:
                                pe.wait_ge(y_ready, it * UNITS + (u - 1))
                                if u == 3:
                                    pe.wait_ge(wo_ready, it + 1)
                                if late(it, u, 5):
                                    pe.wait_ge(y_added, it * (2 * B) + (u - 3))
                            output(task)

                for task in first_tasks:
                    project(task, 0)
                over_pairs(pe, body)
                for j in range(NB):
                    values(j, UNITS - 1, PAIRS - 1)
                pe.wait_ge(y_ready, PAIRS * UNITS)
                pe.wait_ge(y_added, PAIRS * 2 * B - 2)
                for i in range(2):
                    output(("y", 1, i))
                pe.wait_ge(summed, PAIRS * UNITS)
                for tt in range(NT):
                    last = nc.tensor.matmul(ps[:, 0, tt:tt + 1], ssq[:, tt * P:(tt + 1) * P], ones[:, :],
                                            start=True, stop=True)
                last.then_inc(ssq_full, 1)

            @block.scalar
            def _(act):
                def split_weights(part, it):
                    act.wait_ge(w_loaded, it * 16 + 16)
                    nc.scalar.copy(wp[:, 0, :, PART[part]], wraw[:, :, PART[part]]).then_inc(w_hi[part], 1)

                def silu_split(task, which, unit, it):
                    silu_sem, hi_sem, ready = ((q_silu, q_hi, q_ready), (k_silu, k_hi, k_ready))[which]
                    filled(act, task, it)
                    if unit >= 0:
                        act.wait_ge(ready, it * UNITS + (unit + 1))
                    ins = nc.scalar.activation(qk[:, which, :], bank(task), ACT.Silu)
                    ins.then_inc(silu_sem, 1)
                    act.wait_ge(silu_sem, it * UNITS + (unit + 2))
                    nc.scalar.copy(qkp[:, (unit + 1) % 2, 0, which, :], qk[:, which, :]).then_inc(hi_sem, 1)

                def gate_of(u, it):
                    filled(act, ("g", u), it)
                    if late(it, u, 2):
                        act.wait_ge(gated, it * UNITS + (u - 1))
                    nc.scalar.activation(gate[:, u % 2, :], bank(("g", u)), ACT.Tanh, scale=0.5).then_inc(gate_done, 1)

                def values_of(i, u, it):
                    b = u // 2
                    task = ("v", u, i)
                    filled(act, task, it)
                    if late(it, u, 2):
                        act.wait_ge(v_ready, it * (2 * B) + (u + i - 1))
                    nc.scalar.activation(v[:, 2 * i:2 * i + 2, :].rearrange("p t n -> p (t n)"), bank(task),
                                         ACT.Silu).then_inc(v_silu, 1)
                    act.wait_ge(v_silu, it * (2 * B) + (u + i + 1))
                    nc.scalar.copy(vp[:, b % 2, 0, 2 * i:2 * i + 2, :], v[:, 2 * i:2 * i + 2, :]).then_inc(v_hi, 1)

                def scores_hi(u, j, it):
                    if j == 0 and late(it, u, 2):
                        act.wait_ge(o_full, it * UNITS + (u - 1))
                    act.wait_ge(p_masked, it * (UNITS * NB) + (u * NB + j + 1))
                    cols = slice(OFF[j], OFF[j] + S - j * P)
                    nc.scalar.copy(pp[:, u % 2, 0, cols], p[:, cols]).then_inc(p_hi, 1)

                def finish_unit(u, it):
                    h = u % 2
                    act.wait_ge(gated, it * UNITS + (u + 1))
                    if h == 0 and late(it, u, 2):
                        act.wait_ge(y_full, it * (2 * B) + u)
                    nc.scalar.copy(yp[:, 0, h, :], y[:, h, :]).then_inc(y_hi, 1)
                    if late(it, u, 2):
                        act.wait_ge(summed, it * UNITS + (u - 1))
                    nc.scalar.activation(sq[:, h, :], ps[:, O_BANK + h, :], ACT.Square).then_inc(squared, 1)

                for part in range(3):
                    split_weights(part, 0)
                silu_split(("k", -1), 1, -1, 0)
                silu_split(("q", -1), 0, -1, 0)

                def body(it, first, last_pair):
                    for u in range(UNITS):
                        more = not (last_pair and u == UNITS - 1)
                        scores_hi(u, 0, it)
                        if u == UNITS - 2 and not last_pair:
                            split_weights(0, it + 1)
                        if u == UNITS - 1 and not last_pair:
                            split_weights(1, it + 1)
                        if u == 0 and not first:
                            split_weights(2, it)
                        if late(it, u, 2):
                            finish_unit(u - 2, it)
                        if more:
                            silu_split(("k", u), 1, u, it)
                        scores_hi(u, 1, it)
                        if more:
                            silu_split(("q", u), 0, u, it)
                        scores_hi(u, 2, it)
                        if u % 2 == 0:
                            values_of(0, u, it)
                        scores_hi(u, 3, it)
                        if u % 2 == 0:
                            values_of(1, u, it)
                        gate_of(u, it)
                        if u == 2:
                            if not first:
                                act.wait_ge(y_full, it * (2 * B))
                            act.wait_ge(wo_scaled, it * 2 + 2)
                            nc.scalar.copy(wop[:, 0], woraw[:, :, :]).then_inc(wo_hi, 1)

                over_pairs(act, body)
                for u in (UNITS - 2, UNITS - 1):
                    finish_unit(u, PAIRS - 1)

            @block.vector
            def _(dve):
                def low(out, whole, high, ready):
                    nc.vector.tensor_tensor(out, whole, high.bitcast(F32), ALU.subtract).then_inc(ready, 1)

                def qk_low(which, unit, it):
                    hi_sem, ready = ((q_hi, q_ready), (k_hi, k_ready))[which]
                    dve.wait_ge(hi_sem, it * UNITS + (unit + 2))
                    low(qkp[:, (unit + 1) % 2, 1, which, :], qk[:, which, :], qkp[:, (unit + 1) % 2, 0, which, :], ready)

                def values_low(i, u, it):
                    b = u // 2
                    dve.wait_ge(v_hi, it * (2 * B) + (u + i + 1))
                    rows = slice(2 * i, 2 * i + 2)
                    low(vp[:, b % 2, 1, rows, :], v[:, rows, :], vp[:, b % 2, 0, rows, :], v_ready)

                def masked(u, j, it):
                    task = ("s", u, j)
                    cols = slice(OFF[j], OFF[j] + S - j * P)
                    filled(dve, task, it)
                    if u < 2 and j == 0:
                        dve.wait_ge(mask_loaded[u % 2], it * 16 + 16)
                    nc.vector.tensor_tensor(p[:, cols], bank(task)[:, 0:S - j * P], mask[:, u % 2, 0:S - j * P],
                                            ALU.mult).then_inc(p_masked, 1)

                def scores_low(u, j, it):
                    cols = slice(OFF[j], OFF[j] + S - j * P)
                    dve.wait_ge(p_hi, it * (UNITS * NB) + (u * NB + j + 1))
                    low(pp[:, u % 2, 1, cols], p[:, cols], pp[:, u % 2, 0, cols], p_ready)

                def gate_unit(u, it):
                    h = u % 2
                    dve.wait_ge(o_full, it * UNITS + (u + 1))
                    dve.wait_ge(gate_done, it * UNITS + (u + 1))
                    nc.vector.scalar_tensor_tensor(y[:, h, :], gate[:, h, :], 1.0, ps[:, O_BANK + h, :],
                                                   ALU.add, ALU.mult).then_inc(gated, 1)

                def y_low(u, it):
                    h = u % 2
                    dve.wait_ge(y_hi, it * UNITS + (u + 1))
                    low(yp[:, 1, h, :], y[:, h, :], yp[:, 0, h, :], y_ready)

                def add_output(u, i, it):
                    b = (u - 3) // 2 % B
                    dve.wait_ge(y_full, it * (2 * B) + (u - 2 + i))
                    rows = yacc[:, b * TB + 2 * i:b * TB + 2 * i + 2, :].rearrange("p t n -> p (t n)")
                    nc.vector.tensor_tensor(rows, rows, ps[:, Y_BANK + i, :], ALU.add).then_inc(y_added, 1)

                nc.vector.memset(yacc[:, :, :], 0.0).then_inc(zeroed, 1)
                dve.wait_ge(norm_loaded, 16)
                nc.vector.tensor_scalar(normw[:, :], normw[:, :], 0.5, None, ALU.mult).then_inc(norm_halved, 1)
                dve.wait_ge(norm_halved, 1)
                dve.wait_ge(zeroed, 1)
                qk_low(1, -1, 0)
                qk_low(0, -1, 0)

                def body(it, first, last_pair):
                    for u in range(UNITS):
                        more = not (last_pair and u == UNITS - 1)
                        if u == 2:
                            dve.wait_ge(wo_loaded, it * 16 + 16)
                            for h in range(2):
                                nc.vector.tensor_scalar(woraw[:, h, :], woraw[:, h, :], normw[:, at(it * 2 + h)], None,
                                                        ALU.mult).then_inc(wo_scaled, 1)
                        if late(it, u, 2):
                            gate_unit(u - 2, it)
                        masked(u, 0, it)
                        if late(it, u, 2):
                            y_low(u - 2, it)
                        scores_low(u, 0, it)
                        masked(u, 1, it)
                        if more:
                            qk_low(1, u, it)
                        scores_low(u, 1, it)
                        masked(u, 2, it)
                        if more:
                            qk_low(0, u, it)
                        scores_low(u, 2, it)
                        masked(u, 3, it)
                        if u % 2 == 0:
                            values_low(0, u, it)
                        elif late(it, u, 3):
                            add_output(u, 0, it)
                        scores_low(u, 3, it)
                        if u % 2 == 0:
                            values_low(1, u, it)
                        elif late(it, u, 3):
                            add_output(u, 1, it)

                over_pairs(dve, body)
                for u in (UNITS - 2, UNITS - 1):
                    gate_unit(u, PAIRS - 1)
                    y_low(u, PAIRS - 1)
                for i in range(2):
                    add_output(UNITS + 1, i, PAIRS - 1)
                dve.wait_ge(ssq_full, 1)
                nc.vector.tensor_scalar(rms[:, :], ps[:, 0, 0:NT], 1.0 / (H1 * D1), EPS_RMS, ALU.mult,
                                        ALU.add).then_inc(mean_done, 1)

            @block.gpsimd
            def _(pool):
                nc.gpsimd.memset(ones[:, :], 1.0)

                def weights_low(part, it):
                    pool.wait_ge(w_hi[part], it + 1)
                    nc.gpsimd.tensor_tensor(wp[:, 1, :, PART[part]], wraw[:, :, PART[part]],
                                            wp[:, 0, :, PART[part]].bitcast(F32), ALU.subtract).then_inc(w_ready[part], 1)

                def sum_unit(u, it):
                    b, h = (u % UNITS) // 2, u % 2
                    pool.wait_ge(squared, it * UNITS + (u + 1))
                    if h == 1:
                        pool.wait_ge(summed, it * UNITS + u)
                    cols = ssq[:, b * S:(b + 1) * S]
                    nc.gpsimd.tensor_tensor(cols, cols, sq[:, h, :], ALU.add).then_inc(summed, 1)

                sums_zeroed = n.sem("sums_zeroed")
                nc.gpsimd.memset(t["gate"][:, 0:2], 0.0).then_inc(sums_zeroed, 1)
                for part in range(3):
                    weights_low(part, 0)
                pool.wait_ge(sums_zeroed, 1)

                def body(it, first, last_pair):
                    for u in range(UNITS):
                        if u == UNITS - 2 and not last_pair:
                            weights_low(0, it + 1)
                        if u == UNITS - 1 and not last_pair:
                            weights_low(1, it + 1)
                        if u == 0 and not first:
                            weights_low(2, it)
                        if late(it, u, 2):
                            sum_unit(u - 2, it)
                        if u == 2:
                            pool.wait_ge(wo_hi, it + 1)
                            nc.gpsimd.tensor_tensor(wop[:, 1], woraw[:, :, :], wop[:, 0].bitcast(F32),
                                                    ALU.subtract).then_inc(wo_ready, 1)

                over_pairs(pool, body)
                for u in (UNITS - 2, UNITS - 1):
                    sum_unit(u, PAIRS - 1)
                pool.wait_ge(mean_done, 1)
                nc.gpsimd.tensor_tensor(rms[:, :], rms[:, :], t["neg_half"][:, :], ALU.pow).then_inc(rms_done, 1)


def experts_stage(nc, t, d):
    x, yacc, rms, hh = t["x"], t["yacc"], t["rms"], t["h_parts"]
    TE = FE // P
    PIECES = 12
    PC = FT * P // 2
    with ExitStack() as ctx:
        n = Names(nc, ctx, "experts")
        wg = n.sb("wg", [P, 2, KT, FT * P], F32R)
        wu = n.sb("wu", [P, 2, KT, FT * P], F32R)
        w2 = n.sb("w2", [P, 2, FT, D], F32R)
        raw = n.sb("raw", [P, 2, PC], F32)
        rw = n.sb("rw", [P, KT, E], F32)
        rwp = n.sb("rwp", [P, 2, KT, E], F32R)
        spread32 = n.sb("spread32", [EROWS, FE], F32)
        spread = n.sb("spread", [EROWS, FE], BF16)
        expert_id = n.sb("expert_id", [P, E], F32)
        tile8 = [P, NT, E]
        scores = n.sb("scores", tile8, F32)
        norm1 = n.sb("norm1", [P, NT], F32)
        best = n.sb("best", tile8, F32)
        best_id = n.sb("best_id", tile8, U32)
        best_idf = n.sb("best_idf", tile8, F32)
        chosen = n.sb("chosen", [P, 2, NT, E], F32)
        cw = n.sb("cw", tile8, F32)
        rest = n.sb("rest", tile8, F32)
        cwp = n.sb("cwp", [P, NT, 3, E], BF16)
        cwt = n.sb("cwt", [EROWS, B * S], BF16)
        hid = n.sb("hid", [P, 2, S], F32)
        hidp = n.sb("hidp", [P, 2, 2, S], F32R)
        ps = n.psum()
        norm = SplitNorm(n, "n", 1, 3, hh, yacc, 0)
        sg = yacc[:, 0:4, :].rearrange("p (b t) n -> p b (t n)", b=2)
        paired = yacc[:, 4:8, :].rearrange("p (b t) n -> p b (t n)", b=2)
        upd = yacc[:, 8:12, :]

        raw_loaded, raw_high, raw_low = n.sems("raw_loaded", 2), n.sem("raw_high"), n.sem("raw_low")
        small_loaded, spread_cast, rw_high, rw_low = (n.sem(s) for s in ("small_loaded", "spread_cast", "rw_high", "rw_low"))
        scaled, x_added, dve_held, pool_held = n.sem("scaled"), n.sem("x_added"), n.sem("dve_held"), n.sem("pool_held")
        logits_made, router, exp_done = n.sem("logits_made"), n.sem("router"), n.sem("exp_done")
        ids_ready, cwp_done, cw_turned, cwt_done = (n.sem(s) for s in ("ids_ready", "cwp_done", "cw_turned", "cwt_done"))
        g_made, u_made, c_made, y_made = (n.sem(s) for s in ("g_made", "u_made", "c_made", "y_made"))
        silu_done, pair_done, hid_done, hid_high, hid_low = (
            n.sem(s) for s in ("silu_done", "pair_done", "hid_done", "hid_high", "hid_low"))
        down_done, pe_held = n.sem("down_done"), n.sem("pe_held")
        upd_done, stored = n.sem("upd_done"), n.sem("stored")
        G_BANK, U_BANK, C_BANK, Y_BANK, L_BANK = 0, 1, 2, 4, 3

        def piece(m):
            which, rest_ = m // 4, m % 4
            k, cols = rest_ // 2, slice((rest_ % 2) * PC, (rest_ % 2 + 1) * PC)
            if which < 2:
                return d["wg" if which == 0 else "wu"][:, k, cols], [(wg, wu)[which][:, c, k, cols] for c in range(2)]
            cols = slice(rest_ * (FT * D // 4), (rest_ + 1) * (FT * D // 4))
            return (d["w2"].rearrange("p f n -> p (f n)")[:, cols],
                    [w2[:, c].rearrange("p f n -> p (f n)")[:, cols] for c in range(2)])

        with nc.Block() as block:

            @block.sync
            def _(sp):
                sp.dma_start(rw[:, :, :], d["router"]).then_inc(small_loaded, 16)
                sp.dma_start(spread32[:, :], d["spread"]).then_inc(small_loaded, 16)
                for m in range(PIECES):
                    if m >= 2:
                        sp.wait_ge(raw_low, m - 1)
                    sp.dma_start(raw[:, m % 2, :], piece(m)[0]).then_inc(raw_loaded[m % 2], 16)
                with sp.Fori(0, B) as it:
                    sp.wait_ge(x_added, it + (B + 1))
                    sp.dma_start(t["out"][:, bass.ds(it * TB, TB), :], x[:, bass.ds(it * TB, TB), :]).then_inc(stored, 16)
                sp.wait_ge(stored, 16 * B)

            @block.tensor
            def _(pe):
                for b in range(B):
                    norm.tensor_turn(nc, pe, t, ps, b)
                pe.wait_ge(norm.low_done, B)
                pe.wait_ge(rw_low, 1)
                for tt in range(NT):
                    for m, (k, (a, c)) in enumerate([(k, tc) for k in range(KT) for tc in TERMS]):
                        last = nc.tensor.matmul(ps[:, L_BANK, tt * E:(tt + 1) * E], hh[:, a, k, tt * P:(tt + 1) * P],
                                                rwp[:, c, k, :], start=(m == 0), stop=(m == 5))
                last.then_inc(logits_made, 1)

                def hidden(w, bank, f, it, full):
                    for m, (k, (a, c)) in enumerate([(k, tc) for k in range(KT) for tc in TERMS]):
                        last = nc.tensor.matmul(ps[:, bank, :], w[:, a, k, f * P:(f + 1) * P],
                                                hh[:, c, k, at(it * S, S)], start=(m == 0), stop=(m == 5))
                    last.then_inc(full, 1)

                def down(f, it, it_f):
                    pe.wait_ge(hid_low, it_f)
                    for tt in range(TB):
                        for m, (a, c) in enumerate(TERMS):
                            last = nc.tensor.matmul(ps[:, Y_BANK + tt, 0:D], hidp[:, f % 2, a, tt * P:(tt + 1) * P],
                                                    w2[:, c, f, :], start=(f == 0 and m == 0), stop=(f == FT - 1 and m == 2))
                    if f == FT - 1:
                        last.then_inc(y_made, 1)
                    else:
                        last.then_inc(down_done, 1)

                def batch(it, first):
                    for f in range(FT):
                        at_f = it * FT + f
                        if not (first and f == 0):
                            pe.wait_ge(silu_done, at_f)
                        hidden(wg, G_BANK, f, it, g_made)
                        if f > TE:
                            pe.wait_ge(hid_done, at_f)
                        elif not (first and f == 0):
                            if f == 0:
                                pe.wait_ge(hid_done, at_f)
                            else:
                                pe.wait_ge(pair_done, it * TE + f)
                        hidden(wu, U_BANK, f, it, u_made)
                        if f < TE:
                            if first and f == 0:
                                pe.wait_ge(cwp_done, 3)
                                turned = ps[:, 6:8, :].bitcast(BF16).rearrange("p a n -> p (a n)")
                                for tt in range(NT):
                                    last = nc.tensor.transpose(turned[0:EROWS, tt * P:(tt + 1) * P],
                                                               cwp[:, tt, :, :].rearrange("p a e -> p (a e)"), t["identb"][:, :])
                                last.then_inc(cw_turned, 1)
                                pe.wait_ge(cwt_done, 1)
                            else:
                                pe.wait_ge(hid_done, at_f)
                            pe.sem_inc(pe_held, 1)
                            nc.tensor.matmul(ps[:, C_BANK, :], spread[:, f * P:(f + 1) * P], cwt[:, at(it * S, S)],
                                             start=True, stop=True).then_inc(c_made, 1)
                        if f > 0:
                            if f == 1 and not first:
                                pe.wait_ge(upd_done, it)
                            down(f - 1, it, at_f)
                        elif not first:
                            down(FT - 1, it, at_f)

                pe.wait_ge(raw_low, PIECES)
                batch(0, True)
                with pe.Fori(1, B) as it:
                    batch(it, False)
                down(FT - 1, B, B * FT)

            @block.scalar
            def _(act):
                def split(m):
                    act.wait_ge(raw_loaded[m % 2], 16 * (m // 2 + 1))
                    nc.scalar.copy(piece(m)[1][0], raw[:, m % 2, :]).then_inc(raw_high, 1)

                act.wait_ge(small_loaded, 32)
                nc.scalar.copy(rwp[:, 0], rw[:, :, :]).then_inc(rw_high, 1)
                nc.scalar.copy(spread[:, :], spread32[:, :]).then_inc(spread_cast, 1)
                for m in range(PIECES):
                    split(m)
                    if m % 3 == 2:
                        norm.scalar_high(nc, act, t, ps, m // 3)
                act.wait_ge(router, 2)
                nc.scalar.activation(scores[:, :, :], scores[:, :, :], ACT.Exp).then_inc(exp_done, 1)

                def high(f, count):
                    act.wait_ge(hid_done, count)
                    nc.scalar.copy(hidp[:, f % 2, 0, :], hid[:, f % 2, :]).then_inc(hid_high, 1)

                def batch(it, first):
                    for f in range(FT):
                        at_f = it * FT + f
                        act.wait_ge(g_made, at_f + 1)
                        nc.scalar.activation(sg[:, f % 2, :], ps[:, G_BANK, :], ACT.Silu).then_inc(silu_done, 1)
                        if f > 0:
                            high(f - 1, at_f)
                    high(FT - 1, it * FT + FT)

                batch(0, True)
                with act.Fori(1, B) as it:
                    batch(it, False)

            @block.vector
            def _(dve):
                dve.wait_ge(rw_high, 1)
                nc.vector.tensor_tensor(rwp[:, 1], rw[:, :, :], rwp[:, 0].bitcast(F32), ALU.subtract).then_inc(rw_low, 1)
                with dve.Fori(0, B) as it:
                    for tt in range(TB):
                        tile = yacc[:, bass.ds(it * TB + tt, 1), :]
                        last = nc.vector.scalar_tensor_tensor(tile, tile, rms[:, bass.ds(it * TB + tt, 1)],
                                                              t["gate"][:, 2, bass.ds(it, 1), :], ALU.mult, ALU.mult)
                    last.then_inc(scaled, 1)
                with dve.Fori(0, B) as it:
                    dve.wait_ge(x_added, it + 1)
                    dve.sem_inc(dve_held, 1)
                    norm.vector_stats(nc, x, it)
                norm.vector_aggregate(nc, dve)
                norm.vector_norm(nc, dve, x)
                for b in range(B):
                    norm.vector_low(nc, dve, b)

                step = 0

                def then(ins):
                    nonlocal step
                    step += 1
                    ins.then_inc(router, 1)
                    dve.wait_ge(router, step)

                wide = [P, NT, E]
                lg = ps[:, L_BANK, 0:NT * E].rearrange("p (t e) -> p t e", e=E)
                dve.wait_ge(logits_made, 1)
                then(nc.vector.tensor_reduce(norm1[:, :], lg, AX.X, ALU.max))
                then(nc.vector.tensor_tensor(scores[:, :, :], lg, norm1[:, :].unsqueeze(2).to_broadcast(wide), ALU.subtract))
                dve.wait_ge(exp_done, 1)
                then(nc.vector.tensor_reduce(norm1[:, :], scores[:, :, :], AX.X, ALU.add))
                then(nc.vector.reciprocal(norm1[:, :], norm1[:, :]))
                then(nc.vector.tensor_tensor(scores[:, :, :], scores[:, :, :], norm1[:, :].unsqueeze(2).to_broadcast(wide),
                                             ALU.mult))
                for tt in range(NT):
                    last = nc.vector.max(out=best[:, tt, :], in_=scores[:, tt, :])
                then(last)
                for tt in range(NT):
                    last = nc.vector.max_index(best_id[:, tt, :], best[:, tt, :], scores[:, tt, :])
                then(last)
                then(nc.vector.tensor_copy(best_idf[:, :, :], best_id[:, :, :]))
                then(nc.vector.tensor_reduce(norm1[:, :], best[:, :, 0:2], AX.X, ALU.add))
                then(nc.vector.tensor_scalar(norm1[:, :], norm1[:, :], 1e-20, None, ALU.add))
                then(nc.vector.reciprocal(norm1[:, :], norm1[:, :]))
                then(nc.vector.tensor_tensor(best[:, :, 0:2], best[:, :, 0:2],
                                             norm1[:, :].unsqueeze(2).to_broadcast([P, NT, 2]), ALU.mult))
                dve.wait_ge(ids_ready, 1)
                for c in range(2):
                    last = nc.vector.tensor_tensor(chosen[:, c], expert_id[:, :].unsqueeze(1).to_broadcast(wide),
                                                   best_idf[:, :, c:c + 1].to_broadcast(wide), ALU.is_equal)
                then(last)
                for c in range(2):
                    last = nc.vector.tensor_tensor(chosen[:, c], chosen[:, c], best[:, :, c:c + 1].to_broadcast(wide), ALU.mult)
                then(last)
                then(nc.vector.tensor_tensor(cw[:, :, :], chosen[:, 0], chosen[:, 1], ALU.add))
                nc.vector.tensor_copy(cwp[:, :, 0, :], cw[:, :, :]).then_inc(cwp_done, 1)
                dve.wait_ge(cwp_done, 1)
                then(nc.vector.tensor_tensor(rest[:, :, :], cw[:, :, :], cwp[:, :, 0, :], ALU.subtract))
                nc.vector.tensor_copy(cwp[:, :, 1, :], rest[:, :, :]).then_inc(cwp_done, 1)
                dve.wait_ge(cwp_done, 2)
                nc.vector.tensor_tensor(cwp[:, :, 2, :], rest[:, :, :], cwp[:, :, 1, :], ALU.subtract).then_inc(cwp_done, 1)
                dve.wait_ge(cw_turned, 1)
                nc.vector.tensor_copy(cwt[:, :], ps[0:EROWS, 6:8, :].bitcast(BF16).rearrange("p a n -> p (a n)")
                                      ).then_inc(cwt_done, 1)

                def low(f, count):
                    dve.wait_ge(hid_high, count)
                    nc.vector.tensor_tensor(hidp[:, f % 2, 1, :], hid[:, f % 2, :], hidp[:, f % 2, 0, :].bitcast(F32),
                                            ALU.subtract).then_inc(hid_low, 1)

                def batch(it, first):
                    for f in range(FT):
                        at_f = it * FT + f
                        if f > 0:
                            low(f - 1, at_f)
                        dve.wait_ge(u_made, at_f + 1)
                        dve.wait_ge(silu_done, at_f + 1)
                        if f < TE:
                            nc.vector.tensor_tensor(paired[:, f % 2, :], ps[:, U_BANK, :], sg[:, f % 2, :],
                                                    ALU.mult).then_inc(pair_done, 1)
                            dve.wait_ge(pair_done, it * TE + (f + 1))
                            dve.wait_ge(c_made, it * TE + (f + 1))
                            nc.vector.tensor_tensor(hid[:, f % 2, :], ps[:, C_BANK, :], paired[:, f % 2, :],
                                                    ALU.mult).then_inc(hid_done, 1)
                        else:
                            nc.vector.tensor_tensor(hid[:, f % 2, :], ps[:, U_BANK, :], sg[:, f % 2, :],
                                                    ALU.mult).then_inc(hid_done, 1)
                        if f == 0 and not first:
                            output(it)
                    low(FT - 1, it * FT + FT)

                def output(it):
                    dve.wait_ge(y_made, it)
                    dve.wait_ge(x_added, it + (B - 1))
                    if isinstance(it, int):
                        g = t["gate"][:, 3, it - 1:it, :]
                    else:
                        g = t["gate"][:, 3, bass.ds(it - 1, 1), :]
                    nc.vector.tensor_tensor(upd[:, :, :], ps[:, Y_BANK:Y_BANK + TB, 0:D], g.to_broadcast([P, TB, D]),
                                            ALU.mult).then_inc(upd_done, 1)

                batch(0, True)
                with dve.Fori(1, B) as it:
                    batch(it, False)
                output(B)

            @block.gpsimd
            def _(pool):
                nc.gpsimd.iota(expert_id[:, :], [[1, E]], base=0, channel_multiplier=0,
                               allow_small_or_imprecise_dtypes=True).then_inc(ids_ready, 1)
                with pool.Fori(0, B) as it:
                    pool.wait_ge(scaled, it + 1)
                    pool.sem_inc(pool_held, 1)
                    xb = x[:, bass.ds(it * TB, TB), :]
                    nc.gpsimd.tensor_tensor(xb, xb, yacc[:, bass.ds(it * TB, TB), :], ALU.add).then_inc(x_added, 1)

                def low(m):
                    pool.wait_ge(raw_high, m + 1)
                    hi, lo = piece(m)[1]
                    nc.gpsimd.tensor_tensor(lo, raw[:, m % 2, :], hi.bitcast(F32), ALU.subtract).then_inc(raw_low, 1)

                norm.pool_rstd(nc, pool, t)
                for m in range(PIECES):
                    low(m)
                with pool.Fori(0, B) as it:
                    pool.wait_ge(upd_done, it + 1)
                    pool.sem_inc(pool_held, 1)
                    xb = x[:, bass.ds(it * TB, TB), :]
                    nc.gpsimd.tensor_tensor(xb, xb, upd[:, :, :], ALU.add).then_inc(x_added, 1)


ALL_STAGES = [modulation_stage, attention0_stage, ffn0_stage, attention1_stage, experts_stage]



def build(nc, ins, out):
    d = dram_views(ins)
    with ExitStack() as ctx:
        n = Names(nc, ctx, "all")
        t = {
            "x": n.sb("x", [P, NT, D], F32),
            "mod": n.sb("mod", [P, 2, 6, KT, B], F32),
            "gate": n.sb("gate", [P, 4, B, D], F32),
            "ident": n.sb("ident", [P, P], F32),
            "ident16": n.sb("ident16", [P, P], F16),
            "identb": n.sb("identb", [P, P], BF16),
            "later_key": n.sb("later_key", [P, P], BF16),
            "later_key_t": n.sb("later_key_t", [P, P], BF16),
            "neg_half": n.sb("neg_half", [P, NT], F32),
            "h_parts": n.sb("h_parts", [P, 2, KT, B * S], F32R),
            "yacc": n.sb("yacc", [P, NT, D], F32),
            "rms": n.sb("rms", [P, NT], F32),
            "out": out,
            "decay_dram": nc.dram_tensor("decay_masks", [H1, P, S], F32, kind="Internal").ap(),
        }
        for stage in ALL_STAGES:
            before = nc.snapshot_sems()
            stage(nc, t, d)
            if stage is not ALL_STAGES[-1]:
                nc.clear_and_free_semaphores(nc.allocated_since(before))
                nc.all_engine_barrier()


def dram_views(ins):
    return {
        "x": ins["x"],
        "cond": ins["cond"],
        "wmod0": ins["wmod0"],
        "wmod1": ins["wmod1"],
        "slope": ins["slope"].partition_broadcast(P),
        "wqkv0": ins["wqkv0"],
        "wo0": ins["wo0"],
        "bias0": ins["bias0"],
        "norm_scale0": ins["norm_scale0"].partition_broadcast(P),
        "cosd": ins["cosd"],
        "sind": ins["sind"],
        "wffn": ins["wffn"],
        "ffn_rows": ins["ffn_rows"].partition_broadcast(P),
        "w1p": ins["w1p"],
        "wout": ins["wout"],
        "norm_w": ins["norm_w"],
        "router": ins["router"],
        "wg": ins["wg"], "wu": ins["wu"], "w2": ins["w2"], "spread": ins["spread"],
    }


def laid_out(i):
    a = {k: np.asarray(v) for k, v in i.items()}

    def rows(w):
        w = np.asarray(w)
        return np.ascontiguousarray(w.reshape(-1, P, w.shape[1]).transpose(1, 0, 2))

    r = {"x": np.ascontiguousarray(a["L0_attn_x"].reshape(NT, P, D).transpose(1, 0, 2))}
    c = np.stack([a["L0_c"], a["L1_c"]])
    r["cond"] = np.ascontiguousarray(c.reshape(2, B, KT, P).transpose(3, 0, 2, 1))
    r["wmod0"], r["wmod1"] = rows(a["L0_wmod"]), rows(a["L1_wmod"])
    r["slope"] = np.ascontiguousarray(a["L1_attn_slope_rate"].reshape(H1))
    r["wqkv0"] = rows(np.concatenate([a["L0_attn_wq"], a["L0_attn_wk"], a["L0_attn_wv"]], 1))
    r["wo0"] = rows(a["L0_attn_wo"])
    r["bias0"] = np.concatenate([a["L0_attn_bq"], a["L0_attn_bk"], a["L0_attn_bv"], a["L0_attn_bo"]])[None]
    r["norm_scale0"] = np.stack([a["L0_attn_q_norm_scale"], a["L0_attn_k_norm_scale"]])
    f = np.float32
    inv = (f(1.0) / np.power(f(10000.0), np.arange(0, D0, 2, dtype=f) / f(D0))).astype(f)
    ang = np.outer(np.arange(S, dtype=f), inv).astype(f)

    def table(v):
        v = np.concatenate([v, v], 1).astype(f)
        return np.ascontiguousarray(v.reshape(TB, P, D0).transpose(1, 0, 2))

    r["cosd"], r["sind"] = table(np.cos(ang)), table(np.sin(ang))
    r["wffn"] = rows(a["L0_ffn_weight"].T)
    r["ffn_rows"] = np.stack([a["L0_ffn_scale_weight"], a["L0_ffn_bias"]])
    wqkv = a["L1_attn_w_qkv"].reshape(H1, 3, D1, D)
    wgate = a["L1_attn_w_gate"].reshape(H1, D1, D)
    pairs = []
    for p in range(PAIRS):
        h = [2 * p, 2 * p + 1]
        pairs.append(rows(np.concatenate([wqkv[h[0], 0], wqkv[h[0], 1], wqkv[h[1], 0], wqkv[h[1], 1], wgate[h[0]],
                                          wqkv[h[0], 2], wqkv[h[1], 2], wgate[h[1]]], 0).T))
    r["w1p"] = np.stack(pairs)
    r["wout"] = np.ascontiguousarray(a["L1_attn_w_out"].T.reshape(PAIRS, 2, P, D).transpose(0, 2, 1, 3))
    r["norm_w"] = np.ascontiguousarray(a["L1_attn_norm_w"].reshape(H1, P).T)
    r["router"] = rows(a["L1_ffn_gate_w"].T)
    w1 = a["L1_ffn_w1"]

    def hidden(w, s):
        w = np.concatenate([w.transpose(1, 0, 2).reshape(D, FE), s.T, np.zeros((D, FT * P - FA), w.dtype)], 1)
        return rows(w)

    r["wg"], r["wu"] = hidden(w1[:, :, :I], a["L1_ffn_sw1"]), hidden(w1[:, :, I:], a["L1_ffn_sw2"])
    w2 = np.concatenate([a["L1_ffn_w2"].reshape(FE, D), a["L1_ffn_sw3"].T, np.zeros((FT * P - FA, D), f)], 0)
    r["w2"] = rows(w2)
    own = np.zeros((3, E, FE), f)
    for e in range(E):
        own[:, e, e * I:(e + 1) * I] = 1.0
    r["spread"] = own.reshape(EROWS, FE)
    return r


def kernel(**inputs):
    import concourse.bacc as bacc
    from concourse.bass_utils import run_bass_kernel_spmd

    nc = bacc.Bacc("TRN2", target_bir_lowering=False, num_devices=1)
    arrays = laid_out(inputs)
    ins = {k: nc.dram_tensor(f"in_{k}", v.shape, mybir.dt.from_np(v.dtype), kind="ExternalInput").ap()
           for k, v in arrays.items()}
    out = nc.dram_tensor("out", (P, NT, D), F32, kind="ExternalOutput").ap()
    build(nc, ins, out)
    r = run_bass_kernel_spmd(nc, [{f"in_{k}": v for k, v in arrays.items()}], core_ids=[0])
    return r.results[0]["out"].transpose(1, 0, 2).reshape(B, S, D)
```

```python
from contextlib import ExitStack

import numpy as np
import concourse.bass as bass
from concourse import mybir

F32 = mybir.dt.float32
F32R = mybir.dt.float32r
F16 = mybir.dt.float16
BF16 = mybir.dt.bfloat16
U32 = mybir.dt.uint32
ALU = mybir.AluOpType
ACT = mybir.ActivationFunctionType
AX = mybir.AxisListType

P = 128
D = 256
KT = D // P
B, S = 4, 512
NT = B * S // P
TB = S // P
EPS_LN = 1e-5
EPS_RMS = 1e-6

H0, G0, D0 = 16, 4, 16
R0 = H0 // G0
QKV0 = (H0 + 2 * G0) * D0
SLOT = 32
SHIFT = 256.0
MASKED = -1e30

H1, D1 = 16, 128
PAIRS = H1 // 2
UNITS = 2 * B

E, I = 8, 176
FE = E * I
FA = FE + I
FT = -(-FA // P)
EROWS = E * 3


class Names:

    def __init__(self, nc, ctx, stage):
        self.nc, self.ctx, self.stage = nc, ctx, stage

    def sb(self, name, shape, dt):
        return self.ctx.enter_context(self.nc.sbuf_tensor(f"{self.stage}_{name}", shape, dt))

    def psum(self):
        return self.ctx.enter_context(self.nc.psum_tensor(f"{self.stage}_psum", [P, 8, 512], F32))

    def sem(self, name):
        return self.nc.alloc_semaphore(f"{self.stage}_{name}")

    def sems(self, name, n):
        return [self.sem(f"{name}{k}") for k in range(n)]


def at(i, size=1):
    return slice(i, i + size) if isinstance(i, int) else bass.ds(i, size)


def modulation_stage(nc, t, d):
    with ExitStack() as ctx:
        n = Names(nc, ctx, "mod")
        cond = n.sb("cond", [P, 2, KT, B], F32)
        scond = n.sb("scond", [P, 2, KT, B], F32)
        wmod = n.sb("wmod", [P, 2, KT, 6 * D], F32)
        gneg = n.sb("gneg", [P, 2, 2, KT, B], F32)
        gsign = n.sb("gsign", [P, 2, 2, KT, B], F32)
        gpart = n.sb("gpart", [P, 2, 4, B, KT], F32R)
        diag = n.sb("diag", [P, 4, 2, B * KT, P], F32R)
        ones32 = n.sb("ones32", [P, P], F32)
        ones = n.sb("ones", [P, P], F32R)
        dist = n.sb("dist", [P, S], F32)
        nslope = n.sb("nslope", [P, H1], F32)
        decay = n.sb("decay", [P, H1, S], F32)
        st = n.sb("st", [P, NT, 6], F32)
        mv = n.sb("mv", [P, NT, 2], F32)
        rstd = n.sb("rstd", [P, NT], F32)
        ps = n.psum()
        stats_done, aggr_done, var_eps, rstd_done = (n.sem(s) for s in ("stats_done", "aggr_done", "var_eps", "rstd_done"))
        half_set, xn_done = n.sem("half_set"), n.sem("xn_done")
        loaded, silu_done = n.sem("loaded"), n.sem("silu_done")
        cond_loaded, wmod_loaded = n.sem("cond_loaded"), n.sems("wmod_loaded", 2)
        mod_ready, mod_copied, plus_one = n.sem("mod_ready"), n.sem("mod_copied"), n.sem("plus_one")
        gate_step, diag_ready, gates_ready = n.sem("gate_step"), n.sem("diag_ready"), n.sem("gates_ready")
        ident_step, const_ready = n.sem("ident_step"), n.sem("const_ready")
        slope_loaded, slope_neg, decay_ready = n.sem("slope_loaded"), n.sem("slope_neg"), n.sem("decay_ready")
        masked, stored, dist_step = n.sem("masked"), n.sem("stored"), n.sem("dist_step")
        gates_copied = n.sem("gates_copied")
        ones_set, ones_ready, gate_parts = n.sem("ones_set"), n.sem("ones_ready"), n.sem("gate_parts")

        with nc.Block() as block:

            @block.sync
            def _(sp):
                sp.dma_start(cond[:, :, :, :], d["cond"]).then_inc(cond_loaded, 16)
                sp.dma_start(nslope[:, :], d["slope"]).then_inc(slope_loaded, 16)
                sp.dma_start(wmod[:, 0], d["wmod0"]).then_inc(wmod_loaded[0], 16)
                sp.dma_start(t["x"][:, :, :], d["x"]).then_inc(loaded, 16)
                sp.dma_start(wmod[:, 1], d["wmod1"]).then_inc(wmod_loaded[1], 16)
                for h in range(H1):
                    sp.wait_ge(masked, h + 1)
                    sp.dma_start(t["decay_dram"][h], decay[:, h, :]).then_inc(stored, 16)
                sp.wait_ge(loaded, 16)
                sp.wait_ge(stored, 16 * H1)

            @block.gpsimd
            def _(pool):
                nc.gpsimd.memset(t["ident"][:, :], 0.0).then_inc(ident_step, 1)
                nc.gpsimd.memset(t["ident16"][:, :], 0.0).then_inc(ident_step, 1)
                nc.gpsimd.memset(t["identb"][:, :], 0.0).then_inc(ident_step, 1)
                nc.gpsimd.memset(t["later_key"][:, :], 0.0).then_inc(ident_step, 1)
                nc.gpsimd.memset(t["later_key_t"][:, :], 0.0).then_inc(ident_step, 1)
                nc.gpsimd.memset(ones32[:, :], 1.0).then_inc(ones_set, 1)
                nc.gpsimd.memset(t["neg_half"][:, :], -0.5).then_inc(half_set, 1)
                nc.gpsimd.iota(dist[:, :], [[1, S]], base=0, channel_multiplier=-1,
                               allow_small_or_imprecise_dtypes=True).then_inc(dist_step, 1)
                pool.wait_ge(ident_step, 5)
                for m in ("ident", "ident16", "identb"):
                    nc.gpsimd.affine_select(out=t[m][:, :], in_=t[m][:, :], compare_op=ALU.not_equal, fill=1.0,
                                            base=0, pattern=[[-1, P]], channel_multiplier=1)
                nc.gpsimd.affine_select(out=t["later_key"][:, :], in_=t["later_key"][:, :], compare_op=ALU.is_ge,
                                        fill=MASKED, base=0, pattern=[[-1, P]], channel_multiplier=1)
                nc.gpsimd.affine_select(out=t["later_key_t"][:, :], in_=t["later_key_t"][:, :], compare_op=ALU.is_ge,
                                        fill=MASKED, base=0, pattern=[[1, P]],
                                        channel_multiplier=-1).then_inc(const_ready, 1)
                pool.wait_ge(half_set, 1)
                pool.wait_ge(aggr_done, 1)
                nc.gpsimd.tensor_scalar(rstd[:, :], mv[:, :, 1], EPS_LN, None, ALU.add).then_inc(var_eps, 1)
                pool.wait_ge(var_eps, 1)
                nc.gpsimd.tensor_tensor(rstd[:, :], rstd[:, :], t["neg_half"][:, :], ALU.pow).then_inc(rstd_done, 1)
                for h in range(H1):
                    pool.wait_ge(decay_ready, h + 1)
                    nc.gpsimd.affine_select(out=decay[:, h, 0:P], in_=decay[:, h, 0:P], compare_op=ALU.is_ge,
                                            fill=0.0, base=0, pattern=[[1, P]],
                                            channel_multiplier=-1).then_inc(masked, 1)

            @block.scalar
            def _(act):
                act.wait_ge(cond_loaded, 16)
                nc.scalar.activation(scond[:, :, :, :], cond[:, :, :, :], ACT.Silu).then_inc(silu_done, 1)
                act.wait_ge(ones_set, 1)
                nc.scalar.copy(ones[:, :], ones32[:, :]).then_inc(ones_ready, 1)
                act.wait_ge(dist_step, 2)
                act.wait_ge(slope_neg, 1)
                for h in range(H1):
                    nc.scalar.activation(decay[:, h, :], dist[:, :], ACT.Exp,
                                         scale=nslope[:, h:h + 1]).then_inc(decay_ready, 1)
                for g in range(4):
                    act.wait_ge(gates_ready, g + 1)
                    nc.scalar.copy(t["gate"][:, g].rearrange("p (c b) n -> p c (b n)", c=2),
                                   ps[:, 2 * (g % 4):2 * (g % 4) + 2, :]).then_inc(gates_copied, 1)

            @block.vector
            def _(dve):
                dve.wait_ge(dist_step, 1)
                nc.vector.tensor_scalar(dist[:, :], dist[:, :], 0.0, None, ALU.max).then_inc(dist_step, 1)
                dve.wait_ge(slope_loaded, 16)
                nc.vector.tensor_scalar(nslope[:, :], nslope[:, :], -1.0, None, ALU.mult).then_inc(slope_neg, 1)
                dve.wait_ge(loaded, 16)
                for tile in range(NT):
                    nc.vector.bn_stats(st[:, tile, :], t["x"][:, tile, :]).then_inc(stats_done, 1)
                dve.wait_ge(stats_done, NT)
                for tile in range(NT):
                    last = nc.vector.bn_aggr(mv[:, tile, :], st[:, tile, :])
                last.then_inc(aggr_done, 1)
                dve.wait_ge(rstd_done, 1)
                for tile in range(NT):
                    last = nc.vector.tensor_scalar(t["yacc"][:, tile, :], t["x"][:, tile, :], mv[:, tile, 0:1],
                                                   rstd[:, tile:tile + 1], ALU.subtract, ALU.mult)
                last.then_inc(xn_done, 1)
                dve.wait_ge(mod_ready, 1)
                nc.vector.tensor_copy(t["mod"][:, :, :, :, :], ps[:, 0, 0:96].rearrange(
                    "p (l c k b) -> p l c (k b)", l=2, c=6, k=KT).rearrange("p l c (k b) -> p l c k b", k=KT)
                    ).then_inc(mod_copied, 1)
                dve.wait_ge(mod_copied, 1)
                for l in range(2):
                    for c in (1, 4):
                        nc.vector.tensor_scalar(t["mod"][:, l, c], t["mod"][:, l, c], 1.0, None,
                                                ALU.add).then_inc(plus_one, 1)
                for l in range(2):
                    for j, c in enumerate((2, 5)):
                        g = t["mod"][:, l, c].rearrange("p k b -> p (k b)")
                        a = gneg[:, l, j].rearrange("p k b -> p (k b)")
                        s = gsign[:, l, j].rearrange("p k b -> p (k b)")
                        nc.vector.scalar_tensor_tensor(a, g, -1.0, g, ALU.mult, ALU.max).then_inc(gate_step, 1)
                        nc.vector.tensor_scalar(s, g, 0.0, 2.0, ALU.is_ge, ALU.mult).then_inc(gate_step, 1)
                dve.wait_ge(gate_step, 8)
                gn = gneg[:, :, :, :, :].rearrange("p l j k b -> p (l j k b)")
                gs = gsign[:, :, :, :, :].rearrange("p l j k b -> p (l j k b)")
                nc.vector.tensor_scalar(gn, gn, 0.25, None, ALU.max).then_inc(gate_step, 1)
                dve.wait_ge(gate_step, 9)
                nc.vector.scalar_tensor_tensor(gn, gs, -1.0, gn, ALU.add, ALU.mult).then_inc(gate_step, 1)
                dve.wait_ge(gate_step, 10)
                dve.wait_ge(const_ready, 1)
                gnb = gneg[:, :, :, :, :].rearrange("p l j k b -> p (l j) b k")
                nc.vector.tensor_copy(gpart[:, 0], gnb).then_inc(gate_parts, 1)
                dve.wait_ge(gate_parts, 1)
                nc.vector.tensor_tensor(gpart[:, 1], gnb, gpart[:, 0].bitcast(F32), ALU.subtract).then_inc(gate_parts, 1)
                dve.wait_ge(gate_parts, 2)
                for g in range(4):
                    for part in range(2):
                        last = nc.vector.tensor_tensor(
                            diag[:, g, part], t["ident"][:, :].unsqueeze(1).to_broadcast([P, B * KT, P]),
                            gpart[:, part, g].bitcast(F32).rearrange("p b k -> p (b k)").unsqueeze(2)
                            .to_broadcast([P, B * KT, P]), ALU.mult)
                    last.then_inc(diag_ready, 1)

            @block.tensor
            def _(pe):
                pe.wait_ge(silu_done, 1)
                for l in range(2):
                    pe.wait_ge(wmod_loaded[l], 16)
                    for c in range(6):
                        for f in range(KT):
                            at = ((l * 6 + c) * KT + f) * B
                            for k in range(KT):
                                last = nc.tensor.matmul(ps[:, 0, at:at + B], wmod[:, l, k, c * D + f * P:c * D + (f + 1) * P],
                                                        scond[:, l, k, :], start=(k == 0), stop=(k == KT - 1))
                last.then_inc(mod_ready, 1)
                pe.wait_ge(ones_ready, 1)
                for g in range(4):
                    pe.wait_ge(diag_ready, g + 1)
                    for half in range(2):
                        for part in range(2):
                            last = nc.tensor.matmul(ps[:, 2 * g + half, :], ones[:, :],
                                                    diag[:, g, part, half * B:(half + 1) * B, :].rearrange("p c n -> p (c n)"),
                                                    start=(part == 0), stop=(part == 1))
                    last.then_inc(gates_ready, 1)


def attention0_tasks():
    before = [("kt", 0), ("qt", 0), ("kt", 1), ("qt", 1)]
    scores = [[("s", g, tt, pr) for tt in range(TB) for pr in range(2)] for g in range(G0)] + [[]]
    order, late = list(before) + scores[0], []
    for g in range(G0):
        nxt = list(scores[g + 1])
        order += nxt[:2]
        nxt = nxt[2:]
        own = ([("q2", g)] + [("st", g, 0, j) for j in range(2)] + late + [("st", g, 0, 2), ("st", g, 0, 3)]
               + [("st", g, 1, 0), ("st", g, 1, 1), ("pv", g, 0), ("st", g, 1, 2), ("st", g, 1, 3)])
        late = [("pv", g, 1)]
        for n, task in enumerate(own):
            order.append(task)
            if n >= 1 and nxt:
                order.append(nxt.pop(0))
        order += nxt
    return order + late


def attention0_stage(nc, t, d):
    tasks = attention0_tasks()
    place = {task: n for n, task in enumerate(tasks)}
    assert len(tasks) % 4 == 0 and len(place) == len(tasks)
    turns = len(tasks) // 4
    x = t["x"]
    with ExitStack() as ctx:
        n = Names(nc, ctx, "attn0")
        NH = H0 + G0
        wo32 = n.sb("wo32", [P, KT, D], F32)
        wo = n.sb("wo", [P, KT, D], F16)
        bias32 = n.sb("bias32", [1, QKV0 + D], F32)
        bias = n.sb("bias", [1, QKV0 + D], F16)
        ones = n.sb("ones", [1, P], F16)
        qa = n.sb("qa", [P, NT, H0, SLOT], F16)
        ka = n.sb("ka", [P, NT * G0, R0, SLOT], F16)
        va = n.sb("va", [P, NT, G0, D0 + 1], F16)
        ao = n.sb("ao", [P, NT, H0, D0], F16)
        ps = n.psum()
        eps_rms = n.sb("eps_rms", [P, 1], F32)

        weights_loaded = n.sem("weights_loaded")
        tables_loaded = n.sem("tables_loaded")
        weights_cast, tables_ready, padding_set = n.sem("weights_cast"), n.sem("tables_ready"), n.sem("padding_set")
        slot_full = n.sems("slot_full", 4)
        ht_done, qkv_done = n.sem("ht_done"), n.sem("qkv_done")
        sq_done, ss_done, std_done, rrms_done = (n.sem(s) for s in ("sq_done", "ss_done", "std_done", "rrms_done"))
        qn_done, rot_done, q_roped, k_roped, k_spread, v_copied = (
            n.sem(s) for s in ("qn_done", "rot_done", "q_roped", "k_roped", "k_spread", "v_copied"))
        krot_done = n.sem("krot_done")
        kt_done, qt_done, top_done, shift_set, qt2_done = (
            n.sem(s) for s in ("kt_done", "qt_done", "top_done", "shift_set", "qt2_done"))
        exp_done, rden_done, ao_done, aot_done = (
            n.sem(s) for s in ("exp_done", "rden_done", "ao_done", "aot_done"))
        xn_turned, qkv_made, masked = n.sem("xn_turned"), n.sem("qkv_made"), n.sem("masked")
        ao_turned, out_made = n.sem("ao_turned"), n.sem("out_made")
        upd_done, x_done = n.sem("upd_done"), n.sem("x_done")
        pe_held, ones_set = n.sem("pe_held"), n.sem("ones_set")
        eps_set, pool_held = n.sem("eps_set"), n.sem("pool_held")

        def banks(task):
            s = place[task] % 4
            return ps[:, 2 * s:2 * s + 2, :]

        def banks16(task):
            return banks(task).rearrange("p a n -> p (a n)").bitcast(F16)

        def filled(eng, task, it):
            m = place[task]
            eng.wait_ge(slot_full[m % 4], it * turns + (m // 4 + 1))

        def emptied(eng, task, it):
            kind = task[0]
            if kind in ("kt", "qt"):
                eng.wait_ge({"kt": kt_done, "qt": qt_done}[kind], it * 2 + (task[1] + 1))
            elif kind == "s":
                _, g, tt, pr = task
                eng.wait_ge(top_done, it * 32 + (g * 8 + tt * 2 + pr + 1))
            elif kind == "q2":
                eng.wait_ge(qt2_done, it * G0 + (task[1] + 1))
            elif kind == "st":
                _, g, pr, j = task
                eng.wait_ge(exp_done, it * (8 * TB) + ((2 * g + pr) * TB + j + 1))
            else:
                _, g, pr = task
                eng.wait_ge(ao_done, it * 8 + (2 * g + pr + 1))

        with ExitStack() as ctx1:
            n1 = Names(nc, ctx1, "attn0p")
            wqkv32 = n1.sb("wqkv32", [P, KT, QKV0], F32)
            wqkv = n1.sb("wqkv", [P, KT, QKV0], F16)
            norm_scale = n1.sb("norm_scale", [P, 2, D0], F32)
            cosd = n1.sb("cosd", [P, TB, D0], F32)
            sind = n1.sb("sind", [P, TB, D0], F32)
            cos_t = n1.sb("cos_t", [P, TB, 2, D0], F32)
            sin_t = n1.sb("sin_t", [P, TB, 2, D0], F32)
            xn = t["yacc"]
            ht = n1.sb("ht", [P, KT, B * S], F16)
            qkv = n1.sb("qkv", [P, NT, QKV0], F16)
            sq = n1.sb("sq", [P, 2, TB, NH, D0], F32)
            ss = n1.sb("ss", [P, NT, NH], F32)
            qn = n1.sb("qn", [P, 2, TB, NH, D0], F32)
            rc_ = n1.sb("rope_cos", [P, 2, TB, NH, D0], F32)
            rs_ = n1.sb("rope_sin", [P, 2, TB, NH, D0], F32)
            kr = n1.sb("kr", [P, 2, TB, G0, D0], F16)
            eps_rms = n1.sb("eps_rms", [P, 1], F32)
            hd = D0 // 2

            with nc.Block() as block:

                @block.sync
                def _(sp):
                    sp.dma_start(wqkv32[:, :, :], d["wqkv0"]).then_inc(weights_loaded, 16)
                    sp.dma_start(wo32[:, :, :], d["wo0"]).then_inc(weights_loaded, 16)
                    sp.dma_start(bias32[:, :], d["bias0"]).then_inc(weights_loaded, 16)
                    sp.dma_start(norm_scale[:, :, :], d["norm_scale0"]).then_inc(tables_loaded, 16)
                    sp.dma_start(cosd[:, :, :], d["cosd"]).then_inc(tables_loaded, 16)
                    sp.dma_start(sind[:, :, :], d["sind"]).then_inc(tables_loaded, 16)

                @block.tensor
                def _(pe):
                    def turn(b):
                        if b >= 2:
                            pe.wait_ge(ht_done, (b - 1) * KT)
                        for k in range(KT):
                            for tt in range(TB):
                                last = nc.tensor.transpose(ps[:, (b % 2) * 2 + k, tt * P:(tt + 1) * P],
                                                           xn[:, b * TB + tt, k * P:(k + 1) * P], t["ident"][:, :])
                        last.then_inc(xn_turned, 1)

                    def project(b):
                        pe.wait_ge(ht_done, (b + 1) * KT)
                        for tt in range(TB):
                            if b and tt % 2 == 0:
                                pe.wait_ge(qkv_done, 2 * b - 1 + tt // 2)
                            cols = slice((b * TB + tt) * P, (b * TB + tt + 1) * P)
                            for k in range(KT):
                                nc.tensor.matmul(ps[:, 4 + tt, 0:QKV0], ht[:, k, cols], wqkv[:, k, :], start=(k == 0), stop=False)
                            last = nc.tensor.matmul(ps[:, 4 + tt, 0:QKV0], ones[0:1, :], bias[0:1, 0:QKV0],
                                                    start=False, stop=True)
                            if tt % 2:
                                last.then_inc(qkv_made, 1)

                    turn(0)
                    turn(1)
                    pe.wait_ge(weights_cast, 3)
                    pe.wait_ge(ones_set, 1)
                    for b in range(B):
                        project(b)
                        if b + 2 < B:
                            turn(b + 2)

                @block.scalar
                def _(act):
                    act.wait_ge(weights_loaded, 48)
                    nc.scalar.copy(wqkv[:, :, :], wqkv32[:, :, :]).then_inc(weights_cast, 1)
                    nc.scalar.copy(wo[:, :, :], wo32[:, :, :]).then_inc(weights_cast, 1)
                    nc.scalar.copy(bias[:, :], bias32[:, :]).then_inc(weights_cast, 1)

                    def shift_scale(b):
                        act.wait_ge(xn_turned, b + 1)
                        for k in range(KT):
                            nc.scalar.activation(ht[:, k, b * S:(b + 1) * S], ps[:, (b % 2) * 2 + k, :], ACT.Identity,
                                                 scale=t["mod"][:, 0, 1, k, b:b + 1],
                                                 bias=t["mod"][:, 0, 0, k, b:b + 1]).then_inc(ht_done, 1)

                    shift_scale(0)
                    for b in range(B):
                        if b + 1 < B:
                            shift_scale(b + 1)
                        for i in range(2):
                            act.wait_ge(qkv_made, 2 * b + i + 1)
                            nc.scalar.copy(qkv[:, b * TB + 2 * i:b * TB + 2 * i + 2, :],
                                           ps[:, 4 + 2 * i:6 + 2 * i, 0:QKV0]).then_inc(qkv_done, 1)
                    act.wait_ge(eps_set, 1)
                    act.wait_ge(ss_done, B)
                    nc.scalar.activation(ss[:, :, :], ss[:, :, :], ACT.Sqrt, bias=eps_rms[:, 0:1],
                                         scale=1.0 / D0).then_inc(std_done, 1)

                @block.vector
                def _(dve):
                    nc.vector.memset(eps_rms[:, :], EPS_RMS).then_inc(eps_set, 1)
                    for b in range(B):
                        rows = slice(b * TB, (b + 1) * TB)
                        dve.wait_ge(qkv_done, b * 2 + 2)
                        if b >= 2:
                            dve.wait_ge(ss_done, b - 1)
                        nc.vector.tensor_tensor(sq[:, b % 2].rearrange("p t h c -> p t (h c)"), qkv[:, rows, 0:NH * D0],
                                                qkv[:, rows, 0:NH * D0], ALU.mult).then_inc(sq_done, 1)
                        dve.wait_ge(sq_done, b + 1)
                        nc.vector.tensor_reduce(ss[:, rows, :], sq[:, b % 2], AX.X, ALU.add).then_inc(ss_done, 1)
                    dve.wait_ge(std_done, 1)
                    nc.vector.reciprocal(ss[:, :, :], ss[:, :, :]).then_inc(rrms_done, 1)
                    dve.wait_ge(rrms_done, 1)
                    dve.wait_ge(padding_set, 4)
                    dve.wait_ge(tables_ready, 2)
                    for b in range(B):
                        rows, s = slice(b * TB, (b + 1) * TB), b % 2
                        if b >= 2:
                            dve.wait_ge(q_roped, b - 1)
                            dve.wait_ge(krot_done, 2 * (b - 1))
                        nc.vector.tensor_tensor(qn[:, s].rearrange("p t h c -> p (t h) c"),
                                                qkv[:, rows, 0:NH * D0].rearrange("p t (h c) -> p t h c", c=D0),
                                                ss[:, rows, :].unsqueeze(3).to_broadcast([P, TB, NH, D0]),
                                                ALU.mult).then_inc(qn_done, 1)
                        dve.wait_ge(qn_done, b + 1)
                        q4 = [P, TB, H0, D0]
                        nc.vector.tensor_tensor(rc_[:, s, :, 0:H0, :], qn[:, s, :, 0:H0, :],
                                                cos_t[:, :, 0, :].unsqueeze(2).to_broadcast(q4), ALU.mult)
                        nc.vector.tensor_tensor(rs_[:, s, :, 0:H0, :], qn[:, s, :, 0:H0, :],
                                                sin_t[:, :, 0, :].unsqueeze(2).to_broadcast(q4), ALU.mult).then_inc(rot_done, 1)
                        dve.wait_ge(rot_done, b + 1)
                        nc.vector.tensor_tensor(qa[:, rows, :, 0:hd], rc_[:, s, :, 0:H0, 0:hd], rs_[:, s, :, 0:H0, hd:D0],
                                                ALU.subtract)
                        nc.vector.tensor_tensor(qa[:, rows, :, hd:D0], rc_[:, s, :, 0:H0, hd:D0], rs_[:, s, :, 0:H0, 0:hd],
                                                ALU.add).then_inc(q_roped, 1)

                @block.gpsimd
                def _(pool):
                    nc.gpsimd.memset(ones[:, :], 1.0).then_inc(ones_set, 1)
                    nc.gpsimd.memset(qa[:, :, :, :], 0.0).then_inc(padding_set, 1)
                    nc.gpsimd.memset(ka[:, :, :, :], 0.0).then_inc(padding_set, 1)
                    nc.gpsimd.memset(va[:, :, :, :], 1.0).then_inc(padding_set, 1)
                    pool.wait_ge(padding_set, 3)
                    nc.gpsimd.memset(ka[:, :, :, D0:D0 + 1], SHIFT).then_inc(padding_set, 1)
                    pool.wait_ge(tables_loaded, 48)
                    nc.gpsimd.tensor_scalar(norm_scale[:, 0, :], norm_scale[:, 0, :], D0 ** -0.5, None,
                                            ALU.mult).then_inc(tables_ready, 1)
                    pool.wait_ge(tables_ready, 1)
                    for which in range(2):
                        sc = norm_scale[:, which, :].unsqueeze(1).to_broadcast([P, TB, D0])
                        nc.gpsimd.tensor_tensor(cos_t[:, :, which, :], cosd[:, :, :], sc, ALU.mult)
                        last = nc.gpsimd.tensor_tensor(sin_t[:, :, which, :], sind[:, :, :], sc, ALU.mult)
                    last.then_inc(tables_ready, 1)
                    pool.wait_ge(tables_ready, 2)
                    pool.wait_ge(qkv_done, 2 * B)
                    nc.gpsimd.tensor_copy(va[:, :, :, 0:D0], qkv[:, :, NH * D0:QKV0].rearrange(
                        "p t (g c) -> p t g c", c=D0)).then_inc(v_copied, 1)
                    for b in range(B):
                        rows, s, k4 = slice(b * TB, (b + 1) * TB), b % 2, [P, TB, G0, D0]
                        pool.wait_ge(qn_done, b + 1)
                        nc.gpsimd.tensor_tensor(rc_[:, s, :, H0:NH, :], qn[:, s, :, H0:NH, :],
                                                cos_t[:, :, 1, :].unsqueeze(2).to_broadcast(k4), ALU.mult).then_inc(krot_done, 1)
                        nc.gpsimd.tensor_tensor(rs_[:, s, :, H0:NH, :], qn[:, s, :, H0:NH, :],
                                                sin_t[:, :, 1, :].unsqueeze(2).to_broadcast(k4), ALU.mult).then_inc(krot_done, 1)
                        pool.wait_ge(krot_done, b * 2 + 2)
                        nc.gpsimd.tensor_tensor(kr[:, s, :, :, 0:hd], rc_[:, s, :, H0:NH, 0:hd], rs_[:, s, :, H0:NH, hd:D0],
                                                ALU.subtract).then_inc(k_roped, 1)
                        nc.gpsimd.tensor_tensor(kr[:, s, :, :, hd:D0], rc_[:, s, :, H0:NH, hd:D0], rs_[:, s, :, H0:NH, 0:hd],
                                                ALU.add).then_inc(k_roped, 1)
                        pool.wait_ge(k_roped, b * 2 + 2)
                        nc.gpsimd.tensor_copy(ka[:, b * TB * G0:(b + 1) * TB * G0, :, 0:D0],
                                              kr[:, s].rearrange("p t g c -> p (t g) c").unsqueeze(2)
                                              .to_broadcast([P, TB * G0, R0, D0])).then_inc(k_spread, 1)

        qt = n.sb("qt", [P, G0, S], F16)
        qt2 = n.sb("qt2", [P, G0, S], F16)
        kt = n.sb("kt", [P, G0, S], F16)
        top = n.sb("top", [P, TB, H0], F32)
        probs = n.sb("probs", [P, 2, TB, 2, S], F16)
        rden = n.sb("rden", [P, 2, TB, 2], F32)
        aot = n.sb("aot", [P, KT, B * S], F16)
        upd = n.sb("upd", [P, NT, D], F32)

        with nc.Block() as block:

            @block.tensor
            def _(pe):
                def batch(it, first):
                    for m, task in enumerate(tasks):
                        kind, out = task[0], banks(task)
                        if m >= 4:
                            emptied(pe, tasks[m - 4], it)
                        elif not first:
                            emptied(pe, tasks[m - 4], it - 1)
                        if kind in ("kt", "qt"):
                            pe.sem_inc(pe_held, 1)
                            o = banks16(task)
                            for i in range(2):
                                g = 2 * task[1] + i
                                for tt in range(TB):
                                    tile = it * TB + tt
                                    src = (ka[:, at(tile * G0 + g)].rearrange("p a r c -> p (a r c)") if kind == "kt" else
                                           qa[:, at(tile), R0 * g:R0 * (g + 1)].rearrange("p a r c -> p (a r c)"))
                                    last = nc.tensor.transpose(o[:, i * S + tt * P:i * S + (tt + 1) * P], src,
                                                               t["ident16"][:, :])
                        elif kind == "s":
                            _, g, tt, pr = task
                            if (tt, pr) == (0, 0):
                                pe.wait_ge(kt_done, it * 2 + (g // 2 + 1))
                                pe.wait_ge(qt_done, it * 2 + (g // 2 + 1))
                            for h in range(2):
                                r = SLOT * (2 * pr + h)
                                nc.tensor.matmul(out[:, h, 0:(tt + 1) * P], qt[r:r + D0, g, tt * P:(tt + 1) * P],
                                                 kt[r:r + D0, g, 0:(tt + 1) * P], start=True, stop=False)
                            for h in range(2):
                                last = nc.tensor.matmul(out[:, h, tt * P:(tt + 1) * P], t["identb"][:, :],
                                                        t["later_key"][:, :], start=False, stop=True)
                        elif kind == "q2":
                            g = task[1]
                            pe.wait_ge(shift_set, it * G0 + (g + 1))
                            pe.sem_inc(pe_held, 1)
                            o = banks16(task)
                            for tt in range(TB):
                                last = nc.tensor.transpose(o[:, tt * P:(tt + 1) * P],
                                                           qa[:, at(it * TB + tt), R0 * g:R0 * (g + 1)].rearrange(
                                                               "p a r c -> p (a r c)"),
                                                           t["ident16"][:, :])
                        elif kind == "st":
                            _, g, pr, j = task
                            if (pr, j) == (0, 0):
                                pe.wait_ge(qt2_done, it * G0 + (g + 1))
                            for h in range(2):
                                r = SLOT * (2 * pr + h)
                                last = nc.tensor.matmul(out[:, h, 0:S - j * P], kt[r:r + D0 + 1, g, j * P:(j + 1) * P],
                                                        qt2[r:r + D0 + 1, g, j * P:S], start=True, stop=True)
                        else:
                            _, g, pr = task
                            pe.wait_ge(masked, it * 8 + (2 * g + pr + 1))
                            for tt in range(TB):
                                for h in range(2):
                                    o = out[:, 0, (tt * 2 + h) * (D0 + 1):(tt * 2 + h + 1) * (D0 + 1)]
                                    for j in range(tt + 1):
                                        last = nc.tensor.matmul(o, probs[:, pr, j, h, (tt - j) * P:(tt - j + 1) * P],
                                                                va[:, at(it * TB + j), g, :].rearrange("p a c -> p (a c)"),
                                                                start=(j == 0), stop=(j == tt))
                        last.then_inc(slot_full[m % 4], 1)

                batch(0, True)
                with pe.Fori(1, B) as it:
                    batch(it, False)

                def turn(b):
                    o = ps[:, b % 4, :].bitcast(F16)
                    for k in range(KT):
                        for tt in range(TB):
                            last = nc.tensor.transpose(o[:, k * S + tt * P:k * S + (tt + 1) * P],
                                                       ao[:, b * TB + tt, k * 8:(k + 1) * 8].rearrange("p h c -> p (h c)"),
                                                       t["ident16"][:, :])
                    last.then_inc(ao_turned, 1)

                pe.wait_ge(ao_done, B * 8)
                for b in range(B):
                    turn(b)
                for b in range(B):
                    pe.wait_ge(aot_done, b + 1)
                    for tt in range(TB):
                        if b and tt % 2 == 0:
                            pe.wait_ge(upd_done, 2 * b - 1 + tt // 2)
                        out = ps[:, 4 + tt, 0:D]
                        for k in range(KT):
                            nc.tensor.matmul(out, aot[:, k, (b * TB + tt) * P:(b * TB + tt + 1) * P], wo[:, k, :],
                                             start=(k == 0), stop=False)
                        last = nc.tensor.matmul(out, ones[0:1, :], bias[0:1, QKV0:QKV0 + D], start=False, stop=True)
                        if tt % 2:
                            last.then_inc(out_made, 1)

            @block.scalar
            def _(act):
                with act.Fori(0, B) as it:
                    for task in tasks:
                        if task[0] == "st":
                            _, g, pr, j = task
                            filled(act, task, it)
                            if j == 0 and g:
                                filled(act, ("pv", g - 1, pr), it)
                            nc.scalar.activation(probs[:, pr, j, :, 0:S - j * P], banks(task)[:, :, 0:S - j * P],
                                                 ACT.Exp, scale=D0 ** -0.5).then_inc(exp_done, 1)

                for b in range(B):
                    act.wait_ge(ao_turned, b + 1)
                    nc.scalar.copy(aot[:, :, b * S:(b + 1) * S],
                                   ps[:, b % 4, :].bitcast(F16).rearrange("p (k n) -> p k n", k=KT)).then_inc(aot_done, 1)

            @block.vector
            def _(dve):
                with dve.Fori(0, B) as it:
                    for task in tasks:
                        kind = task[0]
                        if kind not in ("kt", "qt", "s", "q2", "pv"):
                            continue
                        filled(dve, task, it)
                        if kind in ("kt", "qt"):
                            dst, done = (kt, kt_done) if kind == "kt" else (qt, qt_done)
                            g = 2 * task[1]
                            nc.vector.tensor_copy(dst[:, g:g + 2, :].rearrange("p g n -> p (g n)"),
                                                  banks16(task)[:, 0:2 * S]).then_inc(done, 1)
                        elif kind == "s":
                            _, g, tt, pr = task
                            h = R0 * g + 2 * pr
                            nc.vector.tensor_reduce(top[:, tt, h:h + 2], banks(task)[:, :, 0:(tt + 1) * P], AX.X,
                                                    ALU.max).then_inc(top_done, 1)
                            if (tt, pr) == (TB - 1, 1):
                                dve.wait_ge(top_done, it * 32 + (g * 8 + tt * 2 + pr + 1))
                                nc.vector.tensor_scalar(qa[:, at(it * TB, TB), R0 * g:R0 * (g + 1), D0], top[:, :, R0 * g:R0 * (g + 1)],
                                                        -1.0 / SHIFT, None, ALU.mult).then_inc(shift_set, 1)
                        elif kind == "q2":
                            g = task[1]
                            nc.vector.tensor_copy(qt2[:, g, :], banks16(task)[:, 0:S]).then_inc(qt2_done, 1)
                        else:
                            _, g, pr = task
                            o = banks(task)[:, 0, 0:8 * (D0 + 1)].rearrange("p (t h c) -> p t h c", h=2, c=D0 + 1)
                            nc.vector.reciprocal(rden[:, pr, :, :], o[:, :, :, D0]).then_inc(rden_done, 1)
                            dve.wait_ge(rden_done, it * 8 + (2 * g + pr + 1))
                            h = R0 * g + 2 * pr
                            nc.vector.tensor_tensor(ao[:, at(it * TB, TB), h:h + 2, :], o[:, :, :, 0:D0],
                                                    rden[:, pr, :, :].unsqueeze(3).to_broadcast([P, TB, 2, D0]),
                                                    ALU.mult).then_inc(ao_done, 1)
                for b in range(B):
                    for i in range(2):
                        dve.wait_ge(out_made, 2 * b + i + 1)
                        nc.vector.tensor_tensor(upd[:, b * TB + 2 * i:b * TB + 2 * i + 2, :], ps[:, 4 + 2 * i:6 + 2 * i, 0:D],
                                                t["gate"][:, 0, b:b + 1, :].to_broadcast([P, 2, D]),
                                                ALU.mult).then_inc(upd_done, 1)

            @block.gpsimd
            def _(pool):
                with pool.Fori(0, B) as it:
                    for g in range(G0):
                        for pr in range(2):
                            pool.wait_ge(exp_done, it * (8 * TB) + (2 * g + pr + 1) * TB)
                            pool.sem_inc(pool_held, 1)
                            tri = probs[:, pr, :, :, 0:P]
                            nc.gpsimd.affine_select(out=tri, in_=tri, compare_op=ALU.is_ge, fill=0.0, base=0,
                                                    pattern=[[0, TB], [0, 2], [1, P]], channel_multiplier=-1
                                                    ).then_inc(masked, 1)
                for b in range(B):
                    pool.wait_ge(upd_done, 2 * b + 2)
                    xs = x[:, b * TB:(b + 1) * TB, :]
                    nc.gpsimd.tensor_tensor(xs, xs, upd[:, b * TB:(b + 1) * TB, :], ALU.add).then_inc(x_done, 1)


class SplitNorm:

    def __init__(self, n, tag, layer, shift_part, parts, xn, psum_slot):
        self.layer, self.shift_part, self.parts, self.xn, self.slot = layer, shift_part, parts, xn, psum_slot
        self.st = n.sb(f"{tag}_st", [P, NT, 6], F32)
        self.mv = n.sb(f"{tag}_mv", [P, NT, 2], F32)
        self.rstd = n.sb(f"{tag}_rstd", [P, NT], F32)
        self.ht = n.sb(f"{tag}_ht", [P, KT, S], F32)
        self.stats_done, self.aggr_done = n.sem(f"{tag}_stats_done"), n.sem(f"{tag}_aggr_done")
        self.var_eps, self.rstd_done = n.sem(f"{tag}_var_eps"), n.sem(f"{tag}_rstd_done")
        self.xn_done, self.turned = n.sem(f"{tag}_xn_done"), n.sem(f"{tag}_turned")
        self.ht_done, self.high_done = n.sem(f"{tag}_ht_done"), n.sem(f"{tag}_high_done")
        self.low_done = n.sem(f"{tag}_low_done")

    def vector_stats(self, nc, x, it):
        for tt in range(TB):
            nc.vector.bn_stats(self.st[:, at(it * TB + tt), :], x[:, at(it * TB + tt), :]).then_inc(self.stats_done, 1)

    def vector_aggregate(self, nc, dve):
        dve.wait_ge(self.stats_done, NT)
        for tile in range(NT):
            last = nc.vector.bn_aggr(self.mv[:, tile, :], self.st[:, tile, :])
        last.then_inc(self.aggr_done, 1)

    def pool_rstd(self, nc, pool, t):
        pool.wait_ge(self.aggr_done, 1)
        nc.gpsimd.tensor_scalar(self.rstd[:, :], self.mv[:, :, 1], EPS_LN, None, ALU.add).then_inc(self.var_eps, 1)
        pool.wait_ge(self.var_eps, 1)
        nc.gpsimd.tensor_tensor(self.rstd[:, :], self.rstd[:, :], t["neg_half"][:, :], ALU.pow).then_inc(self.rstd_done, 1)

    def vector_norm(self, nc, dve, x):
        dve.wait_ge(self.rstd_done, 1)
        for tile in range(NT):
            last = nc.vector.tensor_scalar(self.xn[:, tile, :], x[:, tile, :], self.mv[:, tile, 0:1],
                                           self.rstd[:, tile:tile + 1], ALU.subtract, ALU.mult)
            if tile % TB == TB - 1:
                last.then_inc(self.xn_done, 1)

    def tensor_turn(self, nc, pe, t, ps, b):
        pe.wait_ge(self.xn_done, b + 1)
        if b:
            pe.wait_ge(self.ht_done, b * KT)
        for k in range(KT):
            for tt in range(TB):
                last = nc.tensor.transpose(ps[:, self.slot + k, tt * P:(tt + 1) * P],
                                           self.xn[:, b * TB + tt, k * P:(k + 1) * P], t["ident"][:, :])
        last.then_inc(self.turned, 1)

    def scalar_high(self, nc, act, t, ps, b):
        act.wait_ge(self.turned, b + 1)
        if b:
            act.wait_ge(self.low_done, b)
        for k in range(KT):
            nc.scalar.activation(self.ht[:, k, :], ps[:, self.slot + k, :], ACT.Identity,
                                 scale=t["mod"][:, self.layer, self.shift_part + 1, k, b:b + 1],
                                 bias=t["mod"][:, self.layer, self.shift_part, k, b:b + 1]).then_inc(self.ht_done, 1)
        act.wait_ge(self.ht_done, b * KT + KT)
        nc.scalar.copy(self.parts[:, 0, :, b * S:(b + 1) * S], self.ht[:, :, :]).then_inc(self.high_done, 1)

    def vector_low(self, nc, dve, b):
        dve.wait_ge(self.high_done, b + 1)
        cols = slice(b * S, (b + 1) * S)
        nc.vector.tensor_tensor(self.parts[:, 1, :, cols], self.ht[:, :, :], self.parts[:, 0, :, cols].bitcast(F32),
                                ALU.subtract).then_inc(self.low_done, 1)


def ffn0_stage(nc, t, d):
    x = t["x"]
    with ExitStack() as ctx:
        n = Names(nc, ctx, "ffn0")
        hp = t["h_parts"]
        wraw = n.sb("wraw", [P, KT, D], F32)
        rows = n.sb("rows", [P, 2, D], F32)
        w = n.sb("w", [P, KT, D], F32)
        wp = n.sb("wp", [P, 2, KT, D], F32R)
        gbias = n.sb("gbias", [P, B, D], F32)
        upd = n.sb("upd", [P, NT, D], F32)
        ps = n.psum()
        norm_a = SplitNorm(n, "a", 0, 3, hp, t["yacc"], 0)
        norm_b = SplitNorm(n, "b", 1, 0, hp, n.sb("xn", [P, NT, D], F32), 2)
        loaded, w_scaled, w_high, w_ready = n.sem("loaded"), n.sem("w_scaled"), n.sem("w_high"), n.sem("w_ready")
        gbias_ready = n.sem("gbias_ready")
        made, upd_done, x_done, bias_added = n.sem("made"), n.sem("upd_done"), n.sem("x_done"), n.sem("bias_added")
        x_by_dve = n.sem("x_by_dve")
        OUT = 4

        with nc.Block() as block:

            @block.sync
            def _(sp):
                sp.dma_start(wraw[:, :, :], d["wffn"]).then_inc(loaded, 16)
                sp.dma_start(rows[:, :, :], d["ffn_rows"]).then_inc(loaded, 16)

            @block.tensor
            def _(pe):
                norm_a.tensor_turn(nc, pe, t, ps, 0)
                pe.wait_ge(w_ready, 1)
                for b in range(B):
                    if b + 1 < B:
                        norm_a.tensor_turn(nc, pe, t, ps, b + 1)
                    pe.wait_ge(norm_a.low_done, b + 1)
                    for tt in range(TB):
                        if tt % 2 == 0 and b:
                            pe.wait_ge(upd_done, 2 * b - 1 + tt // 2)
                        for m, (k, (a, c)) in enumerate([(k, tc) for k in range(KT) for tc in TERMS]):
                            last = nc.tensor.matmul(ps[:, OUT + tt // 2, (tt % 2) * D:(tt % 2 + 1) * D],
                                                    hp[:, a, k, b * S + tt * P:b * S + (tt + 1) * P], wp[:, c, k, :],
                                                    start=(m == 0), stop=(m == 5))
                        if tt % 2:
                            last.then_inc(made, 1)
                for b in range(B):
                    norm_b.tensor_turn(nc, pe, t, ps, b)

            @block.scalar
            def _(act):
                act.wait_ge(w_scaled, 1)
                nc.scalar.copy(wp[:, 0], w[:, :, :]).then_inc(w_high, 1)
                for b in range(B):
                    norm_a.scalar_high(nc, act, t, ps, b)
                act.wait_ge(made, 2 * B)
                for b in range(B):
                    norm_b.scalar_high(nc, act, t, ps, b)

            @block.vector
            def _(dve):
                for b in range(B):
                    norm_a.vector_stats(nc, x, b)
                norm_a.vector_aggregate(nc, dve)
                dve.wait_ge(loaded, 32)
                nc.vector.tensor_tensor(w[:, :, :], wraw[:, :, :], rows[:, 0:1, :].to_broadcast([P, KT, D]),
                                        ALU.mult).then_inc(w_scaled, 1)
                dve.wait_ge(w_high, 1)
                nc.vector.tensor_tensor(wp[:, 1], w[:, :, :], wp[:, 0].bitcast(F32), ALU.subtract).then_inc(w_ready, 1)
                norm_a.vector_norm(nc, dve, x)

                def update(b):
                    for i in range(2):
                        dve.wait_ge(made, b * 2 + (i + 1))
                        nc.vector.tensor_tensor(upd[:, b * TB + 2 * i:b * TB + 2 * i + 2, :],
                                                ps[:, OUT + i, :].rearrange("p (t n) -> p t n", t=2),
                                                t["gate"][:, 1, b:b + 1, :].to_broadcast([P, 2, D]),
                                                ALU.mult).then_inc(upd_done, 1)

                for b in range(B):
                    norm_a.vector_low(nc, dve, b)
                    if b:
                        update(b - 1)
                update(B - 1)
                for b in (1, 3):
                    dve.wait_ge(bias_added, b + 1)
                    dve.wait_ge(upd_done, 2 * b + 2)
                    rows_b = slice(b * TB, (b + 1) * TB)
                    nc.vector.tensor_tensor(x[:, rows_b, :], x[:, rows_b, :], upd[:, rows_b, :], ALU.add).then_inc(x_by_dve, 1)
                dve.wait_ge(x_by_dve, 2)
                for b in (1, 3, 0, 2):
                    if b % 2 == 0:
                        dve.wait_ge(x_done, b // 2 + 1)
                    norm_b.vector_stats(nc, x, b)
                norm_b.vector_aggregate(nc, dve)
                norm_b.vector_norm(nc, dve, x)
                for b in range(B):
                    norm_b.vector_low(nc, dve, b)

            @block.gpsimd
            def _(pool):
                norm_a.pool_rstd(nc, pool, t)
                pool.wait_ge(loaded, 32)
                nc.gpsimd.tensor_tensor(gbias[:, :, :], t["gate"][:, 1], rows[:, 1:2, :].to_broadcast([P, B, D]),
                                        ALU.mult).then_inc(gbias_ready, 1)
                pool.wait_ge(gbias_ready, 1)
                for b in range(B):
                    pool.wait_ge(norm_a.xn_done, b + 1)
                    xb = x[:, b * TB:(b + 1) * TB, :]
                    nc.gpsimd.tensor_tensor(xb, xb, gbias[:, b:b + 1, :].to_broadcast([P, TB, D]),
                                            ALU.add).then_inc(bias_added, 1)
                for b in (0, 2):
                    pool.wait_ge(bias_added, b + 1)
                    pool.wait_ge(upd_done, b * 2 + 2)
                    xb = x[:, b * TB:(b + 1) * TB, :]
                    nc.gpsimd.tensor_tensor(xb, xb, upd[:, b * TB:(b + 1) * TB, :], ALU.add).then_inc(x_done, 1)
                norm_b.pool_rstd(nc, pool, t)


TERMS = ((0, 0), (0, 1), (1, 0))


def attention1_order():
    order = []
    for u in range(UNITS):
        other = "v" if u % 2 == 0 else "y"
        order += [("s", u, 0), ("k", u), ("pv", u, 0), ("s", u, 1), ("q", u), ("pv", u, 1), ("s", u, 2), (other, u, 0),
                  ("s", u, 3), ("pv", u, 2), (other, u, 1), ("g", u), ("pv", u, 3)]
    return order


def attention1_stage(nc, t, d):
    order = attention1_order()
    ring_tasks = [task for task in order if task[0] in "sqkgv"]
    first_tasks = [("k", -1), ("q", -1)]
    RING, AHEAD = 4, len(first_tasks)
    place = {task: n + AHEAD for n, task in enumerate(ring_tasks)} | {task: n for n, task in enumerate(first_tasks)}
    assert len(ring_tasks) % RING == 0
    unmade = [("q", UNITS - 1), ("k", UNITS - 1)]
    turns = len(ring_tasks) // RING
    NB = S // P
    OFF = [sum(S - i * P for i in range(j)) for j in range(NB)]
    NP = sum(S - j * P for j in range(NB))
    hh = t["h_parts"]
    with ExitStack() as ctx:
        n = Names(nc, ctx, "attn1")
        wraw = n.sb("wraw", [P, KT, 8 * P], F32)
        wp = n.sb("wp", [P, 2, KT, 8 * P], F32R)
        woraw = n.sb("woraw", [P, 2, D], F32)
        wop = n.sb("wop", [P, 2, 2, D], F32R)
        normw = n.sb("normw", [P, H1], F32)
        mask = n.sb("mask", [P, 2, S], F32)
        qk = n.sb("qk", [P, 2, S], F32)
        qkp = n.sb("qkp", [P, 2, 2, 2, S], F32R)
        v = n.sb("v", [P, TB, 2 * P], F32)
        vp = n.sb("vp", [P, 2, 2, TB, 2 * P], F32R)
        gate = n.sb("gate", [P, 2, S], F32)
        p = n.sb("p", [P, NP], F32)
        pp = n.sb("pp", [P, 2, 2, NP], F32R)
        y = n.sb("y", [P, 2, S], F32)
        yp = n.sb("yp", [P, 2, 2, S], F32R)
        sq = n.sb("sq", [P, 2, S], F32)
        ssq = t["gate"][:, 0:2].rearrange("p l b n -> p (l b n)")
        ones = n.sb("ones", [P, 1], F32)
        yacc, rms = t["yacc"], t["rms"]
        ps = n.psum()
        O_BANK, Y_BANK = 4, 6

        ring_full = n.sems("ring_full", RING)
        w_loaded, wo_loaded, mask_loaded = n.sem("w_loaded"), n.sem("wo_loaded"), n.sems("mask_loaded", 2)
        w_hi, w_ready = n.sems("w_hi", 3), n.sems("w_ready", 3)
        norm_loaded, norm_halved = n.sem("norm_loaded"), n.sem("norm_halved")
        wo_scaled, wo_hi, wo_ready = n.sem("wo_scaled"), n.sem("wo_hi"), n.sem("wo_ready")
        q_silu, q_hi, q_ready = n.sem("q_silu"), n.sem("q_hi"), n.sem("q_ready")
        k_silu, k_hi, k_ready = n.sem("k_silu"), n.sem("k_hi"), n.sem("k_ready")
        v_silu, v_hi, v_ready = n.sem("v_silu"), n.sem("v_hi"), n.sem("v_ready")
        gate_done = n.sem("gate_done")
        p_masked, p_hi, p_ready = n.sem("p_masked"), n.sem("p_hi"), n.sem("p_ready")
        o_full, gated, y_hi, y_ready = n.sem("o_full"), n.sem("gated"), n.sem("y_hi"), n.sem("y_ready")
        squared, summed = n.sem("squared"), n.sem("summed")
        y_full, y_added = n.sem("y_full"), n.sem("y_added")
        zeroed, ssq_full, mean_done, rms_done = n.sem("zeroed"), n.sem("ssq_full"), n.sem("mean_done"), n.sem("rms_done")

        def bank(task):
            return ps[:, place[task] % RING, :]

        def filled(eng, task, it):
            m = place[task]
            i = ring_tasks.index(task) - RING if task in ring_tasks else -1
            missing = 1 if isinstance(it, int) and it == PAIRS - 1 and i >= 0 and ring_tasks[i] in unmade else 0
            eng.wait_ge(ring_full[m % RING], it * turns + (m // RING + 1 - missing))

        def emptied(eng, task, it):
            kind, u = task[0], task[1]
            if kind == "s":
                eng.wait_ge(p_masked, it * (UNITS * NB) + (u * NB + task[2] + 1))
            elif kind == "v":
                eng.wait_ge(v_silu, it * (2 * B) + (u + task[2] + 1))
            elif kind == "g":
                eng.wait_ge(gate_done, it * UNITS + (u + 1))
            else:
                eng.wait_ge({"q": q_silu, "k": k_silu}[kind], it * UNITS + (u + 2))

        PART = (slice(0, 2 * P), slice(2 * P, 7 * P), slice(7 * P, 8 * P))
        COLUMN = {("q", 0): 0, ("k", 0): P, ("q", 1): 2 * P, ("k", 1): 3 * P, ("g", 0): 4 * P, ("v", 0): 5 * P,
                  ("g", 1): 7 * P}

        def late(it, u, units):
            return not isinstance(it, int) or it * UNITS + u >= units

        def over_pairs(eng, body):
            body(0, True, False)
            with eng.Fori(1, PAIRS - 1) as it:
                body(it, False, False)
            body(PAIRS - 1, False, True)

        with nc.Block() as block:

            @block.sync
            def _(sp):
                sp.dma_start(wraw[:, :, :], d["w1p"][0]).then_inc(w_loaded, 16)
                sp.dma_start(normw[:, :], d["norm_w"]).then_inc(norm_loaded, 16)
                for h in range(2):
                    sp.dma_start(mask[:, h, :], t["decay_dram"][h]).then_inc(mask_loaded[h], 16)
                sp.dma_start(woraw[:, :, :], d["wout"][0]).then_inc(wo_loaded, 16)
                with sp.Fori(0, PAIRS - 1) as it:
                    sp.wait_ge(w_ready[2], it + 1)
                    sp.dma_start(wraw[:, :, :], d["w1p"][bass.ds(it + 1, 1)].rearrange("a p k n -> (a p) k n")
                                 ).then_inc(w_loaded, 16)
                    sp.wait_ge(wo_ready, it + 1)
                    sp.dma_start(woraw[:, :, :], d["wout"][bass.ds(it + 1, 1)].rearrange("a p k n -> (a p) k n")
                                 ).then_inc(wo_loaded, 16)
                    for h in range(2):
                        sp.wait_ge(p_masked, it * (UNITS * NB) + (UNITS - 1 + h) * NB)
                        sp.dma_start(mask[:, h, :], t["decay_dram"][bass.ds(it * 2 + (2 + h), 1)].rearrange(
                            "a p n -> (a p) n")).then_inc(mask_loaded[h], 16)

            @block.tensor
            def _(pe):
                def project(task, it):
                    kind, u = task[0], task[1]
                    unit = u + 1 if kind in "qk" else u
                    pair, unit = it + unit // UNITS, unit % UNITS
                    b, h = unit // 2, unit % 2
                    out = bank(task)
                    if kind == "k" and b == 0:
                        pe.wait_ge(w_ready[h], pair + 1)
                    if kind == "v" and b == 0 or kind == "g" and unit == 0:
                        pe.wait_ge(w_ready[1], pair + 1)
                    if kind == "g" and unit == 1:
                        pe.wait_ge(w_ready[2], pair + 1)
                    terms = [(k, tc) for k in range(KT) for tc in TERMS]
                    if kind == "v":
                        col = COLUMN[kind, 0]
                        for i in range(2):
                            tt = b * TB + 2 * task[2] + i
                            for m, (k, (a, c)) in enumerate(terms):
                                last = nc.tensor.matmul(out[:, i * 2 * P:(i + 1) * 2 * P], hh[:, a, k, tt * P:(tt + 1) * P],
                                                        wp[:, c, k, col:col + 2 * P], start=(m == 0), stop=(m == 5))
                    else:
                        col = COLUMN[kind, h]
                        for m, (k, (a, c)) in enumerate(terms):
                            last = nc.tensor.matmul(out, wp[:, a, k, col:col + P], hh[:, c, k, b * S:(b + 1) * S],
                                                    start=(m == 0), stop=(m == 5))
                    last.then_inc(ring_full[place[task] % RING], 1)

                def output(task):
                    i = task[2]
                    for half in range(2):
                        tt = 2 * i + half
                        for m, (h, (a, c)) in enumerate([(h, tc) for h in range(2) for tc in TERMS]):
                            last = nc.tensor.matmul(ps[:, Y_BANK + i, half * D:(half + 1) * D],
                                                    yp[:, a, h, tt * P:(tt + 1) * P], wop[:, c, h, :],
                                                    start=(m == 0), stop=(m == 5))
                    last.then_inc(y_full, 1)

                def values(j, u, it):
                    b, h = (u % UNITS) // 2, u % 2
                    if j == 0:
                        if late(it, u, 2):
                            pe.wait_ge(squared, it * UNITS + (u - 1))
                        if h == 0:
                            pe.wait_ge(v_ready, it * (2 * B) + (u + 2))
                    pe.wait_ge(p_ready, it * (UNITS * NB) + (u * NB + j + 1))
                    for m3, (a, c) in enumerate(TERMS):
                        last = nc.tensor.matmul(ps[:, O_BANK + h, j * P:S], vp[:, b % 2, a, j, h * P:(h + 1) * P],
                                                pp[:, h, c, OFF[j]:OFF[j] + S - j * P],
                                                start=(j == 0 and m3 == 0), stop=(j == NB - 1 and m3 == 2))
                    if j == NB - 1:
                        last.then_inc(o_full, 1)

                def body(it, first, last_pair):
                    for task in order:
                        kind, u = task[0], task[1]
                        b, h = u // 2, u % 2
                        if kind in "sqkgv":
                            if kind in "qk" and u == UNITS - 1 and last_pair:
                                continue
                            m = place[task]
                            i = ring_tasks.index(task) - RING
                            if last_pair and i >= 0 and ring_tasks[i] in unmade:
                                i -= RING
                            if i >= 0:
                                emptied(pe, ring_tasks[i], it)
                            elif not first:
                                emptied(pe, ring_tasks[i], it - 1)
                            elif i >= -AHEAD:
                                emptied(pe, first_tasks[i], 0)
                            if kind != "s":
                                project(task, it)
                                continue
                            j = task[2]
                            if j == 0:
                                pe.wait_ge(k_ready, it * UNITS + (u + 1))
                                pe.wait_ge(q_ready, it * UNITS + (u + 1))
                            for m3, (a, c) in enumerate(TERMS):
                                last = nc.tensor.matmul(bank(task)[:, 0:S - j * P], qkp[:, h, a, 1, j * P:(j + 1) * P],
                                                        qkp[:, h, c, 0, j * P:S], start=(m3 == 0), stop=(m3 == 2))
                            last.then_inc(ring_full[m % RING], 1)
                        elif kind == "pv":
                            if late(it, u, 1):
                                values(task[2], u - 1, it)
                        elif late(it, u, 3):
                            if task[2] == 0:
                                pe.wait_ge(y_ready, it * UNITS + (u - 1))
                                if u == 3:
                                    pe.wait_ge(wo_ready, it + 1)
                                if late(it, u, 5):
                                    pe.wait_ge(y_added, it * (2 * B) + (u - 3))
                            output(task)

                for task in first_tasks:
                    project(task, 0)
                over_pairs(pe, body)
                for j in range(NB):
                    values(j, UNITS - 1, PAIRS - 1)
                pe.wait_ge(y_ready, PAIRS * UNITS)
                pe.wait_ge(y_added, PAIRS * 2 * B - 2)
                for i in range(2):
                    output(("y", 1, i))
                pe.wait_ge(summed, PAIRS * UNITS)
                for tt in range(NT):
                    last = nc.tensor.matmul(ps[:, 0, tt:tt + 1], ssq[:, tt * P:(tt + 1) * P], ones[:, :],
                                            start=True, stop=True)
                last.then_inc(ssq_full, 1)

            @block.scalar
            def _(act):
                def split_weights(part, it):
                    act.wait_ge(w_loaded, it * 16 + 16)
                    nc.scalar.copy(wp[:, 0, :, PART[part]], wraw[:, :, PART[part]]).then_inc(w_hi[part], 1)

                def silu_split(task, which, unit, it):
                    silu_sem, hi_sem, ready = ((q_silu, q_hi, q_ready), (k_silu, k_hi, k_ready))[which]
                    filled(act, task, it)
                    if unit >= 0:
                        act.wait_ge(ready, it * UNITS + (unit + 1))
                    ins = nc.scalar.activation(qk[:, which, :], bank(task), ACT.Silu)
                    ins.then_inc(silu_sem, 1)
                    act.wait_ge(silu_sem, it * UNITS + (unit + 2))
                    nc.scalar.copy(qkp[:, (unit + 1) % 2, 0, which, :], qk[:, which, :]).then_inc(hi_sem, 1)

                def gate_of(u, it):
                    filled(act, ("g", u), it)
                    if late(it, u, 2):
                        act.wait_ge(gated, it * UNITS + (u - 1))
                    nc.scalar.activation(gate[:, u % 2, :], bank(("g", u)), ACT.Tanh, scale=0.5).then_inc(gate_done, 1)

                def values_of(i, u, it):
                    b = u // 2
                    task = ("v", u, i)
                    filled(act, task, it)
                    if late(it, u, 2):
                        act.wait_ge(v_ready, it * (2 * B) + (u + i - 1))
                    nc.scalar.activation(v[:, 2 * i:2 * i + 2, :].rearrange("p t n -> p (t n)"), bank(task),
                                         ACT.Silu).then_inc(v_silu, 1)
                    act.wait_ge(v_silu, it * (2 * B) + (u + i + 1))
                    nc.scalar.copy(vp[:, b % 2, 0, 2 * i:2 * i + 2, :], v[:, 2 * i:2 * i + 2, :]).then_inc(v_hi, 1)

                def scores_hi(u, j, it):
                    if j == 0 and late(it, u, 2):
                        act.wait_ge(o_full, it * UNITS + (u - 1))
                    act.wait_ge(p_masked, it * (UNITS * NB) + (u * NB + j + 1))
                    cols = slice(OFF[j], OFF[j] + S - j * P)
                    nc.scalar.copy(pp[:, u % 2, 0, cols], p[:, cols]).then_inc(p_hi, 1)

                def finish_unit(u, it):
                    h = u % 2
                    act.wait_ge(gated, it * UNITS + (u + 1))
                    if h == 0 and late(it, u, 2):
                        act.wait_ge(y_full, it * (2 * B) + u)
                    nc.scalar.copy(yp[:, 0, h, :], y[:, h, :]).then_inc(y_hi, 1)
                    if late(it, u, 2):
                        act.wait_ge(summed, it * UNITS + (u - 1))
                    nc.scalar.activation(sq[:, h, :], ps[:, O_BANK + h, :], ACT.Square).then_inc(squared, 1)

                for part in range(3):
                    split_weights(part, 0)
                silu_split(("k", -1), 1, -1, 0)
                silu_split(("q", -1), 0, -1, 0)

                def body(it, first, last_pair):
                    for u in range(UNITS):
                        more = not (last_pair and u == UNITS - 1)
                        scores_hi(u, 0, it)
                        if u == UNITS - 2 and not last_pair:
                            split_weights(0, it + 1)
                        if u == UNITS - 1 and not last_pair:
                            split_weights(1, it + 1)
                        if u == 0 and not first:
                            split_weights(2, it)
                        if late(it, u, 2):
                            finish_unit(u - 2, it)
                        if more:
                            silu_split(("k", u), 1, u, it)
                        scores_hi(u, 1, it)
                        if more:
                            silu_split(("q", u), 0, u, it)
                        scores_hi(u, 2, it)
                        if u % 2 == 0:
                            values_of(0, u, it)
                        scores_hi(u, 3, it)
                        if u % 2 == 0:
                            values_of(1, u, it)
                        gate_of(u, it)
                        if u == 2:
                            if not first:
                                act.wait_ge(y_full, it * (2 * B))
                            act.wait_ge(wo_scaled, it * 2 + 2)
                            nc.scalar.copy(wop[:, 0], woraw[:, :, :]).then_inc(wo_hi, 1)

                over_pairs(act, body)
                for u in (UNITS - 2, UNITS - 1):
                    finish_unit(u, PAIRS - 1)

            @block.vector
            def _(dve):
                def low(out, whole, high, ready):
                    nc.vector.tensor_tensor(out, whole, high.bitcast(F32), ALU.subtract).then_inc(ready, 1)

                def qk_low(which, unit, it):
                    hi_sem, ready = ((q_hi, q_ready), (k_hi, k_ready))[which]
                    dve.wait_ge(hi_sem, it * UNITS + (unit + 2))
                    low(qkp[:, (unit + 1) % 2, 1, which, :], qk[:, which, :], qkp[:, (unit + 1) % 2, 0, which, :], ready)

                def values_low(i, u, it):
                    b = u // 2
                    dve.wait_ge(v_hi, it * (2 * B) + (u + i + 1))
                    rows = slice(2 * i, 2 * i + 2)
                    low(vp[:, b % 2, 1, rows, :], v[:, rows, :], vp[:, b % 2, 0, rows, :], v_ready)

                def masked(u, j, it):
                    task = ("s", u, j)
                    cols = slice(OFF[j], OFF[j] + S - j * P)
                    filled(dve, task, it)
                    if u < 2 and j == 0:
                        dve.wait_ge(mask_loaded[u % 2], it * 16 + 16)
                    nc.vector.tensor_tensor(p[:, cols], bank(task)[:, 0:S - j * P], mask[:, u % 2, 0:S - j * P],
                                            ALU.mult).then_inc(p_masked, 1)

                def scores_low(u, j, it):
                    cols = slice(OFF[j], OFF[j] + S - j * P)
                    dve.wait_ge(p_hi, it * (UNITS * NB) + (u * NB + j + 1))
                    low(pp[:, u % 2, 1, cols], p[:, cols], pp[:, u % 2, 0, cols], p_ready)

                def gate_unit(u, it):
                    h = u % 2
                    dve.wait_ge(o_full, it * UNITS + (u + 1))
                    dve.wait_ge(gate_done, it * UNITS + (u + 1))
                    nc.vector.scalar_tensor_tensor(y[:, h, :], gate[:, h, :], 1.0, ps[:, O_BANK + h, :],
                                                   ALU.add, ALU.mult).then_inc(gated, 1)

                def y_low(u, it):
                    h = u % 2
                    dve.wait_ge(y_hi, it * UNITS + (u + 1))
                    low(yp[:, 1, h, :], y[:, h, :], yp[:, 0, h, :], y_ready)

                def add_output(u, i, it):
                    b = (u - 3) // 2 % B
                    dve.wait_ge(y_full, it * (2 * B) + (u - 2 + i))
                    rows = yacc[:, b * TB + 2 * i:b * TB + 2 * i + 2, :].rearrange("p t n -> p (t n)")
                    nc.vector.tensor_tensor(rows, rows, ps[:, Y_BANK + i, :], ALU.add).then_inc(y_added, 1)

                nc.vector.memset(yacc[:, :, :], 0.0).then_inc(zeroed, 1)
                dve.wait_ge(norm_loaded, 16)
                nc.vector.tensor_scalar(normw[:, :], normw[:, :], 0.5, None, ALU.mult).then_inc(norm_halved, 1)
                dve.wait_ge(norm_halved, 1)
                dve.wait_ge(zeroed, 1)
                qk_low(1, -1, 0)
                qk_low(0, -1, 0)

                def body(it, first, last_pair):
                    for u in range(UNITS):
                        more = not (last_pair and u == UNITS - 1)
                        if u == 2:
                            dve.wait_ge(wo_loaded, it * 16 + 16)
                            for h in range(2):
                                nc.vector.tensor_scalar(woraw[:, h, :], woraw[:, h, :], normw[:, at(it * 2 + h)], None,
                                                        ALU.mult).then_inc(wo_scaled, 1)
                        if late(it, u, 2):
                            gate_unit(u - 2, it)
                        masked(u, 0, it)
                        if late(it, u, 2):
                            y_low(u - 2, it)
                        scores_low(u, 0, it)
                        masked(u, 1, it)
                        if more:
                            qk_low(1, u, it)
                        scores_low(u, 1, it)
                        masked(u, 2, it)
                        if more:
                            qk_low(0, u, it)
                        scores_low(u, 2, it)
                        masked(u, 3, it)
                        if u % 2 == 0:
                            values_low(0, u, it)
                        elif late(it, u, 3):
                            add_output(u, 0, it)
                        scores_low(u, 3, it)
                        if u % 2 == 0:
                            values_low(1, u, it)
                        elif late(it, u, 3):
                            add_output(u, 1, it)

                over_pairs(dve, body)
                for u in (UNITS - 2, UNITS - 1):
                    gate_unit(u, PAIRS - 1)
                    y_low(u, PAIRS - 1)
                for i in range(2):
                    add_output(UNITS + 1, i, PAIRS - 1)
                dve.wait_ge(ssq_full, 1)
                nc.vector.tensor_scalar(rms[:, :], ps[:, 0, 0:NT], 1.0 / (H1 * D1), EPS_RMS, ALU.mult,
                                        ALU.add).then_inc(mean_done, 1)

            @block.gpsimd
            def _(pool):
                nc.gpsimd.memset(ones[:, :], 1.0)

                def weights_low(part, it):
                    pool.wait_ge(w_hi[part], it + 1)
                    nc.gpsimd.tensor_tensor(wp[:, 1, :, PART[part]], wraw[:, :, PART[part]],
                                            wp[:, 0, :, PART[part]].bitcast(F32), ALU.subtract).then_inc(w_ready[part], 1)

                def sum_unit(u, it):
                    b, h = (u % UNITS) // 2, u % 2
                    pool.wait_ge(squared, it * UNITS + (u + 1))
                    if h == 1:
                        pool.wait_ge(summed, it * UNITS + u)
                    cols = ssq[:, b * S:(b + 1) * S]
                    nc.gpsimd.tensor_tensor(cols, cols, sq[:, h, :], ALU.add).then_inc(summed, 1)

                sums_zeroed = n.sem("sums_zeroed")
                nc.gpsimd.memset(t["gate"][:, 0:2], 0.0).then_inc(sums_zeroed, 1)
                for part in range(3):
                    weights_low(part, 0)
                pool.wait_ge(sums_zeroed, 1)

                def body(it, first, last_pair):
                    for u in range(UNITS):
                        if u == UNITS - 2 and not last_pair:
                            weights_low(0, it + 1)
                        if u == UNITS - 1 and not last_pair:
                            weights_low(1, it + 1)
                        if u == 0 and not first:
                            weights_low(2, it)
                        if late(it, u, 2):
                            sum_unit(u - 2, it)
                        if u == 2:
                            pool.wait_ge(wo_hi, it + 1)
                            nc.gpsimd.tensor_tensor(wop[:, 1], woraw[:, :, :], wop[:, 0].bitcast(F32),
                                                    ALU.subtract).then_inc(wo_ready, 1)

                over_pairs(pool, body)
                for u in (UNITS - 2, UNITS - 1):
                    sum_unit(u, PAIRS - 1)
                pool.wait_ge(mean_done, 1)
                nc.gpsimd.tensor_tensor(rms[:, :], rms[:, :], t["neg_half"][:, :], ALU.pow).then_inc(rms_done, 1)


def experts_stage(nc, t, d):
    x, yacc, rms, hh = t["x"], t["yacc"], t["rms"], t["h_parts"]
    TE = FE // P
    PIECES = 12
    PC = FT * P // 2
    with ExitStack() as ctx:
        n = Names(nc, ctx, "experts")
        wg = n.sb("wg", [P, 2, KT, FT * P], F32R)
        wu = n.sb("wu", [P, 2, KT, FT * P], F32R)
        w2 = n.sb("w2", [P, 2, FT, D], F32R)
        raw = n.sb("raw", [P, 2, PC], F32)
        rw = n.sb("rw", [P, KT, E], F32)
        rwp = n.sb("rwp", [P, 2, KT, E], F32R)
        spread32 = n.sb("spread32", [EROWS, FE], F32)
        spread = n.sb("spread", [EROWS, FE], BF16)
        expert_id = n.sb("expert_id", [P, E], F32)
        tile8 = [P, NT, E]
        scores = n.sb("scores", tile8, F32)
        norm1 = n.sb("norm1", [P, NT], F32)
        best = n.sb("best", tile8, F32)
        best_id = n.sb("best_id", tile8, U32)
        best_idf = n.sb("best_idf", tile8, F32)
        chosen = n.sb("chosen", [P, 2, NT, E], F32)
        cw = n.sb("cw", tile8, F32)
        rest = n.sb("rest", tile8, F32)
        cwp = n.sb("cwp", [P, NT, 3, E], BF16)
        cwt = n.sb("cwt", [EROWS, B * S], BF16)
        hid = n.sb("hid", [P, 2, S], F32)
        hidp = n.sb("hidp", [P, 2, 2, S], F32R)
        logits_t = t["gate"][0:E, 0:2].rearrange("p l b n -> p (l b n)")
        ps = n.psum()
        norm = SplitNorm(n, "n", 1, 3, hh, yacc, 0)
        sg = yacc[:, 0:4, :].rearrange("p (b t) n -> p b (t n)", b=2)
        paired = yacc[:, 4:8, :].rearrange("p (b t) n -> p b (t n)", b=2)
        upd = yacc[:, 8:12, :]

        raw_loaded, raw_high, raw_low = n.sems("raw_loaded", 2), n.sem("raw_high"), n.sems("raw_low", 2)
        logits_t_made, logits_t_done, x_by_dve = n.sem("logits_t_made"), n.sem("logits_t_done"), n.sem("x_by_dve")
        small_loaded, spread_cast, rw_high, rw_low = (n.sem(s) for s in ("small_loaded", "spread_cast", "rw_high", "rw_low"))
        scaled, x_added, pool_held = n.sem("scaled"), n.sem("x_added"), n.sem("pool_held")
        logits_made, router, exp_done = n.sem("logits_made"), n.sem("router"), n.sem("exp_done")
        ids_ready, cwp_done, cw_turned, cwt_done = (n.sem(s) for s in ("ids_ready", "cwp_done", "cw_turned", "cwt_done"))
        g_made, u_made, c_made, y_made = (n.sem(s) for s in ("g_made", "u_made", "c_made", "y_made"))
        silu_done, pair_done, hid_done, hid_high, hid_low = (
            n.sem(s) for s in ("silu_done", "pair_done", "hid_done", "hid_high", "hid_low"))
        down_done, pe_held = n.sem("down_done"), n.sem("pe_held")
        upd_done, stored = n.sem("upd_done"), n.sem("stored")
        G_BANK, U_BANK, C_BANK, Y_BANK, L_BANK = 0, 1, 2, 4, 3

        def piece(m):
            which, rest_ = m // 4, m % 4
            k, cols = rest_ // 2, slice((rest_ % 2) * PC, (rest_ % 2 + 1) * PC)
            if which < 2:
                return d["wg" if which == 0 else "wu"][:, k, cols], [(wg, wu)[which][:, c, k, cols] for c in range(2)]
            cols = slice(rest_ * (FT * D // 4), (rest_ + 1) * (FT * D // 4))
            return (d["w2"].rearrange("p f n -> p (f n)")[:, cols],
                    [w2[:, c].rearrange("p f n -> p (f n)")[:, cols] for c in range(2)])

        with nc.Block() as block:

            @block.sync
            def _(sp):
                sp.dma_start(rw[:, :, :], d["router"]).then_inc(small_loaded, 16)
                sp.dma_start(spread32[:, :], d["spread"]).then_inc(small_loaded, 16)
                for m in range(PIECES):
                    if m >= 2:
                        sp.wait_ge(raw_low[m % 2], m // 2)
                    sp.dma_start(raw[:, m % 2, :], piece(m)[0]).then_inc(raw_loaded[m % 2], 16)
                with sp.Fori(0, B) as it:
                    sp.wait_ge(x_added, it + (B // 2 + 1))
                    sp.dma_start(t["out"][:, bass.ds(it * TB, TB), :], x[:, bass.ds(it * TB, TB), :]).then_inc(stored, 16)
                sp.wait_ge(stored, 16 * B)

            @block.tensor
            def _(pe):
                def logits(b):
                    pe.wait_ge(norm.low_done, b + 1)
                    for m, (k, (a, c)) in enumerate([(k, tc) for k in range(KT) for tc in TERMS]):
                        last = nc.tensor.matmul(ps[0:E, 4 + b, :], rwp[:, a, k, :], hh[:, c, k, b * S:(b + 1) * S],
                                                start=(m == 0), stop=(m == 5))
                    last.then_inc(logits_t_made, 1)

                norm.tensor_turn(nc, pe, t, ps, 0)
                pe.wait_ge(rw_low, 1)
                for b in range(B):
                    if b + 1 < B:
                        norm.tensor_turn(nc, pe, t, ps, b + 1)
                    logits(b)
                for b in range(B):
                    pe.wait_ge(logits_t_done, b + 1)
                    for tt in range(b * TB, (b + 1) * TB):
                        last = nc.tensor.transpose(ps[:, L_BANK, tt * E:(tt + 1) * E], logits_t[:, tt * P:(tt + 1) * P],
                                                   t["ident"][0:E, 0:E])
                last.then_inc(logits_made, 1)

                def hidden(w, bank, f, it, full):
                    for m, (k, (a, c)) in enumerate([(k, tc) for k in range(KT) for tc in TERMS]):
                        last = nc.tensor.matmul(ps[:, bank, :], w[:, a, k, f * P:(f + 1) * P],
                                                hh[:, c, k, at(it * S, S)], start=(m == 0), stop=(m == 5))
                    last.then_inc(full, 1)

                def down(f, it, it_f):
                    pe.wait_ge(hid_low, it_f)
                    for tt in range(TB):
                        for m, (a, c) in enumerate(TERMS):
                            last = nc.tensor.matmul(ps[:, Y_BANK + tt, 0:D], hidp[:, f % 2, a, tt * P:(tt + 1) * P],
                                                    w2[:, c, f, :], start=(f == 0 and m == 0), stop=(f == FT - 1 and m == 2))
                    if f == FT - 1:
                        last.then_inc(y_made, 1)
                    else:
                        last.then_inc(down_done, 1)

                def batch(it, first):
                    for f in range(FT):
                        at_f = it * FT + f
                        if not (first and f == 0):
                            pe.wait_ge(silu_done, at_f)
                        hidden(wg, G_BANK, f, it, g_made)
                        if f > TE:
                            pe.wait_ge(hid_done, at_f)
                        elif not (first and f == 0):
                            if f == 0:
                                pe.wait_ge(hid_done, at_f)
                            else:
                                pe.wait_ge(pair_done, it * TE + f)
                        hidden(wu, U_BANK, f, it, u_made)
                        if f < TE:
                            if first and f == 0:
                                pe.wait_ge(cwp_done, 3)
                                turned = ps[:, 6:8, :].bitcast(BF16).rearrange("p a n -> p (a n)")
                                for tt in range(NT):
                                    last = nc.tensor.transpose(turned[0:EROWS, tt * P:(tt + 1) * P],
                                                               cwp[:, tt, :, :].rearrange("p a e -> p (a e)"), t["identb"][:, :])
                                last.then_inc(cw_turned, 1)
                                pe.wait_ge(cwt_done, 1)
                            else:
                                pe.wait_ge(hid_done, at_f)
                            pe.sem_inc(pe_held, 1)
                            nc.tensor.matmul(ps[:, C_BANK, :], spread[:, f * P:(f + 1) * P], cwt[:, at(it * S, S)],
                                             start=True, stop=True).then_inc(c_made, 1)
                        if f > 0:
                            if f == 1 and not first:
                                pe.wait_ge(upd_done, it)
                            down(f - 1, it, at_f)
                        elif not first:
                            down(FT - 1, it, at_f)

                for i in range(2):
                    pe.wait_ge(raw_low[i], PIECES // 2)
                batch(0, True)
                with pe.Fori(1, B) as it:
                    batch(it, False)
                down(FT - 1, B, B * FT)

            @block.scalar
            def _(act):
                def split(m):
                    act.wait_ge(raw_loaded[m % 2], 16 * (m // 2 + 1))
                    nc.scalar.copy(piece(m)[1][0], raw[:, m % 2, :]).then_inc(raw_high, 1)

                act.wait_ge(small_loaded, 32)
                nc.scalar.copy(rwp[:, 0], rw[:, :, :]).then_inc(rw_high, 1)
                nc.scalar.copy(spread[:, :], spread32[:, :]).then_inc(spread_cast, 1)
                def copy_logits(b):
                    act.wait_ge(logits_t_made, b + 1)
                    nc.scalar.copy(logits_t[:, b * S:(b + 1) * S], ps[0:E, 4 + b, :]).then_inc(logits_t_done, 1)

                for b, pieces in enumerate(((0, 1), (2, 3), (4, 5, 6), (7, 8))):
                    for m in pieces:
                        split(m)
                    norm.scalar_high(nc, act, t, ps, b)
                    if b:
                        copy_logits(b - 1)
                for m in (9, 10, 11):
                    split(m)
                copy_logits(B - 1)
                act.wait_ge(router, 2)
                nc.scalar.activation(scores[:, :, :], scores[:, :, :], ACT.Exp).then_inc(exp_done, 1)

                def high(f, count):
                    act.wait_ge(hid_done, count)
                    nc.scalar.copy(hidp[:, f % 2, 0, :], hid[:, f % 2, :]).then_inc(hid_high, 1)

                def batch(it, first):
                    for f in range(FT):
                        at_f = it * FT + f
                        if f == 1 and not first:
                            act.wait_ge(y_made, it)
                        if f > 0:
                            high(f - 1, at_f)
                        act.wait_ge(g_made, at_f + 1)
                        nc.scalar.activation(sg[:, f % 2, :], ps[:, G_BANK, :], ACT.Silu).then_inc(silu_done, 1)
                    high(FT - 1, it * FT + FT)

                batch(0, True)
                with act.Fori(1, B) as it:
                    batch(it, False)

            @block.vector
            def _(dve):
                dve.wait_ge(rw_high, 1)
                nc.vector.tensor_tensor(rwp[:, 1], rw[:, :, :], rwp[:, 0].bitcast(F32), ALU.subtract).then_inc(rw_low, 1)
                for b in range(B):
                    for tile in range(b * TB, (b + 1) * TB):
                        last = nc.vector.scalar_tensor_tensor(yacc[:, tile, :], yacc[:, tile, :], rms[:, tile:tile + 1],
                                                              t["gate"][:, 2, b, :], ALU.mult, ALU.mult)
                    last.then_inc(scaled, 1)
                    if b % 2:
                        dve.wait_ge(scaled, b + 1)
                        rows = slice(b * TB, (b + 1) * TB)
                        nc.vector.tensor_tensor(x[:, rows, :], x[:, rows, :], yacc[:, rows, :], ALU.add).then_inc(x_by_dve, 1)
                dve.wait_ge(x_by_dve, 2)
                for b in (1, 0, 3, 2):
                    if b % 2 == 0:
                        dve.wait_ge(x_added, b // 2 + 1)
                    norm.vector_stats(nc, x, b)
                norm.vector_aggregate(nc, dve)
                norm.vector_norm(nc, dve, x)

                def low_piece(m):
                    dve.wait_ge(raw_high, m + 1)
                    hi, lo = piece(m)[1]
                    nc.vector.tensor_tensor(lo, raw[:, m % 2, :], hi.bitcast(F32), ALU.subtract).then_inc(raw_low[1], 1)

                for b, pieces in enumerate(((1, 3), (5,), (7,), (9, 11))):
                    norm.vector_low(nc, dve, b)
                    for m in pieces:
                        low_piece(m)

                step = 0

                def then(ins):
                    nonlocal step
                    step += 1
                    ins.then_inc(router, 1)
                    dve.wait_ge(router, step)

                wide = [P, NT, E]
                lg = ps[:, L_BANK, 0:NT * E].rearrange("p (t e) -> p t e", e=E)
                dve.wait_ge(logits_made, 1)
                then(nc.vector.tensor_reduce(norm1[:, :], lg, AX.X, ALU.max))
                then(nc.vector.tensor_tensor(scores[:, :, :], lg, norm1[:, :].unsqueeze(2).to_broadcast(wide), ALU.subtract))
                dve.wait_ge(exp_done, 1)
                then(nc.vector.tensor_reduce(norm1[:, :], scores[:, :, :], AX.X, ALU.add))
                then(nc.vector.reciprocal(norm1[:, :], norm1[:, :]))
                then(nc.vector.tensor_tensor(scores[:, :, :], scores[:, :, :], norm1[:, :].unsqueeze(2).to_broadcast(wide),
                                             ALU.mult))
                for tt in range(NT):
                    last = nc.vector.max(out=best[:, tt, :], in_=scores[:, tt, :])
                then(last)
                for tt in range(NT):
                    last = nc.vector.max_index(best_id[:, tt, :], best[:, tt, :], scores[:, tt, :])
                then(last)
                then(nc.vector.tensor_copy(best_idf[:, :, :], best_id[:, :, :]))
                then(nc.vector.tensor_reduce(norm1[:, :], best[:, :, 0:2], AX.X, ALU.add))
                then(nc.vector.tensor_scalar(norm1[:, :], norm1[:, :], 1e-20, None, ALU.add))
                then(nc.vector.reciprocal(norm1[:, :], norm1[:, :]))
                then(nc.vector.tensor_tensor(best[:, :, 0:2], best[:, :, 0:2],
                                             norm1[:, :].unsqueeze(2).to_broadcast([P, NT, 2]), ALU.mult))
                dve.wait_ge(ids_ready, 1)
                for c in range(2):
                    last = nc.vector.tensor_tensor(chosen[:, c], expert_id[:, :].unsqueeze(1).to_broadcast(wide),
                                                   best_idf[:, :, c:c + 1].to_broadcast(wide), ALU.is_equal)
                then(last)
                for c in range(2):
                    last = nc.vector.tensor_tensor(chosen[:, c], chosen[:, c], best[:, :, c:c + 1].to_broadcast(wide), ALU.mult)
                then(last)
                then(nc.vector.tensor_tensor(cw[:, :, :], chosen[:, 0], chosen[:, 1], ALU.add))
                nc.vector.tensor_copy(cwp[:, :, 0, :], cw[:, :, :]).then_inc(cwp_done, 1)
                dve.wait_ge(cwp_done, 1)
                then(nc.vector.tensor_tensor(rest[:, :, :], cw[:, :, :], cwp[:, :, 0, :], ALU.subtract))
                nc.vector.tensor_copy(cwp[:, :, 1, :], rest[:, :, :]).then_inc(cwp_done, 1)
                dve.wait_ge(cwp_done, 2)
                nc.vector.tensor_tensor(cwp[:, :, 2, :], rest[:, :, :], cwp[:, :, 1, :], ALU.subtract).then_inc(cwp_done, 1)
                dve.wait_ge(cw_turned, 1)
                nc.vector.tensor_copy(cwt[:, :], ps[0:EROWS, 6:8, :].bitcast(BF16).rearrange("p a n -> p (a n)")
                                      ).then_inc(cwt_done, 1)

                def low(f, count):
                    dve.wait_ge(hid_high, count)
                    nc.vector.tensor_tensor(hidp[:, f % 2, 1, :], hid[:, f % 2, :], hidp[:, f % 2, 0, :].bitcast(F32),
                                            ALU.subtract).then_inc(hid_low, 1)

                def batch(it, first):
                    for f in range(FT):
                        at_f = it * FT + f
                        if f > 0:
                            low(f - 1, at_f)
                        dve.wait_ge(u_made, at_f + 1)
                        dve.wait_ge(silu_done, at_f + 1)
                        if f < TE:
                            nc.vector.tensor_tensor(paired[:, f % 2, :], ps[:, U_BANK, :], sg[:, f % 2, :],
                                                    ALU.mult).then_inc(pair_done, 1)
                            dve.wait_ge(pair_done, it * TE + (f + 1))
                            dve.wait_ge(c_made, it * TE + (f + 1))
                            nc.vector.tensor_tensor(hid[:, f % 2, :], ps[:, C_BANK, :], paired[:, f % 2, :],
                                                    ALU.mult).then_inc(hid_done, 1)
                        else:
                            nc.vector.tensor_tensor(hid[:, f % 2, :], ps[:, U_BANK, :], sg[:, f % 2, :],
                                                    ALU.mult).then_inc(hid_done, 1)
                        if f == 0 and not first:
                            output(it)
                    low(FT - 1, it * FT + FT)

                def output(it):
                    dve.wait_ge(y_made, it)
                    dve.wait_ge(x_added, it + (B // 2 - 1))
                    if isinstance(it, int):
                        g = t["gate"][:, 3, it - 1:it, :]
                    else:
                        g = t["gate"][:, 3, bass.ds(it - 1, 1), :]
                    nc.vector.tensor_tensor(upd[:, :, :], ps[:, Y_BANK:Y_BANK + TB, 0:D], g.to_broadcast([P, TB, D]),
                                            ALU.mult).then_inc(upd_done, 1)

                batch(0, True)
                with dve.Fori(1, B) as it:
                    batch(it, False)
                output(B)

            @block.gpsimd
            def _(pool):
                nc.gpsimd.iota(expert_id[:, :], [[1, E]], base=0, channel_multiplier=0,
                               allow_small_or_imprecise_dtypes=True).then_inc(ids_ready, 1)
                for b in (0, 2):
                    pool.wait_ge(scaled, b + 1)
                    rows = slice(b * TB, (b + 1) * TB)
                    nc.gpsimd.tensor_tensor(x[:, rows, :], x[:, rows, :], yacc[:, rows, :], ALU.add).then_inc(x_added, 1)

                def low(m):
                    pool.wait_ge(raw_high, m + 1)
                    hi, lo = piece(m)[1]
                    nc.gpsimd.tensor_tensor(lo, raw[:, m % 2, :], hi.bitcast(F32), ALU.subtract).then_inc(raw_low[0], 1)

                low(0)
                norm.pool_rstd(nc, pool, t)
                for m in range(2, PIECES, 2):
                    low(m)
                with pool.Fori(0, B) as it:
                    pool.wait_ge(upd_done, it + 1)
                    pool.sem_inc(pool_held, 1)
                    xb = x[:, bass.ds(it * TB, TB), :]
                    nc.gpsimd.tensor_tensor(xb, xb, upd[:, :, :], ALU.add).then_inc(x_added, 1)


ALL_STAGES = [modulation_stage, attention0_stage, ffn0_stage, attention1_stage, experts_stage]



def build(nc, ins, out):
    d = dram_views(ins)
    with ExitStack() as ctx:
        n = Names(nc, ctx, "all")
        t = {
            "x": n.sb("x", [P, NT, D], F32),
            "mod": n.sb("mod", [P, 2, 6, KT, B], F32),
            "gate": n.sb("gate", [P, 4, B, D], F32),
            "ident": n.sb("ident", [P, P], F32),
            "ident16": n.sb("ident16", [P, P], F16),
            "identb": n.sb("identb", [P, P], BF16),
            "later_key": n.sb("later_key", [P, P], BF16),
            "later_key_t": n.sb("later_key_t", [P, P], BF16),
            "neg_half": n.sb("neg_half", [P, NT], F32),
            "h_parts": n.sb("h_parts", [P, 2, KT, B * S], F32R),
            "yacc": n.sb("yacc", [P, NT, D], F32),
            "rms": n.sb("rms", [P, NT], F32),
            "out": out,
            "decay_dram": nc.dram_tensor("decay_masks", [H1, P, S], F32, kind="Internal").ap(),
        }
        for stage in ALL_STAGES:
            before = nc.snapshot_sems()
            stage(nc, t, d)
            if stage is not ALL_STAGES[-1]:
                nc.clear_and_free_semaphores(nc.allocated_since(before))
                nc.all_engine_barrier()


def dram_views(ins):
    return {
        "x": ins["x"],
        "cond": ins["cond"],
        "wmod0": ins["wmod0"],
        "wmod1": ins["wmod1"],
        "slope": ins["slope"].partition_broadcast(P),
        "wqkv0": ins["wqkv0"],
        "wo0": ins["wo0"],
        "bias0": ins["bias0"],
        "norm_scale0": ins["norm_scale0"].partition_broadcast(P),
        "cosd": ins["cosd"],
        "sind": ins["sind"],
        "wffn": ins["wffn"],
        "ffn_rows": ins["ffn_rows"].partition_broadcast(P),
        "w1p": ins["w1p"],
        "wout": ins["wout"],
        "norm_w": ins["norm_w"],
        "router": ins["router"],
        "wg": ins["wg"], "wu": ins["wu"], "w2": ins["w2"], "spread": ins["spread"],
    }


def laid_out(i):
    a = {k: np.asarray(v) for k, v in i.items()}

    def rows(w):
        w = np.asarray(w)
        return np.ascontiguousarray(w.reshape(-1, P, w.shape[1]).transpose(1, 0, 2))

    r = {"x": np.ascontiguousarray(a["L0_attn_x"].reshape(NT, P, D).transpose(1, 0, 2))}
    c = np.stack([a["L0_c"], a["L1_c"]])
    r["cond"] = np.ascontiguousarray(c.reshape(2, B, KT, P).transpose(3, 0, 2, 1))
    r["wmod0"], r["wmod1"] = rows(a["L0_wmod"]), rows(a["L1_wmod"])
    r["slope"] = np.ascontiguousarray(a["L1_attn_slope_rate"].reshape(H1))
    r["wqkv0"] = rows(np.concatenate([a["L0_attn_wq"], a["L0_attn_wk"], a["L0_attn_wv"]], 1))
    r["wo0"] = rows(a["L0_attn_wo"])
    r["bias0"] = np.concatenate([a["L0_attn_bq"], a["L0_attn_bk"], a["L0_attn_bv"], a["L0_attn_bo"]])[None]
    r["norm_scale0"] = np.stack([a["L0_attn_q_norm_scale"], a["L0_attn_k_norm_scale"]])
    f = np.float32
    inv = (f(1.0) / np.power(f(10000.0), np.arange(0, D0, 2, dtype=f) / f(D0))).astype(f)
    ang = np.outer(np.arange(S, dtype=f), inv).astype(f)

    def table(v):
        v = np.concatenate([v, v], 1).astype(f)
        return np.ascontiguousarray(v.reshape(TB, P, D0).transpose(1, 0, 2))

    r["cosd"], r["sind"] = table(np.cos(ang)), table(np.sin(ang))
    r["wffn"] = rows(a["L0_ffn_weight"].T)
    r["ffn_rows"] = np.stack([a["L0_ffn_scale_weight"], a["L0_ffn_bias"]])
    wqkv = a["L1_attn_w_qkv"].reshape(H1, 3, D1, D)
    wgate = a["L1_attn_w_gate"].reshape(H1, D1, D)
    pairs = []
    for p in range(PAIRS):
        h = [2 * p, 2 * p + 1]
        pairs.append(rows(np.concatenate([wqkv[h[0], 0], wqkv[h[0], 1], wqkv[h[1], 0], wqkv[h[1], 1], wgate[h[0]],
                                          wqkv[h[0], 2], wqkv[h[1], 2], wgate[h[1]]], 0).T))
    r["w1p"] = np.stack(pairs)
    r["wout"] = np.ascontiguousarray(a["L1_attn_w_out"].T.reshape(PAIRS, 2, P, D).transpose(0, 2, 1, 3))
    r["norm_w"] = np.ascontiguousarray(a["L1_attn_norm_w"].reshape(H1, P).T)
    r["router"] = rows(a["L1_ffn_gate_w"].T)
    w1 = a["L1_ffn_w1"]

    def hidden(w, s):
        w = np.concatenate([w.transpose(1, 0, 2).reshape(D, FE), s.T, np.zeros((D, FT * P - FA), w.dtype)], 1)
        return rows(w)

    r["wg"], r["wu"] = hidden(w1[:, :, :I], a["L1_ffn_sw1"]), hidden(w1[:, :, I:], a["L1_ffn_sw2"])
    w2 = np.concatenate([a["L1_ffn_w2"].reshape(FE, D), a["L1_ffn_sw3"].T, np.zeros((FT * P - FA, D), f)], 0)
    r["w2"] = rows(w2)
    own = np.zeros((3, E, FE), f)
    for e in range(E):
        own[:, e, e * I:(e + 1) * I] = 1.0
    r["spread"] = own.reshape(EROWS, FE)
    return r


def kernel(**inputs):
    import concourse.bacc as bacc
    from concourse.bass_utils import run_bass_kernel_spmd

    nc = bacc.Bacc("TRN2", target_bir_lowering=False, num_devices=1)
    arrays = laid_out(inputs)
    ins = {k: nc.dram_tensor(f"in_{k}", v.shape, mybir.dt.from_np(v.dtype), kind="ExternalInput").ap()
           for k, v in arrays.items()}
    out = nc.dram_tensor("out", (P, NT, D), F32, kind="ExternalOutput").ap()
    build(nc, ins, out)
    r = run_bass_kernel_spmd(nc, [{f"in_{k}": v for k, v in arrays.items()}], core_ids=[0])
    return r.results[0]["out"].transpose(1, 0, 2).reshape(B, S, D)
```
